# Optimizing a Trainium2 kernel written in Bass

```python
import numpy as np
import jax
import jax.numpy as jnp

def _softmax(x, axis=-1):
    return jax.nn.softmax(x, axis=axis)

def _gelu(x):
    return jax.nn.gelu(x, approximate=True)

def _silu(x):
    return jax.nn.silu(x)

def _sigmoid(x):
    return jax.nn.sigmoid(x)

def _layernorm(x, axis=-1, eps=1e-05):
    m = jnp.mean(x, axis=axis, keepdims=True)
    v = jnp.var(x, axis=axis, keepdims=True)
    return (x - m) / jnp.sqrt(v + eps)

def _scatter_add(tgt, idx, src, axis=0):
    return tgt.at[idx].add(src)

def _segment_sum(src, seg, n):
    return jax.ops.segment_sum(src, seg, n)
kernel_name = 'mk_perceiver_d1_seqx_r4_1b7396'

def setup_inputs(seed: int=0):
    np.random.seed(seed)
    _w = jnp.asarray

    def _rec_inputs():
        import jax
        import jax.numpy as jnp
        _rk = jax.random.key(seed)
        x = 0.002226 + 0.9996 * jax.random.normal(jax.random.fold_in(_rk, 1), (4, 256, 256), jnp.float32)
        _lenS = 256 - jax.random.randint(jax.random.fold_in(_rk, 7), (4,), 0, max(1, 256 // 4) + 1, jnp.int32)
        _lenS2 = 4096 - jax.random.randint(jax.random.fold_in(_rk, 8), (4,), 0, max(1, 4096 // 4) + 1, jnp.int32)
        _ctx_1024P = jax.random.normal(jax.random.fold_in(_rk, 11), (4, 16, 256), jnp.float32)
        _ctx_1024c = jax.random.dirichlet(jax.random.fold_in(_rk, 511), 0.3 * jnp.ones((16,), jnp.float32), (4, 4096))
        _ctx_1024t = jnp.einsum('bsk,bkd->bsd', _ctx_1024c, _ctx_1024P)
        _ctx_1024t = _ctx_1024t * jax.lax.rsqrt(jnp.mean(jnp.square(_ctx_1024t)) + 1e-12) * 0.953939
        ctx_1024 = -0.000125008 + 0.999885 * (_ctx_1024t + 0.3 * jax.random.normal(jax.random.fold_in(_rk, 611), (4, 4096, 256), jnp.float32))
        _validS = jnp.arange(256)[None, :] < _lenS[:, None]
        _validS2 = jnp.arange(4096)[None, :] < _lenS2[:, None]
        _causal = jnp.tril(jnp.ones((256, 256), dtype=bool))
        mask_BxS2_bk0 = jnp.logical_not(jnp.broadcast_to(_validS2[:, :], (4, 4096)))
        return (x, ctx_1024, mask_BxS2_bk0)
    x, ctx_1024, mask_BxS2_bk0 = _rec_inputs()

    def _L0_xattn_setup():
        import jax, jax.numpy as jnp
        import numpy as np
        EPS = 1e-05

        def layer_norm(x, g, b):
            mu = jnp.mean(x, axis=-1, keepdims=True)
            var = jnp.mean((x - mu) ** 2, axis=-1, keepdims=True)
            return (x - mu) * jax.lax.rsqrt(var + EPS) * g + b
        key = jax.random.key(seed)
        ks = jax.random.split(key, 8)
        b, n, l, D = (8, 1024, 64, 256)
        heads, dim_head = (16, 64)
        inner = heads * dim_head
        x = jax.random.normal(ks[0], (b, n, D), dtype=jnp.float32)
        latents = jax.random.normal(ks[1], (b, l, D), dtype=jnp.float32)
        mask = jax.random.randint(ks[2], (b, n), 0, 2) > 0
        Wq = jax.random.normal(ks[3], (D, inner), dtype=jnp.float32) * D ** (-0.5)
        Wkv = jax.random.normal(ks[4], (D, 2 * inner), dtype=jnp.float32) * D ** (-0.5)
        Wout = jax.random.normal(ks[5], (inner, D), dtype=jnp.float32) * inner ** (-0.5)
        g1 = jnp.ones((D,), jnp.float32)
        b1 = jnp.zeros((D,), jnp.float32)
        g2 = jnp.ones((D,), jnp.float32)
        b2 = jnp.zeros((D,), jnp.float32)
        return {'x': x, 'latents': latents, 'mask': mask, 'g1': g1, 'b1': b1, 'g2': g2, 'b2': b2, 'Wq': Wq, 'Wkv': Wkv, 'Wout': Wout}
    _L0_xattn_all = _L0_xattn_setup()
    _L0_xattn_in = {k: v for k, v in _L0_xattn_all.items() if k in ('g1', 'b1', 'g2', 'b2', 'Wq', 'Wkv', 'Wout')}
    del _L0_xattn_all

    def _L0_attn_setup():
        import jax, jax.numpy as jnp
        import numpy as np
        B, S, D = (4, 512, 256)
        key = jax.random.key(seed)
        k1, k2, k3, k4 = jax.random.split(key, 4)
        x = jax.random.normal(k1, (B, S, D), dtype=jnp.float32)
        Qw = jax.random.normal(k2, (D, D), dtype=jnp.float32) / 40
        Kw = jax.random.normal(k3, (D, D), dtype=jnp.float32) / 40
        Vw = jax.random.normal(k4, (D, D), dtype=jnp.float32) / 40
        return {'x': x, 'Qw': Qw, 'Kw': Kw, 'Vw': Vw}
    _L0_attn_all = _L0_attn_setup()
    _L0_attn_in = {k: v for k, v in _L0_attn_all.items() if k in ('Qw', 'Kw', 'Vw')}
    del _L0_attn_all

    def _L0_ffn_setup():
        import jax, jax.numpy as jnp
        import numpy as np
        DIM = 256
        DEPTH = 2
        HEADS = 8
        DIM_HEAD = 64
        WINDOW = 128
        INNER = HEADS * DIM_HEAD
        HID = int(DIM * 4 * 2 / 3)
        B, N = (2, 2048)
        QK_SCALE = 8.0

        def shift_token(t):
            t1, t2 = jnp.split(t, 2, axis=-1)
            t2 = jnp.pad(t2, ((0, 0), (1, 0), (0, 0)))[:, :-1]
            return jnp.concatenate([t1, t2], axis=-1)

        def l2norm(t):
            return t / jnp.clip(jnp.linalg.norm(t, axis=-1, keepdims=True), 1e-12)

        def rotate_half(x):
            x1, x2 = jnp.split(x, 2, axis=-1)
            return jnp.concatenate([-x2, x1], axis=-1)

        def rotary_xpos(q, k):
            n = q.shape[-2]
            half_idx = jnp.arange(0, DIM_HEAD, 2, dtype=jnp.float32)
            inv_freq = 1.0 / 10000.0 ** (half_idx / DIM_HEAD)
            t = jnp.arange(n, dtype=jnp.float32)
            freqs = t[:, None] * inv_freq[None, :]
            freqs = jnp.concatenate([freqs, freqs], axis=-1)
            base = (half_idx + 0.4 * DIM_HEAD) / (1.4 * DIM_HEAD)
            power = (t - n // 2) / float(WINDOW // 2)
            scale = base[None, :] ** power[:, None]
            scale = jnp.concatenate([scale, scale], axis=-1)
            cos, sin = (jnp.cos(freqs), jnp.sin(freqs))
            q = q * cos * scale + rotate_half(q) * sin * scale
            k = k * cos / scale + rotate_half(k) * sin / scale
            return (q, k)

        def local_attention(q, k, v):
            b, h, n, d = q.shape
            w = n // WINDOW
            bq = q.reshape(b, h, w, WINDOW, d) * QK_SCALE
            bk = k.reshape(b, h, w, WINDOW, d)
            bv = v.reshape(b, h, w, WINDOW, d)

            def look_around(t):
                p = jnp.pad(t, ((0, 0), (0, 0), (1, 0), (0, 0), (0, 0)))
                return jnp.concatenate([p[:, :, :w], p[:, :, 1:]], axis=3)
            bk, bv = (look_around(bk), look_around(bv))
            bt = jnp.arange(n).reshape(w, WINDOW)
            btp = jnp.pad(bt, ((1, 0), (0, 0)), constant_values=-1)
            btk = jnp.concatenate([btp[:w], btp[1:]], axis=1)
            sim = jnp.einsum('bhwid,bhwjd->bhwij', bq, bk)
            i = bt[:, :, None]
            j = btk[:, None, :]
            mask = (i < j) | (i > j + WINDOW) | (j == -1)
            sim = jnp.where(mask, -jnp.finfo(sim.dtype).max, sim)
            attn = jax.nn.softmax(sim, axis=-1)
            out = jnp.einsum('bhwij,bhwjd->bhwid', attn, bv)
            return out.reshape(b, h, n, d)

        def _layer(x, wqkv, qs, ksc, wo, lg, lb, w1, b1, w2, b2):
            b, n, _ = x.shape
            h = shift_token(x)
            qkv = h @ wqkv
            q, k, v = jnp.split(qkv, 3, axis=-1)
            to_heads = lambda t: t.reshape(b, n, HEADS, DIM_HEAD).transpose(0, 2, 1, 3)
            q, k, v = (to_heads(q), to_heads(k), to_heads(v))
            q = l2norm(q) * qs
            k = l2norm(k) * ksc
            q, k = rotary_xpos(q, k)
            o = local_attention(q, k, v)
            o = o.transpose(0, 2, 1, 3).reshape(b, n, INNER)
            x = x + o @ wo
            h = shift_token(x)
            mu = h.mean(-1, keepdims=True)
            var = h.var(-1, keepdims=True)
            h = (h - mu) / jnp.sqrt(var + 1e-05) * lg + lb
            h = h @ w1 + b1
            a, g = jnp.split(h, 2, axis=-1)
            h = a * jax.nn.gelu(g, approximate=False)
            x = x + h @ w2 + b2
            return x
        key = jax.random.key(seed)
        ks = jax.random.split(key, 6)
        return {'x': jax.random.normal(ks[0], (B, N, DIM), jnp.float32), 'wqkv': jax.random.normal(ks[1], (DEPTH, DIM, 3 * INNER), jnp.float32) * 0.02, 'q_scale': jnp.ones((DEPTH, DIM_HEAD), jnp.float32), 'k_scale': jnp.ones((DEPTH, DIM_HEAD), jnp.float32), 'wo': jax.random.normal(ks[2], (DEPTH, INNER, DIM), jnp.float32) * 0.02, 'ln_g': jnp.ones((DEPTH, DIM), jnp.float32), 'ln_b': jnp.zeros((DEPTH, DIM), jnp.float32), 'w1': jax.random.normal(ks[3], (DEPTH, DIM, 2 * HID), jnp.float32) * 0.02, 'b1': jnp.zeros((DEPTH, 2 * HID), jnp.float32), 'w2': jax.random.normal(ks[4], (DEPTH, HID, DIM), jnp.float32) * 0.02, 'b2': jnp.zeros((DEPTH, DIM), jnp.float32)}
    _L0_ffn_all = _L0_ffn_setup()
    _L0_ffn_in = {k: v for k, v in _L0_ffn_all.items() if k in ('wqkv', 'q_scale', 'k_scale', 'wo', 'ln_g', 'ln_b', 'w1', 'b1', 'w2', 'b2')}
    del _L0_ffn_all
    return {'x': x, 'ctx_1024': ctx_1024, 'mask_BxS2_bk0': mask_BxS2_bk0, 'L0_xattn_g1': _L0_xattn_in['g1'], 'L0_xattn_b1': _L0_xattn_in['b1'], 'L0_xattn_g2': _L0_xattn_in['g2'], 'L0_xattn_b2': _L0_xattn_in['b2'], 'L0_xattn_Wq': _L0_xattn_in['Wq'], 'L0_xattn_Wkv': _L0_xattn_in['Wkv'], 'L0_xattn_Wout': _L0_xattn_in['Wout'], 'L0_attn_Qw': _L0_attn_in['Qw'], 'L0_attn_Kw': _L0_attn_in['Kw'], 'L0_attn_Vw': _L0_attn_in['Vw'], 'L0_ffn_wqkv': _L0_ffn_in['wqkv'], 'L0_ffn_q_scale': _L0_ffn_in['q_scale'], 'L0_ffn_k_scale': _L0_ffn_in['k_scale'], 'L0_ffn_wo': _L0_ffn_in['wo'], 'L0_ffn_ln_g': _L0_ffn_in['ln_g'], 'L0_ffn_ln_b': _L0_ffn_in['ln_b'], 'L0_ffn_w1': _L0_ffn_in['w1'], 'L0_ffn_b1': _L0_ffn_in['b1'], 'L0_ffn_w2': _L0_ffn_in['w2'], 'L0_ffn_b2': _L0_ffn_in['b2']}

def reference(x, ctx_1024, mask_BxS2_bk0, L0_xattn_g1, L0_xattn_b1, L0_xattn_g2, L0_xattn_b2, L0_xattn_Wq, L0_xattn_Wkv, L0_xattn_Wout, L0_attn_Qw, L0_attn_Kw, L0_attn_Vw, L0_ffn_wqkv, L0_ffn_q_scale, L0_ffn_k_scale, L0_ffn_wo, L0_ffn_ln_g, L0_ffn_ln_b, L0_ffn_w1, L0_ffn_b1, L0_ffn_w2, L0_ffn_b2):
    import jax
    import jax.numpy as jnp

    def _L0_xattn_ref(x, latents, mask, g1, b1, g2, b2, Wq, Wkv, Wout):
        import jax, jax.numpy as jnp
        import numpy as np
        EPS = 1e-05

        def layer_norm(x, g, b):
            mu = jnp.mean(x, axis=-1, keepdims=True)
            var = jnp.mean((x - mu) ** 2, axis=-1, keepdims=True)
            return (x - mu) * jax.lax.rsqrt(var + EPS) * g + b
        heads, dim_head = (16, 64)
        b, n, D = x.shape
        l = latents.shape[1]
        xn = layer_norm(x, g1, b1)
        ln_lat = layer_norm(latents, g2, b2)
        q = ln_lat @ Wq
        kv = jnp.concatenate([xn, ln_lat], axis=1) @ Wkv
        k, v = jnp.split(kv, 2, axis=-1)

        def to_heads(t):
            return t.reshape(t.shape[0], t.shape[1], heads, dim_head).transpose(0, 2, 1, 3)
        q, k, v = (to_heads(q), to_heads(k), to_heads(v))
        scale = 1.0 / np.sqrt(np.sqrt(dim_head)).astype(np.float32)
        weight = jnp.einsum('bhld,bhnd->bhln', q * scale, k * scale)
        full_mask = jnp.concatenate([mask, jnp.ones((b, l), dtype=bool)], axis=1)
        neg = -jnp.finfo(weight.dtype).max
        weight = jnp.where(full_mask[:, None, None, :], weight, neg)
        weight = jax.nn.softmax(weight.astype(jnp.float32), axis=-1).astype(q.dtype)
        out = jnp.einsum('bhln,bhnd->bhld', weight, v)
        out = out.transpose(0, 2, 1, 3).reshape(b, l, heads * dim_head)
        return out @ Wout

    def _L0_attn_ref(x, Qw, Kw, Vw):
        import jax, jax.numpy as jnp
        import numpy as np
        B, S, D = (4, 512, 256)
        Q = x @ Qw
        K = x @ Kw
        V = x @ Vw
        d = x.shape[-1]
        S_len = x.shape[-2]
        mask = jnp.where(jnp.tril(jnp.ones((S_len, S_len), dtype=x.dtype)) == 0, -jnp.inf, 0.0).astype(x.dtype)
        scores = jnp.einsum('bqd,bkd->bqk', Q, K) / jnp.sqrt(jnp.asarray(d, x.dtype))
        scores = scores + mask
        attn = jax.nn.softmax(scores, axis=-1)
        return jnp.einsum('bqk,bkd->bqd', attn, V)

    def _L0_ffn_ref(x, wqkv, q_scale, k_scale, wo, ln_g, ln_b, w1, b1, w2, b2):
        import jax, jax.numpy as jnp
        import numpy as np
        DIM = 256
        DEPTH = 2
        HEADS = 8
        DIM_HEAD = 64
        WINDOW = 128
        INNER = HEADS * DIM_HEAD
        HID = int(DIM * 4 * 2 / 3)
        B, N = (2, 2048)
        QK_SCALE = 8.0

        def shift_token(t):
            t1, t2 = jnp.split(t, 2, axis=-1)
            t2 = jnp.pad(t2, ((0, 0), (1, 0), (0, 0)))[:, :-1]
            return jnp.concatenate([t1, t2], axis=-1)

        def l2norm(t):
            return t / jnp.clip(jnp.linalg.norm(t, axis=-1, keepdims=True), 1e-12)

        def rotate_half(x):
            x1, x2 = jnp.split(x, 2, axis=-1)
            return jnp.concatenate([-x2, x1], axis=-1)

        def rotary_xpos(q, k):
            n = q.shape[-2]
            half_idx = jnp.arange(0, DIM_HEAD, 2, dtype=jnp.float32)
            inv_freq = 1.0 / 10000.0 ** (half_idx / DIM_HEAD)
            t = jnp.arange(n, dtype=jnp.float32)
            freqs = t[:, None] * inv_freq[None, :]
            freqs = jnp.concatenate([freqs, freqs], axis=-1)
            base = (half_idx + 0.4 * DIM_HEAD) / (1.4 * DIM_HEAD)
            power = (t - n // 2) / float(WINDOW // 2)
            scale = base[None, :] ** power[:, None]
            scale = jnp.concatenate([scale, scale], axis=-1)
            cos, sin = (jnp.cos(freqs), jnp.sin(freqs))
            q = q * cos * scale + rotate_half(q) * sin * scale
            k = k * cos / scale + rotate_half(k) * sin / scale
            return (q, k)

        def local_attention(q, k, v):
            b, h, n, d = q.shape
            w = n // WINDOW
            bq = q.reshape(b, h, w, WINDOW, d) * QK_SCALE
            bk = k.reshape(b, h, w, WINDOW, d)
            bv = v.reshape(b, h, w, WINDOW, d)

            def look_around(t):
                p = jnp.pad(t, ((0, 0), (0, 0), (1, 0), (0, 0), (0, 0)))
                return jnp.concatenate([p[:, :, :w], p[:, :, 1:]], axis=3)
            bk, bv = (look_around(bk), look_around(bv))
            bt = jnp.arange(n).reshape(w, WINDOW)
            btp = jnp.pad(bt, ((1, 0), (0, 0)), constant_values=-1)
            btk = jnp.concatenate([btp[:w], btp[1:]], axis=1)
            sim = jnp.einsum('bhwid,bhwjd->bhwij', bq, bk)
            i = bt[:, :, None]
            j = btk[:, None, :]
            mask = (i < j) | (i > j + WINDOW) | (j == -1)
            sim = jnp.where(mask, -jnp.finfo(sim.dtype).max, sim)
            attn = jax.nn.softmax(sim, axis=-1)
            out = jnp.einsum('bhwij,bhwjd->bhwid', attn, bv)
            return out.reshape(b, h, n, d)

        def _layer(x, wqkv, qs, ksc, wo, lg, lb, w1, b1, w2, b2):
            b, n, _ = x.shape
            h = shift_token(x)
            qkv = h @ wqkv
            q, k, v = jnp.split(qkv, 3, axis=-1)
            to_heads = lambda t: t.reshape(b, n, HEADS, DIM_HEAD).transpose(0, 2, 1, 3)
            q, k, v = (to_heads(q), to_heads(k), to_heads(v))
            q = l2norm(q) * qs
            k = l2norm(k) * ksc
            q, k = rotary_xpos(q, k)
            o = local_attention(q, k, v)
            o = o.transpose(0, 2, 1, 3).reshape(b, n, INNER)
            x = x + o @ wo
            h = shift_token(x)
            mu = h.mean(-1, keepdims=True)
            var = h.var(-1, keepdims=True)
            h = (h - mu) / jnp.sqrt(var + 1e-05) * lg + lb
            h = h @ w1 + b1
            a, g = jnp.split(h, 2, axis=-1)
            h = a * jax.nn.gelu(g, approximate=False)
            x = x + h @ w2 + b2
            return x
        for l in range(DEPTH):
            x = _layer(x, wqkv[l], q_scale[l], k_scale[l], wo[l], ln_g[l], ln_b[l], w1[l], b1[l], w2[l], b2[l])
        return x
    x = x + _L0_xattn_ref(ctx_1024, _layernorm(x, axis=-1), mask_BxS2_bk0, L0_xattn_g1, L0_xattn_b1, L0_xattn_g2, L0_xattn_b2, L0_xattn_Wq, L0_xattn_Wkv, L0_xattn_Wout)
    x = x + _L0_attn_ref(_layernorm(x, axis=-1), L0_attn_Qw, L0_attn_Kw, L0_attn_Vw)
    x = x + _L0_ffn_ref(_layernorm(x, axis=-1), L0_ffn_wqkv, L0_ffn_q_scale, L0_ffn_k_scale, L0_ffn_wo, L0_ffn_ln_g, L0_ffn_ln_b, L0_ffn_w1, L0_ffn_b1, L0_ffn_w2, L0_ffn_b2)
    return x

_drawn_inputs = setup_inputs


def setup_inputs(seed=0):
    import zlib

    import numpy as np

    out = dict(_drawn_inputs(seed))
    spreads = {'L0_xattn_g1': (1.0, 0.2),
     'L0_xattn_b1': (0.0, 0.1),
     'L0_xattn_g2': (1.0, 0.2),
     'L0_xattn_b2': (0.0, 0.1),
     'L0_ffn_q_scale': (1.0, 0.6),
     'L0_ffn_k_scale': (1.0, 0.6),
     'L0_ffn_ln_g': (1.0, 0.6),
     'L0_ffn_ln_b': (0.0, 0.8),
     'L0_ffn_b1': (0.0, 0.8),
     'L0_ffn_b2': (0.0, 0.1)}
    factors = {'L0_attn_Qw': 7.421, 'L0_attn_Kw': 7.502}
    for name, (base, spread) in spreads.items():
        noise = np.random.default_rng([zlib.crc32(name.encode()), seed]).standard_normal(out[name].shape)
        drawn = base * np.exp(spread * noise) if base else spread * noise
        out[name] = jnp.asarray(drawn.astype(out[name].dtype))
    for name, factor in factors.items():
        out[name] = (out[name] * factor).astype(out[name].dtype)
    return out
```

```python
from contextlib import ExitStack

import numpy as np

import concourse.bass as bass
from concourse import mybir

F32 = mybir.dt.float32
F32R = mybir.dt.float32r
I32 = mybir.dt.int32
U8 = mybir.dt.uint8
ALU = mybir.AluOpType
ACT = mybir.ActivationFunctionType
X_AXIS = mybir.AxisListType.X

P = 128
BIG = 3.0e38
FAR = 1.0e25
EPS = 1e-5

B, L, D = 4, 256, 256
CTX = 4096
H, DH = 16, 64
CH = 256
NCH = CTX // CH
KC = D // P
QT = L // P
KT = CH // P
NG = H // 2
GU = 2 * QT
TILES = B * QT
PLAN = NCH + 2

LH, LDH, LI = 8, 64, 512
HID = 682
HB = 6
DEPTH = 2


def split_product(pe, out, stationary, moving, first, last):
    (s_hi, s_lo), (m_hi, m_lo) = stationary, moving
    pe.matmul(out, s_hi, m_hi, start=first, stop=False)
    pe.matmul(out, s_hi, m_lo, start=False, stop=False)
    return pe.matmul(out, s_lo, m_hi, start=False, stop=last)


def prepare_stage(nc, t, sems, args):
    s = {n: sems(n) for n in (
        "ident_loaded", "wkv_loaded", "wq_loaded", "wout_loaded", "params_loaded", "mask_loaded", "iota_loaded",
        "hi_done", "lo_done", "any_done", "plan_rows", "plan_moved", "plan_done", "ident_split")}
    weights = [("wkv_loaded", t.wkv_raw, t.wkv), ("wq_loaded", t.wq_raw, t.wq), ("wout_loaded", t.wout_raw, t.wout)]
    with nc.Block() as block:
        @block.sync
        def _(sp):
            sp.dma_start(t.ident[:], args["ident"]).then_inc(s["ident_loaded"], 16)
            sp.dma_start(t.mask_rows[:], args["mask_BxS2_bk0"]).then_inc(s["mask_loaded"], 16)
            sp.dma_start(t.iota[:], args["iota"]).then_inc(s["iota_loaded"], 16)
            sp.dma_start(t.first_key[:], args["first_key"]).then_inc(s["iota_loaded"], 16)
            sp.dma_start(t.wkv_raw[:], args["L0_xattn_Wkv"].rearrange("(k p) n -> p k n", p=P)).then_inc(s["wkv_loaded"], 16)
            sp.dma_start(t.wq_raw[:], args["L0_xattn_Wq"].rearrange("(k p) n -> p k n", p=P)).then_inc(s["wq_loaded"], 16)
            sp.dma_start(t.wout_raw[:], args["L0_xattn_Wout"].rearrange("(k p) n -> p k n", p=P)).then_inc(s["wout_loaded"], 16)
            for col, name in enumerate(("g1", "b1", "g2", "b2")):
                with nc.allow_non_contiguous_dma("a vector of the width onto the partitions"):
                    sp.dma_start(t.norm[:, col, :], args[f"L0_xattn_{name}"].rearrange("(k p) -> p k", p=P)
                                 ).then_inc(s["params_loaded"], 16)
            sp.wait_ge(s["plan_rows"], 1)
            sp.dma_start(t.plan_flat[0:1, :].rearrange("p (b c) -> p b c", b=B), t.plan_rows[:]).then_inc(s["plan_moved"], 16)
            sp.wait_ge(s["params_loaded"], 64)
            sp.wait_ge(s["plan_moved"], 16)

        @block.scalar
        def _(act):
            for loaded, raw, (hi, lo) in weights:
                act.wait_ge(s[loaded], 16)
                act.activation(hi[:], raw[:], ACT.Copy).then_inc(s["hi_done"], 1)

        @block.vector
        def _(dve):
            dve.wait_ge(s["mask_loaded"], 16)
            dve.wait_ge(s["iota_loaded"], 32)
            step = [0]

            def then(ins):
                step[0] += 1
                ins.then_inc(s["any_done"], 1)
                dve.wait_ge(s["any_done"], step[0])

            flags, upto, place = t.scratch[0:B, 0:NCH], t.scratch[0:B, 16:32], t.scratch[0:B, 32:48]
            then(dve.tensor_reduce(flags, t.mask_rows[:].rearrange("b (c k) -> b c k", k=CH), X_AXIS, ALU.max))
            then(dve.memset(t.ones[:], 1.0))
            then(dve.tensor_tensor_scan(upto, t.ones[0:B, :], flags, 0.0, ALU.mult, ALU.add))
            then(dve.tensor_scalar(place, flags, -1001.0, 1000.0, ALU.mult, ALU.add))
            then(dve.tensor_tensor(place, place, upto, ALU.add))
            hits = t.hits[0:B]
            then(dve.tensor_tensor(hits, place.unsqueeze(1).broadcast_to([B, NCH, NCH]),
                                   t.iota[:].unsqueeze(2).broadcast_to([B, NCH, NCH]), ALU.is_equal))
            then(dve.tensor_tensor(hits, hits, t.first_key[:].unsqueeze(1).broadcast_to([B, NCH, NCH]), ALU.mult))
            then(dve.tensor_reduce(t.plan_rows[:, 0:NCH], hits, X_AXIS, ALU.add))
            then(dve.tensor_scalar(t.plan_rows[:, NCH:NCH + 1], upto[:, NCH - 1:NCH], 1.0, None, ALU.add))
            dve.memset(t.plan_rows[:, NCH + 1:NCH + 2], 0.0).then_inc(s["plan_rows"], 1)
            dve.wait_ge(s["plan_moved"], 16)
            flat = t.plan_flat[:].rearrange("p (b c) -> p b c", b=B)
            for b in range(1, B):
                then(dve.tensor_tensor(flat[:, b, NCH + 1:NCH + 2], flat[:, b - 1, NCH + 1:NCH + 2],
                                       flat[:, b - 1, NCH:NCH + 1], ALU.add))
            dve.tensor_copy(t.plan[:], t.plan_flat[:]).then_inc(s["plan_done"], 1)
            for n, (_, raw, (hi, lo)) in enumerate(weights):
                dve.wait_ge(s["hi_done"], n + 1)
                dve.tensor_tensor(lo[:], raw[:], hi[:].bitcast(F32), ALU.subtract).then_inc(s["lo_done"], 1)
            dve.wait_ge(s["lo_done"], 3)


def cross_stage(nc, t, sems, args):
    names = (
        "x_loaded", "raw_loaded", "pen_loaded", "pen_used",
        "lat_var", "lat_std", "lat_z", "lat_turned", "lat_wide", "lat_hi", "lat_ready",
        "q_done", "q_hi", "q_ready", "state_zero",
        "stats_done", "var", "std", "rstd_done", "z_ready", "z_turned", "wide", "x_hi", "x_ready",
        "proj_done", "k_hi", "k_ready", "v_act", "v_dve",
        "s_done", "s_read", "bias_ready", "alpha_ready", "p_ready", "t_done", "pt_act", "pt_dve",
        "pv_done", "rescaled", "o_added", "dve_step", "pool_step",
        "o_norm", "o_turned", "ot_hi", "ot_lo", "out_done", "x_added")
    s = {n: sems(n) for n in names}
    tokens = args["ctx_1024"].rearrange("b n d -> (b n) d")
    mask_row = args["mask_BxS2_bk0"].rearrange("b (o n) -> o (b n)", o=1)
    x_batches = args["x"].rearrange("b (t p) d -> b p t d", p=P)
    wk = [w[:, :, 0:H * DH] for w in t.wkv]
    wv = [w[:, :, H * DH:2 * H * DH] for w in t.wkv]
    banks = [t.turn[0], t.turn[1], t.proj]

    def counts(eng, b):
        n = eng.value_load(t.plan[0:1, bass.ds(b * PLAN + NCH, 1)], min_val=1, max_val=NCH + 1)
        before = eng.value_load(t.plan[0:1, bass.ds(b * PLAN + NCH + 1, 1)], min_val=0, max_val=(B - 1) * (NCH + 1))
        return n, before

    with nc.Block() as block:
        @block.sync
        def _(sp):
            with sp.Fori(0, B) as b:
                count, before = counts(sp, b)
                with sp.Fori(0, count) as i:
                    n = before + i
                    first_key = sp.value_load(t.plan[0:1, bass.ds(b * PLAN + i, 1)], min_val=0, max_val=B * CTX - CH)
                    sp.wait_ge(s["z_ready"], n + 1)
                    sp.dma_start(t.raw[:], tokens[bass.ds(first_key, CH), :].rearrange("(t p) d -> p t d", p=P)).then_inc(s["raw_loaded"], 16)
                    sp.wait_ge(s["pen_used"], n + 1)
                    sp.dma_start(t.mask8[:], mask_row[:, bass.ds(first_key, CH)].partition_broadcast(P)).then_inc(s["pen_loaded"], 16)

        @block.tensor
        def _(pe):
            def queries(b):
                pe.wait_ge(s["lat_z"], b + 1)
                for kc in range(KC):
                    for kt in range(KT):
                        last = pe.transpose(t.proj[:, (kc * KT + kt) * P:(kc * KT + kt + 1) * P],
                                            t.z[:, kt, kc * P:(kc + 1) * P], t.ident[:])
                last.then_inc(s["lat_turned"], 1)
                pe.wait_ge(s["lat_ready"], b + 1)
                for u in range(4):
                    if u == 3:
                        pe.wait_ge(s["q_ready"], 4 * b + 1)
                    for m in range(2):
                        mt = 2 * u + m
                        for kc in range(KC):
                            last = split_product(pe, banks[u % 3][:, m * L:(m + 1) * L],
                                                 [w[:, kc, mt * P:(mt + 1) * P] for w in t.wq],
                                                 [x[:, kc, :] for x in t.xt], kc == 0, kc == KC - 1)
                    last.then_inc(s["q_done"], 1)

            def projections(b, n):
                pe.wait_ge(s["q_ready"], 4 * b + 4)
                pe.wait_ge(s["x_ready"], n + 1)
                for u in range(8):
                    if 3 <= u < 7:
                        pe.wait_ge(s["k_ready"], 4 * n + u - 2)
                    if u == 7:
                        pe.wait_ge(s["v_act"], 2 * n + 1)
                    bank = banks[u % 3]
                    if u < 4:
                        for m in range(2):
                            mt = 2 * u + m
                            for kc in range(KC):
                                last = split_product(pe, bank[:, m * CH:(m + 1) * CH],
                                                     [w[:, kc, mt * P:(mt + 1) * P] for w in wk],
                                                     [x[:, kc, :] for x in t.xt], kc == 0, kc == KC - 1)
                    else:
                        kt, half = (u - 4) // 2, (u - 4) % 2
                        for kc in range(KC):
                            last = split_product(pe, bank[:], [x[:, kc, kt * P:(kt + 1) * P] for x in t.xt],
                                                 [w[:, kc, half * 512:(half + 1) * 512] for w in wv], kc == 0, kc == KC - 1)
                    last.then_inc(s["proj_done"], 1)

            def scores(n, g):
                if g % 2 == 0:
                    pe.wait_ge(s["k_ready"], 4 * n + g // 2 + 1)
                pe.wait_ge(s["s_read"], 8 * n + g + 1)
                for u in range(GU):
                    h, qt = 2 * g + u // QT, u % QT
                    pe.matmul(t.s_ps[g % 2][:, u, :], t.qh[:, h, qt * P:(qt + 1) * P], t.kp[:, h, :], start=True, stop=False)
                    last = pe.matmul(t.s_ps[g % 2][:, u, :], t.ql[:, h, qt * P:(qt + 1) * P], t.kp[:, h, :], start=False, stop=True)
                last.then_inc(s["s_done"], 1)

            def turn_probs(n, g):
                pe.wait_ge(s["p_ready"], 8 * n + g + 1)
                if g == 0:
                    pe.wait_ge(s["v_act"], 2 * n + 2)
                    pe.wait_ge(s["v_dve"], 2 * n + 2)
                else:
                    pe.wait_ge(s["pt_act"], 8 * n + g)
                    pe.wait_ge(s["pt_dve"], 8 * n + g)
                for u in range(GU):
                    for kt in range(KT):
                        last = pe.transpose(t.turn[u // 2][:, ((u % 2) * KT + kt) * P:((u % 2) * KT + kt + 1) * P],
                                            t.probs[g % 3][:, u, kt * P:(kt + 1) * P], t.ident[:])
                last.then_inc(s["t_done"], 1)

            def weighted_values(n, g):
                pe.wait_ge(s["pt_act"], 8 * n + g + 1)
                pe.wait_ge(s["pt_dve"], 8 * n + g + 1)
                pe.wait_ge(s["o_added"], 8 * n + g + NG)
                for u in range(GU):
                    h = 2 * g + u // QT
                    for kt in range(KT):
                        last = pe.matmul(t.pv_ps[:, u, :], t.pt[g % 3][:, u, kt, :], t.v[:, kt, h * DH:(h + 1) * DH],
                                         start=(kt == 0), stop=(kt == KT - 1))
                last.then_inc(s["pv_done"], 1)

            def next_keys(n):
                pe.wait_ge(s["z_ready"], n + 2)
                for kc in range(KC):
                    for kt in range(KT):
                        last = pe.transpose(t.proj[:, (kc * KT + kt) * P:(kc * KT + kt + 1) * P],
                                            t.z[:, kt, kc * P:(kc + 1) * P], t.ident[:])
                last.then_inc(s["z_turned"], 1)

            def output_projection(b):
                pe.wait_ge(s["o_norm"], b + 2)
                for u in range(4):
                    if u >= 2:
                        pe.wait_ge(s["ot_lo"], 4 * b + u - 1)
                    for k in range(2):
                        for qt in range(QT):
                            last = pe.transpose(t.turn[u % 2][:, k * L + qt * P:k * L + (qt + 1) * P],
                                                t.onorm[:, qt, (2 * u + k) * P:(2 * u + k + 1) * P], t.ident[:])
                    last.then_inc(s["o_turned"], 1)
                pe.wait_ge(s["ot_lo"], 4 * b + 4)
                for qt in range(QT):
                    for k in range(8):
                        last = split_product(pe, t.s_ps[qt][:, 0, :], [o[:, k, qt * P:(qt + 1) * P] for o in t.ot],
                                             [w[:, k, :] for w in t.wout], k == 0, k == 7)
                    last.then_inc(s["out_done"], 1)

            with pe.Fori(0, B) as b:
                count, before = counts(pe, b)
                queries(b)
                with pe.Fori(0, count) as i:
                    n = pe.snap(before + i)
                    projections(b, n)
                    for j in range(NG + 4):
                        if j < NG:
                            scores(n, j)
                        if j >= 4:
                            weighted_values(n, j - 4)
                        if 2 <= j < NG + 2:
                            turn_probs(n, j - 2)
                        if j == 6:
                            next_keys(n)
                output_projection(b)

        @block.scalar
        def _(act):
            def softmax_part(n, g):
                act.wait_ge(s["bias_ready"], 8 * n + g + 1)
                act.wait_ge(s["rescaled"], 8 * n + g + 1)
                act.activation(t.alpha[:, GU * g:GU * (g + 1)], t.mdiff[:, GU * g:GU * (g + 1)], ACT.Exp,
                               scale=0.125).then_inc(s["alpha_ready"], 1)
                for u in range(GU):
                    at = GU * g + u
                    last = act.activation(t.probs[g % 3][:, u, :], t.s_sb[g % 2][:, u, :], ACT.Exp,
                                          bias=t.mbias[:, at:at + 1], scale=0.125, accum_out=t.rowsum[:, at:at + 1])
                last.then_inc(s["p_ready"], 1)

            def store_turned(n, g):
                act.wait_ge(s["t_done"], 8 * n + g + 1)
                if g >= 3:
                    act.wait_ge(s["pv_done"], 8 * n + g - 2)
                act.activation(t.pt[g % 3][:, 0:2, :, :].rearrange("p u k q -> p (u k q)"), t.turn[0][:], ACT.Copy
                               ).then_inc(s["pt_act"], 1)

            with act.Fori(0, B) as b:
                count, before = counts(act, b)
                act.wait_ge(s["x_added"], 2 * b + 2)
                act.dma_start(t.xres[:], x_batches[bass.ds(b, 1)].rearrange("o p t d -> (o p) t d")).then_inc(s["x_loaded"], 16)
                for m in range(2):
                    act.wait_ge(s["lat_var"], 2 * b + m + 1)
                    act.activation(t.std[:], t.mv[:, :, 1], ACT.Sqrt, bias=t.eps[:]).then_inc(s["lat_std"], 1)
                act.wait_ge(s["lat_wide"], b + 1)
                act.activation(t.xt[0][:].rearrange("p k n -> p (k n)"), t.wide[:].rearrange("p k n -> p (k n)"), ACT.Copy
                               ).then_inc(s["lat_hi"], 1)
                for u in range(4):
                    act.wait_ge(s["q_done"], 4 * b + u + 1)
                    pair = banks[u % 3][:].rearrange("p (m n) -> p m n", m=2)
                    for o in range(2):
                        for half in (slice(0, DH), slice(DH, P)):
                            last = act.activation(t.qh[half, 4 * u + o:4 * u + 4:2, :], pair[o * DH:(o + 1) * DH], ACT.Copy)
                    last.then_inc(s["q_hi"], 1)
                with act.Fori(0, count) as i:
                    n = act.snap(before + i)
                    for u in range(4):
                        act.wait_ge(s["proj_done"], 8 * n + u + 1)
                        pair = banks[u % 3][:].rearrange("p (m n) -> p m n", m=2)
                        heads = t.kp[0:DH, 4 * u:4 * u + 4, :].rearrange("p (m o) n -> p m o n", o=2)
                        act.activation(heads[:, :, 0, :], pair[0:DH], ACT.Copy)
                        act.activation(heads[:, :, 1, :], pair[DH:P], ACT.Copy).then_inc(s["k_hi"], 1)
                    for u in (4, 6):
                        act.wait_ge(s["proj_done"], 8 * n + u + 1)
                        act.activation(t.v[:, (u - 4) // 2, 0:512], banks[u % 3][:], ACT.Copy).then_inc(s["v_act"], 1)
                    for g in range(NG + 2):
                        if g < NG:
                            softmax_part(n, g)
                        if g >= 2:
                            store_turned(n, g - 2)
                        if g == 2:
                            act.wait_ge(s["var"], n + 1)
                            act.activation(t.std[:], t.mv[:, :, 1], ACT.Sqrt, bias=t.eps[:]).then_inc(s["std"], 1)
                        if g == 7:
                            act.wait_ge(s["wide"], n + 1)
                            act.activation(t.xt[0][:].rearrange("p k n -> p (k n)"),
                                           t.wide[:].rearrange("p k n -> p (k n)"), ACT.Copy).then_inc(s["x_hi"], 1)
                for u in range(4):
                    act.wait_ge(s["o_turned"], 4 * b + u + 1)
                    act.activation(t.ot[0][:, 2 * u:2 * u + 2, :].rearrange("p k n -> p (k n)"), t.turn[u % 2][:], ACT.Copy
                                   ).then_inc(s["ot_hi"], 1)

        @block.gpsimd
        def _(pool):
            with pool.Fori(0, B) as b:
                count, before = counts(pool, b)
                with pool.Fori(0, count) as i:
                    n = pool.snap(before + i)
                    for g in range(NG):
                        cols = slice(GU * g, GU * (g + 1))
                        if g == 0:
                            pool.wait_ge(s["state_zero"], b + 1)
                        pool.wait_ge(s["alpha_ready"], 8 * n + g + 1)
                        pool.wait_ge(s["o_added"], 8 * n + g + 1)
                        pool.tensor_tensor(t.o[:, cols, :], t.o[:, cols, :],
                                           t.alpha[:, cols].unsqueeze(2).broadcast_to([P, GU, DH]), ALU.mult)
                        pool.tensor_tensor(t.den[:, cols], t.den[:, cols], t.alpha[:, cols], ALU.mult).then_inc(s["pool_step"], 1)
                        pool.wait_ge(s["pool_step"], 8 * n + g + 1)
                        pool.wait_ge(s["p_ready"], 8 * n + g + 1)
                        pool.tensor_tensor(t.den[:, cols], t.den[:, cols], t.rowsum[:, cols], ALU.add).then_inc(s["rescaled"], 1)

        @block.vector
        def _(dve):
            dve.memset(t.eps[:], EPS).then_inc(s["s_read"], 2)
            dve.memset(t.pen[:], 0.0).then_inc(s["o_added"], NG)
            dve.memset(t.mbias[:], 0.0).then_inc(s["rescaled"], NG)
            dve.memset(t.mstate[:], 0.0).then_inc(s["z_ready"], 1)
            dve.memset(t.mdiff[:], 0.0).then_inc(s["pen_used"], 1)
            dve.memset(t.std[:], 0.0).then_inc(s["x_added"], 2)
            dve.memset(t.rstd[:], 0.0).then_inc(s["o_norm"], 1)
            dve.memset(t.mnew[:], 0.0).then_inc(s["x_ready"], 1)
            STEPS = 6

            def keys_wide(bank, gain, shift):
                for kc in range(KC):
                    last = dve.tensor_scalar(t.wide[:, kc, :], bank[:, kc * CH:(kc + 1) * CH], t.norm[:, gain, kc:kc + 1],
                                             t.norm[:, shift, kc:kc + 1], ALU.mult, ALU.add)
                return last

            with dve.Fori(0, B) as b:
                count, before = counts(dve, b)
                local = [0]

                def then(ins):
                    local[0] += 1
                    ins.then_inc(s["dve_step"], 1)
                    dve.wait_ge(s["dve_step"], b * STEPS + local[0])

                dve.wait_ge(s["x_loaded"], 16 * b + 16)
                for m, (src, dst) in enumerate(((t.xres, t.z1), (t.z1, t.z))):
                    dve.bn_stats(t.stats[:, 0, :], src[:, 0, :])
                    then(dve.bn_stats(t.stats[:, 1, :], src[:, 1, :]))
                    if m == 0:
                        dve.memset(t.mstate[:], -BIG)
                    else:
                        dve.memset(t.pen[:], 0.0)
                    dve.bn_aggr(t.mv[:, 0, :], t.stats[:, 0, :])
                    dve.bn_aggr(t.mv[:, 1, :], t.stats[:, 1, :]).then_inc(s["lat_var"], 1)
                    dve.wait_ge(s["lat_std"], 2 * b + m + 1)
                    then(dve.reciprocal(t.rstd[:], t.std[:]))
                    for k in range(2):
                        last = dve.tensor_scalar(dst[:, k, :], src[:, k, :], t.mv[:, k, 0:1], t.rstd[:, k:k + 1],
                                                 ALU.subtract, ALU.mult)
                    if m == 0:
                        then(last)
                    else:
                        last.then_inc(s["lat_z"], 1)
                dve.memset(t.den[:], 0.0)
                dve.memset(t.o[:], 0.0).then_inc(s["state_zero"], 1)
                dve.wait_ge(s["lat_turned"], b + 1)
                keys_wide(t.proj, 2, 3).then_inc(s["lat_wide"], 1)
                dve.wait_ge(s["lat_hi"], b + 1)
                dve.tensor_tensor(t.xt[1][:], t.wide[:], t.xt[0][:].bitcast(F32), ALU.subtract).then_inc(s["lat_ready"], 1)
                for u in range(4):
                    dve.wait_ge(s["q_hi"], 4 * b + u + 1)
                    pair = banks[u % 3][:].rearrange("p (m n) -> p m n", m=2)
                    for o in range(2):
                        for half in (slice(0, DH), slice(DH, P)):
                            last = dve.tensor_tensor(t.ql[half, 4 * u + o:4 * u + 4:2, :], pair[o * DH:(o + 1) * DH],
                                                     t.qh[half, 4 * u + o:4 * u + 4:2, :].bitcast(F32), ALU.subtract)
                    last.then_inc(s["q_ready"], 1)

                with dve.Fori(0, count) as i:
                    n = dve.snap(before + i)
                    for u in range(4):
                        dve.wait_ge(s["k_hi"], 4 * n + u + 1)
                        pair = banks[u % 3][:].rearrange("p (m n) -> p m n", m=2)
                        hi = t.kp[0:DH, 4 * u:4 * u + 4, :].rearrange("p (m o) n -> p m o n", o=2).bitcast(F32)
                        lo = t.kp[DH:P, 4 * u:4 * u + 4, :].rearrange("p (m o) n -> p m o n", o=2)
                        dve.tensor_tensor(lo[:, :, 0, :], pair[0:DH], hi[:, :, 0, :], ALU.subtract)
                        dve.tensor_tensor(lo[:, :, 1, :], pair[DH:P], hi[:, :, 1, :], ALU.subtract).then_inc(s["k_ready"], 1)
                    for u in (5, 7):
                        dve.wait_ge(s["proj_done"], 8 * n + u + 1)
                        dve.tensor_copy(t.v[:, (u - 4) // 2, 512:1024], banks[u % 3][:]).then_inc(s["v_dve"], 1)
                    for g in range(NG + 5):
                        if g >= 5:
                            cols = slice(GU * (g - 5), GU * (g - 4))
                            dve.wait_ge(s["pv_done"], 8 * n + g - 4)
                            dve.wait_ge(s["rescaled"], 8 * n + g - 4 + NG)
                            dve.tensor_tensor(t.o[:, cols, :], t.o[:, cols, :], t.pv_ps[:], ALU.add).then_inc(s["o_added"], 1)
                        if g == 1:
                            dve.wait_ge(s["raw_loaded"], 16 * n + 16)
                            dve.bn_stats(t.stats[:, 0, :], t.raw[:, 0, :])
                            dve.bn_stats(t.stats[:, 1, :], t.raw[:, 1, :]).then_inc(s["stats_done"], 1)
                        if g == 3:
                            dve.wait_ge(s["std"], n + 1)
                            dve.reciprocal(t.rstd[:], t.std[:]).then_inc(s["rstd_done"], 1)
                        if g < NG:
                            cols = slice(GU * g, GU * (g + 1))
                            dve.wait_ge(s["s_done"], 8 * n + g + 1)
                            if g >= 2:
                                dve.wait_ge(s["p_ready"], 8 * n + g - 1)
                            dve.memset(t.tick[:], 0.0)
                            for u in range(GU):
                                at = GU * g + u
                                last = dve.tensor_tensor_reduce(
                                    out=t.s_sb[g % 2][:, u, :], in0=t.s_ps[g % 2][:, u, :], in1=t.pen[:], scale=1.0,
                                    scalar=t.mstate[:, at:at + 1], op0=ALU.add, op1=ALU.max, accum_out=t.mnew[:, at:at + 1])
                            last.then_inc(s["s_read"], 1)
                            dve.wait_ge(s["s_read"], 8 * n + g + 3)
                            dve.tensor_tensor(t.mdiff[:, cols], t.mstate[:, cols], t.mnew[:, cols], ALU.subtract)
                            dve.tensor_scalar(t.mbias[:, cols], t.mnew[:, cols], -0.125, None, ALU.mult).then_inc(s["bias_ready"], 1)
                            dve.wait_ge(s["bias_ready"], 8 * n + g + 1)
                            dve.tensor_copy(t.mstate[:, cols], t.mnew[:, cols])
                        if g == 1:
                            dve.bn_aggr(t.mv[:, 0, :], t.stats[:, 0, :])
                            dve.bn_aggr(t.mv[:, 1, :], t.stats[:, 1, :]).then_inc(s["var"], 1)
                        if g == 3:
                            for k in range(2):
                                last = dve.tensor_scalar(t.z[:, k, :], t.raw[:, k, :], t.mv[:, k, 0:1], t.rstd[:, k:k + 1],
                                                         ALU.subtract, ALU.mult)
                            last.then_inc(s["z_ready"], 1)
                        if 2 <= g < NG + 2:
                            dve.wait_ge(s["t_done"], 8 * n + g - 1)
                            if g - 2 >= 3:
                                dve.wait_ge(s["pv_done"], 8 * n + g - 4)
                            dve.tensor_copy(t.pt[(g - 2) % 3][:, 2:4, :, :].rearrange("p u k q -> p (u k q)"), t.turn[1][:]
                                            ).then_inc(s["pt_dve"], 1)
                        if g == 7:
                            dve.wait_ge(s["z_turned"], n + 1)
                            keys_wide(t.proj, 0, 1).then_inc(s["wide"], 1)
                        if g == 9:
                            dve.wait_ge(s["pen_loaded"], 16 * n + 16)
                            dve.tensor_scalar(t.pen[:], t.mask8[:], -1.0, BIG, ALU.add, ALU.mult).then_inc(s["pen_used"], 1)
                            dve.wait_ge(s["x_hi"], n + 1)
                            dve.tensor_tensor(t.xt[1][:], t.wide[:], t.xt[0][:].bitcast(F32), ALU.subtract).then_inc(s["x_ready"], 1)
                dve.wait_ge(s["o_added"], 8 * (before + count) + NG)
                dve.wait_ge(s["rescaled"], 8 * (before + count) + NG)
                then(dve.reciprocal(t.inv[:], t.den[:]))
                dve.tensor_tensor(t.onorm[:].rearrange("p q (h d) -> p h q d", h=H),
                                  t.o[:].rearrange("p (h q) d -> p h q d", q=QT),
                                  t.inv[:].rearrange("p (h q) -> p h q", q=QT).unsqueeze(3).broadcast_to([P, H, QT, DH]),
                                  ALU.mult).then_inc(s["o_norm"], 1)
                for u in range(4):
                    dve.wait_ge(s["ot_hi"], 4 * b + u + 1)
                    out, hi = (o[:, 2 * u:2 * u + 2, :].rearrange("p k n -> p (k n)") for o in (t.ot[1], t.ot[0]))
                    dve.tensor_tensor(out, t.turn[u % 2][:], hi.bitcast(F32), ALU.subtract).then_inc(s["ot_lo"], 1)
                for qt in range(QT):
                    dve.wait_ge(s["out_done"], 2 * b + qt + 1)
                    dve.tensor_tensor(t.x[:, bass.ds(b * QT + qt, 1), :].rearrange("p o n -> p (o n)"), t.xres[:, qt, :],
                                      t.s_ps[qt][:, 0, :], ALU.add).then_inc(s["x_added"], 1)


def split_blocks(w, k, cols):
    return [part[:, k, cols] for part in w]


def attend_stage(nc, t, sems, args):
    s = {n: sems(n) for n in (
        "w_loaded", "w_hi", "w_ready", "mask_loaded", "step", "var", "std", "z_ready", "turned", "xt_hi", "xt_ready",
        "qk_done", "qk_hi", "qk_ready", "v_done", "v_act", "v_dve", "s_done", "s_read", "bias_ready", "p_ready",
        "t_done", "pt_ready", "pv_done", "x_done")}
    with nc.Block() as block:
        @block.sync
        def _(sp):
            for k, name in enumerate("QKV"):
                sp.dma_start(t.w_raw[k][:], args[f"L0_attn_{name}w"].rearrange("(k p) n -> p k n", p=P)).then_inc(s["w_loaded"], 16)
            sp.dma_start(t.causal[:], args["causal"]).then_inc(s["mask_loaded"], 16)

        @block.tensor
        def _(pe):
            for half in range(2):
                pe.wait_ge(s["z_ready"], 4 * half + 4)
                for kc in range(KC):
                    for k in range(4):
                        last = pe.transpose(t.bank[2 * half + kc][:, k * P:(k + 1) * P],
                                            t.z[:, 4 * half + k, kc * P:(kc + 1) * P], t.ident[:])
                    last.then_inc(s["turned"], 1)
            pe.wait_ge(s["w_ready"], 3)
            for half in range(2):
                pe.wait_ge(s["xt_ready"], 2 * half + 2)
                for m in range(4):
                    which, mt = m // 2, m % 2
                    for kc in range(KC):
                        last = split_product(pe, t.bank[(4 + 4 * half + m) % 8][:],
                                             split_blocks(t.w[which], kc, slice(mt * P, (mt + 1) * P)),
                                             split_blocks(t.xt, kc, slice(half * 512, half * 512 + 512)), kc == 0, kc == KC - 1)
                    last.then_inc(s["qk_done"], 1)
            for pair in range(4):
                pe.wait_ge(s["qk_ready"], pair + 1)
                for k in range(2):
                    for kc in range(KC):
                        last = split_product(pe, t.bank[4 + pair][:, k * D:(k + 1) * D],
                                             split_blocks(t.xt, kc, slice((2 * pair + k) * P, (2 * pair + k + 1) * P)),
                                             split_blocks(t.w[2], kc, slice(0, D)), kc == 0, kc == KC - 1)
                last.then_inc(s["v_done"], 1)
            for b in range(B):
                pe.wait_ge(s["qk_ready"], 8)
                for qt in range(QT):
                    for kc in range(KC):
                        last = split_product(pe, t.bank[b][:, qt * L:(qt + 1) * L],
                                             split_blocks(t.qt, kc, slice(b * L + qt * P, b * L + (qt + 1) * P)),
                                             split_blocks(t.kt, kc, slice(b * L, (b + 1) * L)), kc == 0, kc == KC - 1)
                last.then_inc(s["s_done"], 1)
            for b in range(B):
                pe.wait_ge(s["p_ready"], b + 1)
                pe.wait_ge(s["v_act"], 2)
                pe.wait_ge(s["v_dve"], 2)
                for k, (qt, kt) in enumerate(((0, 0), (1, 0), (1, 1))):
                    last = pe.transpose(t.bank[4 + b][:, k * P:(k + 1) * P], t.p[:, 2 * b + qt, kt * P:(kt + 1) * P], t.ident[:])
                last.then_inc(s["t_done"], 1)
            for b in range(B):
                pe.wait_ge(s["pt_ready"], b + 1)
                pe.matmul(t.bank[b][:, 0:D], t.pt[:, b, 0, :], t.v[:, 2 * b, :], start=True, stop=True)
                pe.matmul(t.bank[b][:, D:2 * D], t.pt[:, b, 1, :], t.v[:, 2 * b, :], start=True, stop=False)
                pe.matmul(t.bank[b][:, D:2 * D], t.pt[:, b, 2, :], t.v[:, 2 * b + 1, :], start=False, stop=True
                          ).then_inc(s["pv_done"], 1)

        @block.scalar
        def _(act):
            for k in range(3):
                act.wait_ge(s["w_loaded"], 48)
                act.activation(t.w[k][0][:], t.w_raw[k][:], ACT.Copy).then_inc(s["w_hi"], 1)
            act.wait_ge(s["var"], 1)
            act.activation(t.std[:], t.mv[:, :, 1], ACT.Sqrt, bias=t.eps[:]).then_inc(s["std"], 1)
            for a in range(4):
                half, kc = a // 2, a % 2
                act.wait_ge(s["turned"], a + 1)
                act.activation(t.xt[0][:, kc, half * 512:half * 512 + 512], t.bank[a][:], ACT.Copy).then_inc(s["xt_hi"], 1)
            for c in range(8):
                half, which, mt = c // 4, c % 4 // 2, c % 2
                act.wait_ge(s["qk_done"], c + 1)
                act.activation((t.qt, t.kt)[which][0][:, mt, half * 512:half * 512 + 512], t.bank[(4 + c) % 8][:], ACT.Copy
                               ).then_inc(s["qk_hi"], 1)
            for pair in (0, 2):
                act.wait_ge(s["v_done"], pair + 1)
                act.activation(t.v[:, 2 * pair:2 * pair + 2, :].rearrange("p k n -> p (k n)"), t.bank[4 + pair][:], ACT.Copy
                               ).then_inc(s["v_act"], 1)
            for b in range(B):
                act.wait_ge(s["bias_ready"], b + 1)
                for qt in range(QT):
                    at = 2 * b + qt
                    last = act.activation(t.p[:, at, :], t.s_sb[:, at, :], ACT.Exp, bias=t.bias[:, at:at + 1],
                                          scale=1.0 / 16.0, accum_out=t.rowsum[:, at:at + 1])
                last.then_inc(s["p_ready"], 1)

        @block.vector
        def _(dve):
            step = [0]

            def then(ins):
                step[0] += 1
                ins.then_inc(s["step"], 1)
                dve.wait_ge(s["step"], step[0])

            for k in range(TILES):
                last = dve.bn_stats(t.stats[:, k, :], t.x[:, k, :])
            then(last)
            for k in range(TILES):
                last = dve.bn_aggr(t.mv[:, k, :], t.stats[:, k, :])
            last.then_inc(s["var"], 1)
            dve.wait_ge(s["std"], 1)
            then(dve.reciprocal(t.rstd[:], t.std[:]))
            for k in range(TILES):
                dve.tensor_scalar(t.z[:, k, :], t.x[:, k, :], t.mv[:, k, 0:1], t.rstd[:, k:k + 1], ALU.subtract, ALU.mult
                                  ).then_inc(s["z_ready"], 1)
            for k in range(3):
                dve.wait_ge(s["w_hi"], k + 1)
                dve.tensor_tensor(t.w[k][1][:], t.w_raw[k][:], t.w[k][0][:].bitcast(F32), ALU.subtract).then_inc(s["w_ready"], 1)
            for a in range(4):
                half, kc = a // 2, a % 2
                dve.wait_ge(s["xt_hi"], a + 1)
                hi, lo = (x[:, kc, half * 512:half * 512 + 512] for x in t.xt)
                dve.tensor_tensor(lo, t.bank[a][:], hi.bitcast(F32), ALU.subtract).then_inc(s["xt_ready"], 1)
            for c in range(8):
                half, which, mt = c // 4, c % 4 // 2, c % 2
                dve.wait_ge(s["qk_hi"], c + 1)
                hi, lo = (x[:, mt, half * 512:half * 512 + 512] for x in (t.qt, t.kt)[which])
                dve.tensor_tensor(lo, t.bank[(4 + c) % 8][:], hi.bitcast(F32), ALU.subtract).then_inc(s["qk_ready"], 1)
            for pair in (1, 3):
                dve.wait_ge(s["v_done"], pair + 1)
                dve.tensor_copy(t.v[:, 2 * pair:2 * pair + 2, :].rearrange("p k n -> p (k n)"), t.bank[4 + pair][:]
                                ).then_inc(s["v_dve"], 1)
            dve.wait_ge(s["mask_loaded"], 16)
            for b in range(B):
                dve.wait_ge(s["s_done"], b + 1)
                for qt in range(QT):
                    at = 2 * b + qt
                    last = dve.tensor_tensor_reduce(
                        out=t.s_sb[:, at, :], in0=t.bank[b][:, qt * L:(qt + 1) * L], in1=t.causal[:, qt, :], scale=1.0,
                        scalar=-BIG, op0=ALU.add, op1=ALU.max, accum_out=t.mx[:, at:at + 1])
                then(last)
                dve.tensor_scalar(t.bias[:, 2 * b:2 * b + 2], t.mx[:, 2 * b:2 * b + 2], -1.0 / 16.0, None, ALU.mult
                                  ).then_inc(s["bias_ready"], 1)
            for b in range(B):
                dve.wait_ge(s["t_done"], b + 1)
                dve.tensor_copy(t.pt[:, b, :, :].rearrange("p k q -> p (k q)"), t.bank[4 + b][:, 0:3 * P]).then_inc(s["pt_ready"], 1)
            then(dve.reciprocal(t.inv[:], t.rowsum[:]))
            for b in range(B):
                dve.wait_ge(s["pv_done"], b + 1)
                for qt in range(QT):
                    at = 2 * b + qt
                    last = dve.scalar_tensor_tensor(out=t.x[:, at, :], in0=t.bank[b][:, qt * D:(qt + 1) * D],
                                                    scalar=t.inv[:, at:at + 1], in1=t.x[:, at, :], op0=ALU.mult, op1=ALU.add)
            last.then_inc(s["x_done"], 1)
            dve.wait_ge(s["x_done"], 1)


ORDER = ("B0 B1 C0 C1 B2 B3 D0 E0 C2 C3 B4 B5 D1 E1 C4 C5 B6 B7 D2 E2 C6 C7 D3 E3").split()


def transformer_stage(nc, t, sems, args, out):
    names = (
        "const_loaded", "vec_loaded", "stage_loaded", "split_done",
        "table_step", "tables_ready", "first_var", "first_std", "y_ready", "turned", "xt_hi", "xt_ready", "edge_ready",
        "qkv_done", "qkv_copied", "squared", "reduced", "rooted", "cos_part", "rotated", "c_done", "c_hi", "c_ready",
        "s_done", "s_read", "bias_ready", "p_ready", "t_done", "pt_act", "pt_dve", "pv_done", "o_half",
        "o_turned", "o_hi", "o_ready", "e_done", "e_added", "half_stats", "stats_shifted", "var", "std", "mv_ready",
        "mv_shifted", "edge_row", "edge_done", "z_ready", "wide_ready", "up_done", "gelu_done", "gated", "u_hi", "u_ready",
        "down_done", "b2_added", "step", "first_step", "split_step", "result", "stored")
    s = {n: sems(n) for n in names}
    HEADS = LH * B
    STEPS = 4 * TILES + HEADS + 2 * B

    def halves(bank):
        return bank[:].rearrange("p (b n) -> p b n", b=2)

    def keys_of(h):
        return ((0, slice(0, P), slice(0, P)), (1, slice(P, 3 * P), slice(0, L)))

    with nc.Block() as block:
        @block.sync
        def _(sp):
            sp.dma_start(t.rot_cos[:], args["rot_cos"]).then_inc(s["const_loaded"], 16)
            sp.dma_start(t.rot_sin[:], args["rot_sin"]).then_inc(s["const_loaded"], 16)
            sp.dma_start(t.window[:], args["window"]).then_inc(s["const_loaded"], 16)
            sp.dma_start(t.staging[:].rearrange("p (k n) -> p k n", k=KC),
                         args["L0_ffn_wqkv"][0].rearrange("(k p) n -> p k n", p=P)).then_inc(s["stage_loaded"], 16)
            sp.wait_ge(s["split_step"], 1)
            with sp.Fori(0, DEPTH) as l:
                def layer(name):
                    return args[f"L0_ffn_{name}"][bass.ds(l, 1)]

                def load(dst, src, sem):
                    sp.dma_start(dst, src).then_inc(s[sem], 16)

                sp.wait_ge(s["y_ready"], 8 * l + 8)
                with nc.allow_non_contiguous_dma("vectors onto the partitions"):
                    load(t.scales[:, 0, :], layer("q_scale").partition_broadcast(P).rearrange("p o n -> p (o n)"), "vec_loaded")
                    load(t.scales[:, 1, :], layer("k_scale").partition_broadcast(P).rearrange("p o n -> p (o n)"), "vec_loaded")
                    load(t.ln[:, 0, :], layer("ln_g").rearrange("o (k p) -> p (o k)", p=P), "vec_loaded")
                    load(t.ln[:, 1, :], layer("ln_b").rearrange("o (k p) -> p (o k)", p=P), "vec_loaded")
                    load(t.b2[:], layer("b2").partition_broadcast(P).rearrange("p o n -> p (o n)"), "vec_loaded")
                    for side in range(2):
                        b1 = layer("b1")[:, side * HID:(side + 1) * HID]
                        load(t.b1[:, side, 0:5], b1[:, 0:5 * P].rearrange("o (m p) -> p (o m)", p=P), "vec_loaded")
                        load(t.b1[0:HID - 5 * P, side, 5:6], b1[:, 5 * P:HID].rearrange("o (m p) -> p (o m)", m=1), "vec_loaded")
                sp.wait_ge(s["split_done"], 4 * l + 1)
                load(t.staging[:, 0:4 * D].rearrange("p (k n) -> p k n", k=4),
                     layer("wo").rearrange("o (k p) n -> p (o k) n", p=P), "stage_loaded")
                sp.wait_ge(s["split_done"], 4 * l + 2)
                load(t.staging[:, 0:4 * HID].rearrange("p (k n) -> p k n", k=KC),
                     layer("w1").rearrange("o (k p) n -> p (o k) n", p=P), "stage_loaded")
                sp.wait_ge(s["half_stats"], l + 1)
                tails = t.tail_stats[:].rearrange("p (b q) n -> p b q n", q=2)
                stats = t.stats[:].rearrange("p (b q) n -> p b q n", q=2)
                load(t.stats[1:P, :, 6:12], t.tail_stats[0:P - 1, :, :], "stats_shifted")
                load(stats[0:1, :, 1, 6:12], tails[P - 1:P, :, 0, :], "stats_shifted")
                sp.wait_ge(s["mv_ready"], l + 1)
                up = t.mv_up[:].rearrange("p (b q) n -> p b q n", q=2)
                mv = t.mv[:].rearrange("p (b q) n -> p b q n", q=2)
                load(t.mv_up[0:P - 1, :, :], t.mv[1:P, :, :], "mv_shifted")
                load(up[P - 1:P, :, 0, :], mv[0:1, :, 1, :], "mv_shifted")
                sp.wait_ge(s["split_done"], 4 * l + 3)
                load(t.staging[:, 0:5 * D].rearrange("p (k n) -> p k n", k=5),
                     layer("w2")[:, 0:5 * P, :].rearrange("o (k p) n -> p (o k) n", p=P), "stage_loaded")
                load(t.staging[0:HID - 5 * P, 5 * D:6 * D], layer("w2")[:, 5 * P:HID, :].rearrange("o k n -> (o k) n"),
                     "stage_loaded")
                sp.wait_ge(s["split_done"], 4 * l + 4)
                load(t.staging[:].rearrange("p (k n) -> p k n", k=KC),
                     args["L0_ffn_wqkv"][DEPTH - 1].rearrange("(k p) n -> p k n", p=P), "stage_loaded")
            sp.wait_ge(s["result"], 1)
            sp.dma_start(out.rearrange("b (t p) d -> p (b t) d", p=P), t.x[:]).then_inc(s["stored"], 16)
            sp.wait_ge(s["stored"], 16)
            sp.wait_ge(s["split_done"], 4 * DEPTH + 1)

        @block.gpsimd
        def _(pool):
            for part in t.w1 + t.w2:
                pool.memset(part[:].bitcast(F32), 0.0)
            pool.memset(t.tick[:], 0.0)
            pool.memset(t.b1[:], 0.0).then_inc(s["split_step"], 1)
            pool.wait_ge(s["split_step"], 1)

            def split(parts, raw, loads, base):
                hi, lo = parts
                pool.wait_ge(s["stage_loaded"], loads)
                pool.tensor_tensor(t.tick[:, 1:2], t.tick[:, 0:1], t.tick[:, 0:1], ALU.add)
                for k in range(len(raw)):
                    last = pool.tensor_copy(hi[k], raw[k])
                last.then_inc(s["split_step"], 1)
                pool.wait_ge(s["split_step"], base)
                for k in range(len(raw)):
                    last = pool.tensor_tensor(lo[k], raw[k], hi[k].bitcast(F32), ALU.subtract)
                last.then_inc(s["split_done"], 1)

            whole = t.staging[:].rearrange("p (k n) -> p k n", k=KC)
            split([[w[:]] for w in t.wqkv], [whole], 16, 2)
            with pool.Fori(0, DEPTH) as l:
                def cosines(i):
                    pool.wait_ge(s["qkv_copied"], 24 * l + 3 * i + 2)
                    if i:
                        pool.wait_ge(s["rotated"], 8 * l + i)
                    for w in range(2):
                        last = pool.tensor_tensor(
                            t.cos_part[:, w, :, :], t.qk_sb[i % 2][:, w, :].rearrange("p (h d) -> p h d", h=LH),
                            t.cos[:, i % 2, w, :].unsqueeze(1).broadcast_to([P, LH, LDH]), ALU.mult)
                    last.then_inc(s["cos_part"], 1)

                pool.wait_ge(s["vec_loaded"], 144 * l + 144)
                pool.wait_ge(s["const_loaded"], 48)
                for q in range(QT):
                    pool.tensor_tensor(t.cos[:, q], t.rot_cos[:, q], t.scales[:], ALU.mult)
                    for a, b in ((0, 32), (32, 0)):
                        last = pool.tensor_tensor(t.sin[:, q, :, a:a + 32], t.rot_sin[:, q, :, a:a + 32],
                                                  t.scales[:, :, b:b + 32], ALU.mult)
                last.then_inc(s["tables_ready"], 1)
                pool.wait_ge(s["tables_ready"], l + 1)
                for step in ORDER:
                    if step[0] == "B":
                        cosines(int(step[1]))
                    if step == "C0":
                        split([[w[:]] for w in t.wo], [t.staging[:, 0:4 * D].rearrange("p (k n) -> p k n", k=4)],
                              80 * l + 32, 4 * l + 3)
                sides = [w[:].rearrange("p k (s n) -> p k s n", s=2)[:, :, :, 0:HID] for w in t.w1]
                raw = t.staging[:, 0:4 * HID].rearrange("p (k s n) -> p k s n", k=KC, s=2)
                split([[w[:, k] for k in range(KC)] for w in sides], [raw[:, k] for k in range(KC)], 80 * l + 48, 4 * l + 4)
                pool.wait_ge(s["z_ready"], 2 * l + 2)
                pool.tensor_tensor(t.y[:], t.y[:], t.b2[:].unsqueeze(1).broadcast_to([P, TILES, D]), ALU.add).then_inc(s["b2_added"], 1)
                split([[w[:, 0:5, :], w[0:HID - 5 * P, 5, :]] for w in t.w2],
                      [t.staging[:, 0:5 * D].rearrange("p (k n) -> p k n", k=5), t.staging[0:HID - 5 * P, 5 * D:6 * D]],
                      80 * l + 80, 4 * l + 5)
                split([[w[:]] for w in t.wqkv], [whole], 80 * l + 96, 4 * l + 6)

        @block.tensor
        def _(pe):
            with pe.Fori(0, DEPTH) as l:
                def turn_latents(src, ready, value):
                    for a in range(4):
                        half, kc = a // 2, a % 2
                        if kc == 0:
                            pe.wait_ge(s[ready], value(half))
                        for k in range(4):
                            last = pe.transpose(t.bank[a][:, k * P:(k + 1) * P], src[:, 4 * half + k, kc * P:(kc + 1) * P], t.ident[:])
                        last.then_inc(s["turned"], 1)

                def project(i):
                    if i == 0:
                        pe.wait_ge(s["xt_ready"], 8 * l + 4)
                        pe.wait_ge(s["split_done"], 4 * l + 1)
                    b, q = i // 2, i % 2
                    for w in range(3):
                        if i:
                            pe.wait_ge(s["qkv_copied"], 24 * l + 3 * (i - 1) + w + 1)
                        for kc in range(KC):
                            last = split_product(pe, t.bank[w][:], [x[:, kc, b, q * P:(q + 1) * P] for x in t.xt],
                                                 split_blocks(t.wqkv, kc, slice(w * LI, (w + 1) * LI)), kc == 0, kc == KC - 1)
                        last.then_inc(s["qkv_done"], 1)

                def turn_heads(i):
                    pe.wait_ge(s["rotated"], 8 * l + i + 1)
                    for c in range(3):
                        if i or c:
                            pe.wait_ge(s["c_ready"], 24 * l + 3 * i + c)
                        for k in range(4):
                            src = t.rot_k[i % 2][:, k * P:(k + 1) * P] if c == 2 else \
                                t.rot_q[i % 2][:, 4 * c + k, :, :].rearrange("p o d -> p (o d)")
                            last = pe.transpose(t.bank[3][:, k * P:(k + 1) * P], src, t.ident[:])
                        last.then_inc(s["c_done"], 1)

                def attend(b):
                    n = 32 * l + 8 * b
                    for j in range(LH + 3):
                        if j < LH:
                            if j == 0:
                                pe.wait_ge(s["c_ready"], 24 * l + 6 * b + 6)
                            if j >= 2:
                                pe.wait_ge(s["s_read"], n + j - 1)
                            for q, cols, keys in keys_of(j):
                                pe.matmul(t.bank[4 + j % 2][:, cols], t.qh[:, j, q * P:(q + 1) * P], t.kp[:, j, keys], start=True, stop=False)
                                last = pe.matmul(t.bank[4 + j % 2][:, cols], t.ql[:, j, q * P:(q + 1) * P], t.kp[:, j, keys], start=False, stop=True)
                            last.then_inc(s["s_done"], 1)
                        if j >= 3:
                            h = j - 3
                            pe.wait_ge(s["pt_act" if h % 2 else "pt_dve"], 16 * l + 4 * b + h // 2 + 1)
                            if h == 4:
                                pe.wait_ge(s["o_half"], 8 * l + 2 * b + 1)
                            o = t.bank[7][:].rearrange("p (q h d) -> p q h d", q=QT, h=4)
                            v = [t.v[:, (2 * b + k) % 4, h * LDH:(h + 1) * LDH] for k in range(2)]
                            pe.matmul(o[:, 0, h % 4, :], t.pt[h % 2][:, 0, :], v[0], start=True, stop=True)
                            pe.matmul(o[:, 1, h % 4, :], t.pt[h % 2][:, 1, :], v[0], start=True, stop=False)
                            pe.matmul(o[:, 1, h % 4, :], t.pt[h % 2][:, 2, :], v[1], start=False, stop=True).then_inc(s["pv_done"], 1)
                        if 2 <= j < LH + 2:
                            h = j - 2
                            pe.wait_ge(s["p_ready"], n + h + 1)
                            if h == 0 and b:
                                pe.wait_ge(s["e_added"], 8 * l + 2 * b)
                            if h:
                                pe.wait_ge(s["pt_dve" if h % 2 else "pt_act"], 16 * l + 4 * b + (h + 1) // 2)
                            for k in range(3):
                                last = pe.transpose(t.bank[6][:, k * P:(k + 1) * P], t.p[h % 4][:, k * P:(k + 1) * P], t.ident[:])
                            last.then_inc(s["t_done"], 1)

                def project_output(b):
                    if b == 0:
                        pe.wait_ge(s["split_done"], 4 * l + 2)
                    pe.wait_ge(s["o_half"], 8 * l + 2 * b + 2)
                    for q in range(QT):
                        if q:
                            pe.wait_ge(s["o_ready"], 8 * l + 2 * b + q)
                        for k in range(4):
                            last = pe.transpose(t.bank[6][:, k * P:(k + 1) * P], t.o[:, q, k * P:(k + 1) * P], t.ident[:])
                        last.then_inc(s["o_turned"], 1)
                    for q in range(QT):
                        pe.wait_ge(s["o_ready"], 8 * l + 2 * b + q + 1)
                        for k in range(4):
                            last = split_product(pe, t.bank[7 - q][:, 0:D], [o[:, q, k, :] for o in t.ot],
                                                 [w[:, k, :] for w in t.wo], k == 0, k == 3)
                        last.then_inc(s["e_done"], 1)

                def up(k):
                    half, m = k // 6, k % 6
                    if m == 0:
                        pe.wait_ge(s["xt_ready"], 8 * l + 4 + 2 * half + 2)
                    if k == 0:
                        pe.wait_ge(s["xt_ready"], 8 * l + 8)
                        pe.wait_ge(s["split_done"], 4 * l + 3)
                    if k >= 3:
                        pe.wait_ge(s["gated"], 12 * l + k - 2)
                    for side, bank in ((1, t.pairs[k % 3][0]), (0, t.pairs[k % 3][1])):
                        for kc in range(KC):
                            last = split_product(pe, halves(bank), [w[:, kc, side * 768 + m * P:side * 768 + (m + 1) * P] for w in t.w1],
                                                 [x[:, kc, 2 * half:2 * half + 2, 0:L] for x in t.xt], kc == 0, kc == KC - 1)
                        last.then_inc(s["up_done"], 1)

                def down(half):
                    pe.wait_ge(s["u_ready"], 12 * l + 6 * half + 6)
                    if half == 0:
                        pe.wait_ge(s["split_done"], 4 * l + 4)
                    for k in range(4):
                        tile = 4 * half + k
                        if tile >= 2:
                            pe.wait_ge(s["y_ready"], 8 * l + 8 + tile - 1)
                        for m in range(HB):
                            last = split_product(pe, t.bank[(4, 7)[tile % 2]][:, 0:D], [u[:, m, k * P:(k + 1) * P] for u in t.u],
                                                 [w[:, m, :] for w in t.w2], m == 0, m == HB - 1)
                        last.then_inc(s["down_done"], 1)

                turn_latents(t.y, "y_ready", lambda half: 8 * l + 8)
                for step in ORDER:
                    {"B": project, "C": turn_heads, "D": attend, "E": project_output}[step[0]](int(step[1]))
                pe.wait_ge(s["edge_row"], l + 1)
                pe.matmul(t.bank[4][:, 0:B], t.ones[:], t.edge[:], start=True, stop=True).then_inc(s["edge_done"], 1)
                turn_latents(t.z, "z_ready", lambda half: 2 * l + half + 1)
                for k in range(8):
                    up(k)
                down(0)
                for k in range(8, 12):
                    up(k)
                down(1)

        @block.scalar
        def _(act):
            act.wait_ge(s["first_var"], 1)
            act.activation(t.std[:], t.mv[:, :, 1], ACT.Sqrt, bias=t.eps[:]).then_inc(s["first_std"], 1)
            with act.Fori(0, DEPTH) as l:
                def store_tile(i):
                    for w in range(3):
                        act.wait_ge(s["qkv_done"], 24 * l + 3 * i + w + 1)
                        if w == 0 and i >= 2:
                            act.wait_ge(s["rotated"], 8 * l + i - 1)
                        dst = t.qk_sb[i % 2][:, w, :] if w < 2 else t.v[:, i % 4, :]
                        act.activation(dst, t.bank[w][:], ACT.Copy).then_inc(s["qkv_copied"], 1)
                    act.wait_ge(s["qkv_copied"], 24 * l + 3 * i + 3)
                    if i:
                        act.wait_ge(s["reduced"], 8 * l + i)
                    act.activation(t.squares[:], t.qk_sb[i % 2][:], ACT.Square).then_inc(s["squared"], 1)
                    act.wait_ge(s["reduced"], 8 * l + i + 1)
                    act.activation(t.norms[:], t.sums[:], ACT.Sqrt).then_inc(s["rooted"], 1)

                def store_heads(i):
                    q = slice((i % 2) * P, (i % 2 + 1) * P)
                    for c in range(3):
                        act.wait_ge(s["c_done"], 24 * l + 3 * i + c + 1)
                        bank = t.bank[3][:].rearrange("p (k n) -> p k n", k=4)
                        if c < 2:
                            act.activation(t.qh[:, 4 * c:4 * c + 4, q], bank, ACT.Copy).then_inc(s["c_hi"], 1)
                        else:
                            act.activation(t.kp[0:LDH, 0:LH:2, q], bank[0:LDH], ACT.Copy)
                            act.activation(t.kp[0:LDH, 1:LH:2, q], bank[LDH:P], ACT.Copy).then_inc(s["c_hi"], 1)

                def attend(b):
                    n = 32 * l + 8 * b
                    for j in range(LH + 2):
                        if j < LH:
                            act.wait_ge(s["bias_ready"], n + j + 1)
                            for q, cols, _ in keys_of(j):
                                last = act.activation(t.p[j % 4][:, cols], t.p[j % 4][:, cols], ACT.Exp,
                                                      bias=t.bias[:, j, q:q + 1], scale=t.q_norm[:, 2 * b + q, j:j + 1],
                                                      accum_out=t.rowsum[:, j, q:q + 1])
                            last.then_inc(s["p_ready"], 1)
                        if j >= 2 and j % 2:
                            h = j - 2
                            act.wait_ge(s["t_done"], n + h + 1)
                            if h >= 2:
                                act.wait_ge(s["pv_done"], n + h - 1)
                            act.activation(t.pt[h % 2][:].rearrange("p k q -> p (k q)"), t.bank[6][:, 0:3 * P], ACT.Copy
                                           ).then_inc(s["pt_act"], 1)

                def store_output(b):
                    for q in range(QT):
                        act.wait_ge(s["o_turned"], 8 * l + 2 * b + q + 1)
                        act.activation(t.ot[0][:, q, :, :].rearrange("p k n -> p (k n)"), t.bank[6][:], ACT.Copy).then_inc(s["o_hi"], 1)

                for a in range(4):
                    half, kc = a // 2, a % 2
                    act.wait_ge(s["turned"], 8 * l + a + 1)
                    act.activation(t.xt[0][:, kc, 2 * half:2 * half + 2, kc:kc + L], halves(t.bank[a]), ACT.Copy).then_inc(s["xt_hi"], 1)
                for step in ORDER:
                    {"B": store_tile, "C": store_heads, "D": attend, "E": store_output}[step[0]](int(step[1]))
                act.wait_ge(s["var"], l + 1)
                act.activation(t.std[:], t.mv[:, :, 1], ACT.Sqrt, bias=t.eps[:]).then_inc(s["std"], 1)
                for a in range(4):
                    half, kc = a // 2, a % 2
                    act.wait_ge(s["wide_ready"], 4 * l + a + 1)
                    act.activation(t.xt[0][:, kc, 2 * half:2 * half + 2, 0:L + kc], t.wide[:, kc, 2 * half:2 * half + 2, 0:L + kc],
                                   ACT.Copy).then_inc(s["xt_hi"], 1)

                def gelu(k):
                    act.wait_ge(s["up_done"], 24 * l + 2 * k + 1)
                    if k >= 2:
                        act.wait_ge(s["gated"], 12 * l + k - 1)
                    act.activation(t.gelu[k % 2][:], t.pairs[k % 3][0][:], ACT.Gelu, bias=t.b1[:, 1, k % 6:k % 6 + 1]
                                   ).then_inc(s["gelu_done"], 1)

                def hidden_hi(k):
                    act.wait_ge(s["gated"], 12 * l + k + 1)
                    if k == 6:
                        act.wait_ge(s["down_done"], 8 * l + 4)
                    act.activation(t.u[0][:, k % 6, :], t.hidden[k % 2][:], ACT.Copy).then_inc(s["u_hi"], 1)

                for k in range(12):
                    gelu(k)
                    if k:
                        hidden_hi(k - 1)
                hidden_hi(11)

        @block.vector
        def _(dve):
            first = [0]

            def at_first(ins):
                first[0] += 1
                ins.then_inc(s["first_step"], 1)
                dve.wait_ge(s["first_step"], first[0])

            dve.memset(t.ones[:], 1.0)
            dve.memset(t.mv_up[:], 0.0)
            at_first(dve.memset(t.stats[:], 0.0))
            for k in (6, 9):
                last = dve.memset(t.stats[0:1, 0:TILES:2, k:k + 1], 64.0)
            at_first(last)
            for k in range(TILES):
                last = dve.bn_stats(t.tail_stats[:, k, :], t.x[:, k, :])
            at_first(last)
            for k in range(TILES):
                last = dve.bn_aggr(t.mv[:, k, :], t.tail_stats[:, k, :])
            last.then_inc(s["first_var"], 1)
            dve.wait_ge(s["first_std"], 1)
            at_first(dve.reciprocal(t.rstd[:], t.std[:]))
            for k in range(TILES):
                dve.tensor_scalar(t.y[:, k, :], t.x[:, k, :], t.mv[:, k, 0:1], t.rstd[:, k:k + 1], ALU.subtract, ALU.mult
                                  ).then_inc(s["y_ready"], 1)

            with dve.Fori(0, DEPTH) as l:
                step_count = [0]

                def then(ins):
                    step_count[0] += 1
                    ins.then_inc(s["step"], 1)
                    dve.wait_ge(s["step"], STEPS * l + step_count[0])

                def low_part(lo, full, hi):
                    return dve.tensor_tensor(lo, full, hi.bitcast(F32), ALU.subtract)

                def rotate_tile(i):
                    qk = t.qk_sb[i % 2][:].rearrange("p w (h d) -> p w h d", h=LH)
                    dve.wait_ge(s["qkv_copied"], 24 * l + 3 * i + 2)
                    if i == 0:
                        dve.wait_ge(s["tables_ready"], l + 1)
                    for a, b in ((0, 32), (32, 0)):
                        for w in range(2):
                            last = dve.tensor_tensor(t.sin_part[:, w, :, a:a + 32], qk[:, w, :, b:b + 32],
                                                     t.sin[:, i % 2, w, a:a + 32].unsqueeze(1).broadcast_to([P, LH, 32]), ALU.mult)
                    dve.wait_ge(s["squared"], 8 * l + i + 1)
                    dve.tensor_reduce(t.sums[:], t.squares[:].rearrange("p w (h d) -> p (w h) d", h=LH), X_AXIS, ALU.add
                                      ).then_inc(s["reduced"], 1)
                    dve.wait_ge(s["reduced"], 8 * l + i + 1)
                    dve.wait_ge(s["cos_part"], 8 * l + i + 1)
                    if i >= 2:
                        dve.wait_ge(s["c_done"], 24 * l + 3 * (i - 1))
                    dve.tensor_tensor(t.rot_q[i % 2][:], t.cos_part[:, 0].unsqueeze(2).broadcast_to([P, LH, 2, LDH]),
                                      t.sin_part[:, 0].unsqueeze(2).broadcast_to([P, LH, 2, LDH]), ALU.add)
                    k_view = t.rot_k[i % 2][:].rearrange("p (h d) -> p h d", h=LH)
                    then(dve.tensor_tensor(k_view, t.cos_part[:, 1], t.sin_part[:, 1], ALU.add))
                    dve.wait_ge(s["rooted"], 8 * l + i + 1)
                    then(dve.tensor_scalar(t.norms_kept[:], t.norms[:], 1e-12, None, ALU.max))
                    then(dve.reciprocal(t.inverses[:], t.norms_kept[:]))
                    dve.tensor_scalar(t.q_norm[:, i, :], t.inverses[:, 0:LH], 8.0, None, ALU.mult)
                    dve.tensor_tensor(k_view, k_view, t.inverses[:, LH:2 * LH].unsqueeze(2).broadcast_to([P, LH, LDH]), ALU.mult
                                      ).then_inc(s["rotated"], 1)
                    then(dve.memset(t.tick_dve[:], 0.0))

                def store_heads(i):
                    q = slice((i % 2) * P, (i % 2 + 1) * P)
                    for c in range(3):
                        dve.wait_ge(s["c_hi"], 24 * l + 3 * i + c + 1)
                        bank = t.bank[3][:].rearrange("p (k n) -> p k n", k=4)
                        if c < 2:
                            last = low_part(t.ql[:, 4 * c:4 * c + 4, q], bank, t.qh[:, 4 * c:4 * c + 4, q])
                        else:
                            low_part(t.kp[LDH:P, 0:LH:2, q], bank[0:LDH], t.kp[0:LDH, 0:LH:2, q])
                            last = low_part(t.kp[LDH:P, 1:LH:2, q], bank[LDH:P], t.kp[0:LDH, 1:LH:2, q])
                        last.then_inc(s["c_ready"], 1)

                def normalise(b, half):
                    dve.wait_ge(s["pv_done"], 32 * l + 8 * b + 4 * half + 4)
                    then(dve.reciprocal(t.inv[:], t.rowsum[:, 4 * half:4 * half + 4, :]))
                    o = t.bank[7][:].rearrange("p (q h d) -> p q h d", q=QT, h=4)
                    for q in range(QT):
                        last = dve.tensor_tensor(t.o[:, q, half * L:(half + 1) * L].rearrange("p (h d) -> p h d", h=4), o[:, q],
                                                 t.inv[:, :, q].unsqueeze(2).broadcast_to([P, 4, LDH]), ALU.mult)
                    last.then_inc(s["o_half"], 1)

                def attend(b):
                    n = 32 * l + 8 * b
                    for j in range(LH + 2):
                        if j == 7:
                            normalise(b, 0)
                        if j < LH:
                            dve.wait_ge(s["s_done"], n + j + 1)
                            if j >= 4:
                                dve.wait_ge(s["t_done"], n + j - 3)
                            dve.memset(t.tick_dve[:], 0.0)
                            for q, cols, _ in keys_of(j):
                                last = dve.tensor_tensor_reduce(
                                    out=t.p[j % 4][:, cols], in0=t.bank[4 + j % 2][:, cols], in1=t.window[:, cols], scale=1.0,
                                    scalar=-BIG, op0=ALU.add, op1=ALU.max, accum_out=t.mx[:, j, q:q + 1])
                            last.then_inc(s["s_read"], 1)
                            dve.wait_ge(s["s_read"], n + j + 1)
                            dve.scalar_tensor_tensor(out=t.bias[:, j, :], in0=t.mx[:, j, :], scalar=-1.0,
                                                     in1=t.q_norm[:, 2 * b:2 * b + 2, j], op0=ALU.mult, op1=ALU.mult
                                                     ).then_inc(s["bias_ready"], 1)
                            then(dve.memset(t.tick_dve[:], 0.0))
                        if j >= 2 and j % 2 == 0:
                            h = j - 2
                            dve.wait_ge(s["t_done"], n + h + 1)
                            if h >= 2:
                                dve.wait_ge(s["pv_done"], n + h - 1)
                            dve.tensor_copy(t.pt[h % 2][:].rearrange("p k q -> p (k q)"), t.bank[6][:, 0:3 * P]).then_inc(s["pt_dve"], 1)
                    normalise(b, 1)

                def store_output(b):
                    for q in range(QT):
                        dve.wait_ge(s["o_hi"], 8 * l + 2 * b + q + 1)
                        lo, hi = (o[:, q, :, :].rearrange("p k n -> p (k n)") for o in (t.ot[1], t.ot[0]))
                        low_part(lo, t.bank[6][:], hi).then_inc(s["o_ready"], 1)
                    for q in range(QT):
                        dve.wait_ge(s["e_done"], 8 * l + 2 * b + q + 1)
                        dve.tensor_tensor(t.y[:, 2 * b + q, :], t.y[:, 2 * b + q, :], t.bank[7 - q][:, 0:D], ALU.add
                                          ).then_inc(s["e_added"], 1)

                dve.wait_ge(s["y_ready"], 8 * l + 8)
                for part in t.xt:
                    last = dve.memset(part[:, 1, :, 0:1].bitcast(F32), 0.0)
                for a in range(4):
                    half, kc = a // 2, a % 2
                    dve.wait_ge(s["xt_hi"], 8 * l + a + 1)
                    lo, hi = (x[:, kc, 2 * half:2 * half + 2, kc:kc + L] for x in (t.xt[1], t.xt[0]))
                    low_part(lo, halves(t.bank[a]), hi).then_inc(s["xt_ready"], 1)
                for step in ORDER:
                    {"B": rotate_tile, "C": store_heads, "D": attend, "E": store_output}[step[0]](int(step[1]))

                dve.wait_ge(s["e_added"], 8 * l + 8)
                for k in range(TILES):
                    dve.bn_stats(t.stats[:, k, 0:6], t.y[:, k, 0:P])
                    last = dve.bn_stats(t.tail_stats[:, k, :], t.y[:, k, P:D])
                last.then_inc(s["half_stats"], 1)
                dve.wait_ge(s["stats_shifted"], 32 * l + 32)
                dve.memset(t.tick_dve[:], 0.0)
                for k in range(TILES):
                    last = dve.bn_aggr(t.mv[:, k, :], t.stats[:, k, :])
                last.then_inc(s["var"], 1)
                dve.wait_ge(s["std"], l + 1)
                dve.reciprocal(t.mv[:, :, 1], t.std[:]).then_inc(s["mv_ready"], 1)
                dve.wait_ge(s["mv_ready"], l + 1)
                dve.scalar_tensor_tensor(out=t.edge[:], in0=t.mv[0:1, 0:TILES:2, 0], scalar=-1.0, in1=t.mv[0:1, 0:TILES:2, 1],
                                         op0=ALU.mult, op1=ALU.mult).then_inc(s["edge_row"], 1)
                for k in range(TILES):
                    dve.tensor_scalar(t.z[:, k, 0:P], t.y[:, k, 0:P], t.mv[:, k, 0:1], t.mv[:, k, 1:2], ALU.subtract, ALU.mult)
                dve.wait_ge(s["mv_shifted"], 32 * l + 32)
                for k in range(TILES):
                    last = dve.tensor_scalar(t.z[:, k, P:D], t.y[:, k, P:D], t.mv_up[:, k, 0:1], t.mv_up[:, k, 1:2], ALU.subtract, ALU.mult)
                    if k % 4 == 3:
                        last.then_inc(s["z_ready"], 1)
                dve.wait_ge(s["edge_done"], l + 1)
                dve.tensor_scalar(t.wide[:, 1, :, 0], t.bank[4][:, 0:B], t.ln[:, 0, 1:2], t.ln[:, 1, 1:2], ALU.mult, ALU.add)
                for a in range(4):
                    half, kc = a // 2, a % 2
                    dve.wait_ge(s["turned"], 8 * l + 4 + a + 1)
                    dve.tensor_scalar(t.wide[:, kc, 2 * half:2 * half + 2, kc:kc + L], halves(t.bank[a]), t.ln[:, 0, kc:kc + 1],
                                      t.ln[:, 1, kc:kc + 1], ALU.mult, ALU.add).then_inc(s["wide_ready"], 1)
                for a in range(4):
                    half, kc = a // 2, a % 2
                    dve.wait_ge(s["xt_hi"], 8 * l + 4 + a + 1)
                    lo, hi, full = (x[:, kc, 2 * half:2 * half + 2, 0:L + kc] for x in (t.xt[1], t.xt[0], t.wide))
                    low_part(lo, full, hi).then_inc(s["xt_ready"], 1)

                def gate(k):
                    dve.wait_ge(s["up_done"], 24 * l + 2 * k + 2)
                    dve.wait_ge(s["gelu_done"], 12 * l + k + 1)
                    if k >= 2:
                        dve.wait_ge(s["u_ready"], 12 * l + k - 1)
                    dve.scalar_tensor_tensor(out=t.hidden[k % 2][:], in0=t.pairs[k % 3][1][:], scalar=t.b1[:, 0, k % 6:k % 6 + 1],
                                             in1=t.gelu[k % 2][:], op0=ALU.add, op1=ALU.mult).then_inc(s["gated"], 1)

                def hidden_lo(k):
                    dve.wait_ge(s["u_hi"], 12 * l + k + 1)
                    low_part(t.u[1][:, k % 6, :], t.hidden[k % 2][:], t.u[0][:, k % 6, :]).then_inc(s["u_ready"], 1)

                def add_down(half):
                    if half == 0:
                        dve.wait_ge(s["b2_added"], l + 1)
                    for k in range(4):
                        tile = 4 * half + k
                        dve.wait_ge(s["down_done"], 8 * l + tile + 1)
                        dve.tensor_tensor(t.y[:, tile, :], t.y[:, tile, :], t.bank[(4, 7)[tile % 2]][:, 0:D], ALU.add
                                          ).then_inc(s["y_ready"], 1)

                for k in range(12):
                    gate(k)
                    if k == 7:
                        add_down(0)
                    if k:
                        hidden_lo(k - 1)
                hidden_lo(11)
                add_down(1)
                assert step_count[0] == STEPS, step_count
            dve.wait_ge(s["y_ready"], 8 * DEPTH + 8)
            dve.tensor_tensor(t.x[:], t.x[:], t.y[:], ALU.add).then_inc(s["result"], 1)


def latent_stages(nc, t, sem_maker, args, out):
    with ExitStack() as ctx:
        def sb(name, shape, dt=F32):
            return ctx.enter_context(nc.sbuf_tensor(f"a_{name}", shape, dt))

        def parts(name, shape):
            return [sb(f"{name}_{part}", shape, F32R) for part in ("hi", "lo")]

        t.w_raw = [sb(f"w_raw{k}", [P, KC, D]) for k in range(3)]
        t.w = [parts(f"w{k}", [P, KC, D]) for k in range(3)]
        t.causal = sb("causal", [P, QT, L])
        t.z, t.v, t.s_sb, t.p = (sb(n, [P, TILES, D]) for n in ("z", "v", "s_sb", "p"))
        t.xt, t.qt, t.kt = (parts(n, [P, KC, B * L]) for n in ("xt", "qt", "kt"))
        t.pt = sb("pt", [P, B, 3, P])
        t.stats, t.mv = sb("stats", [P, TILES, 6]), sb("mv", [P, TILES, 2])
        t.std, t.rstd, t.mx, t.bias, t.rowsum, t.inv = (sb(n, [P, TILES]) for n in ("std", "rstd", "mx", "bias", "rowsum", "inv"))
        t.bank = [ctx.enter_context(nc.psum_tensor(f"a_bank{k}", [P, 512], F32)) for k in range(8)]
        attend_stage(nc, t, sem_maker(ctx, "att"), args)
    with ExitStack() as ctx:
        def sb(name, shape, dt=F32):
            return ctx.enter_context(nc.sbuf_tensor(f"f_{name}", shape, dt))

        def parts(name, shape):
            return [sb(f"{name}_{part}", shape, F32R) for part in ("hi", "lo")]

        t.y = sb("y", [P, TILES, D])
        t.wqkv, t.wo = parts("wqkv", [P, KC, 3 * LI]), parts("wo", [P, 4, D])
        t.w1, t.w2 = parts("w1", [P, KC, 2 * HB * P]), parts("w2", [P, HB, D])
        t.staging = sb("staging", [P, KC * 3 * LI])
        t.xt = parts("xt", [P, KC, B, L + 2])
        t.rot_cos, t.rot_sin, t.cos, t.sin = (sb(n, [P, QT, 2, LDH]) for n in ("rot_cos", "rot_sin", "cos", "sin"))
        t.window = sb("window", [P, 3 * P])
        t.scales, t.ln, t.b2, t.b1 = sb("scales", [P, 2, LDH]), sb("ln", [P, 2, KC]), sb("b2", [P, D]), sb("b1", [P, 2, HB])
        work = sb("work", [P, 5120])
        t.qk_sb = [work[:, k * 1024:(k + 1) * 1024].rearrange("p (w n) -> p w n", w=2) for k in range(2)]
        t.cos_part, t.sin_part = (work[:, k * 1024:(k + 1) * 1024].rearrange("p (w h d) -> p w h d", w=2, h=LH) for k in (2, 3))
        t.squares = work[:, 4096:5120].rearrange("p (w n) -> p w n", w=2)
        t.z = work[:, 0:2048].rearrange("p (k n) -> p k n", k=TILES)
        t.wide = work[:, 2048:2048 + 2 * B * (L + 2)].rearrange("p (k b n) -> p k b n", k=KC, b=B)
        heads = sb("heads", [P, 3 * LH * L], F32R)
        t.qh, t.ql, t.kp = (heads[:, k * LH * L:(k + 1) * LH * L].rearrange("p (h n) -> p h n", h=LH) for k in range(3))
        t.u = [heads[:, k * HB * 512:(k + 1) * HB * 512].rearrange("p (m n) -> p m n", m=HB) for k in range(2)]
        soft = sb("soft", [P, 6 * 3 * P])
        t.p = [soft[:, k * 384:(k + 1) * 384] for k in range(4)]
        t.pt = [soft[:, k * 384:(k + 1) * 384].rearrange("p (k q) -> p k q", k=3) for k in (4, 5)]
        t.gelu = [soft[:, k * 512:(k + 1) * 512] for k in range(2)]
        t.hidden = [soft[:, k * 512:(k + 1) * 512] for k in range(2, 4)]
        t.rot_q = [sb(f"rot_q{k}", [P, LH, 2, LDH]) for k in range(2)]
        t.rot_k = [sb(f"rot_k{k}", [P, LI]) for k in range(2)]
        t.v = sb("v", [P, 4, LI])
        t.o = sb("o", [P, QT, LI])
        t.ot = parts("ot", [P, QT, 4, P])
        t.stats, t.tail_stats, t.mv, t.mv_up = sb("stats", [P, TILES, 12]), sb("tail_stats", [P, TILES, 6]), sb("mv", [P, TILES, 2]), sb("mv_up", [P, TILES, 2])
        t.std, t.rstd = sb("std", [P, TILES]), sb("rstd", [P, TILES])
        t.sums, t.norms, t.norms_kept, t.inverses = (sb(n, [P, 2 * LH]) for n in ("sums", "norms", "norms_kept", "inverses"))
        t.q_norm = sb("q_norm", [P, TILES, LH])
        t.mx, t.bias, t.rowsum = (sb(n, [P, LH, QT]) for n in ("mx", "bias", "rowsum"))
        t.inv = sb("inv", [P, 4, QT])
        t.ones, t.edge = sb("ones", [1, P]), sb("edge", [1, B])
        t.tick, t.tick_dve = sb("tick", [P, 2]), sb("tick_dve", [P, 1])
        t.bank = [ctx.enter_context(nc.psum_tensor(f"f_bank{k}", [P, 512], F32)) for k in range(8)]
        t.pairs = [(t.bank[0], t.bank[1]), (t.bank[2], t.bank[3]), (t.bank[5], t.bank[6])]
        transformer_stage(nc, t, sem_maker(ctx, "ffn"), args, out)


def program(nc, args, out):
    with ExitStack() as whole:
        class Tensors:
            pass

        t = Tensors()

        def sem_maker(ctx, prefix):
            return lambda name: ctx.enter_context(nc.semaphore(f"{prefix}_{name}"))

        t.x = whole.enter_context(nc.sbuf_tensor("x", [P, TILES, D], F32))
        t.ident = whole.enter_context(nc.sbuf_tensor("ident", [P, P], F32))
        t.eps = whole.enter_context(nc.sbuf_tensor("eps", [P, 1], F32))
        with ExitStack() as ctx:
            def sb(name, shape, dt=F32):
                return ctx.enter_context(nc.sbuf_tensor(name, shape, dt))

            def parts(name, shape):
                return [sb(f"{name}_{part}", shape, F32R) for part in ("hi", "lo")]

            t.wkv, t.wq, t.wout = parts("wkv", [P, KC, 2 * H * DH]), parts("wq", [P, KC, H * DH]), parts("wout", [P, 8, D])
            t.norm = sb("norm", [P, 4, KC])
            t.plan = sb("plan", [1, B * PLAN], I32)
            with ExitStack() as inner:
                def raw(name, shape, dt=F32):
                    return inner.enter_context(nc.sbuf_tensor(name, shape, dt))

                t.wkv_raw, t.wq_raw, t.wout_raw = raw("wkv_raw", [P, KC, 2 * H * DH]), raw("wq_raw", [P, KC, H * DH]), raw("wout_raw", [P, 8, D])
                t.mask_rows = raw("mask_rows", [B, CTX], U8)
                t.iota = raw("iota", [B, NCH])
                t.first_key = raw("first_key", [B, NCH])
                t.ones = raw("ones", [B, NCH])
                t.scratch = raw("scratch", [B, 3 * NCH])
                t.hits = raw("hits", [B, NCH, NCH])
                t.plan_rows = raw("plan_rows", [B, PLAN])
                t.plan_flat = raw("plan_flat", [1, B * PLAN])
                prepare_stage(nc, t, sem_maker(inner, "prep"), args)
            t.xres, t.raw, t.z1, t.z = (sb(n, [P, 2, D]) for n in ("xres", "raw", "z1", "z"))
            t.wide = sb("wide", [P, KC, CH])
            t.xt = parts("xt", [P, KC, CH])
            t.mask8 = sb("mask8", [P, CH], U8)
            t.pen = sb("pen", [P, CH])
            t.tick = sb("tick", [P, 1])
            t.stats, t.mv, t.std, t.rstd = sb("stats", [P, 2, 6]), sb("mv", [P, 2, 2]), sb("std", [P, 2]), sb("rstd", [P, 2])
            t.qh, t.ql, t.kp = (sb(n, [P, H, L], F32R) for n in ("qh", "ql", "kp"))
            t.v = sb("v", [P, KT, H * DH])
            t.s_sb = [sb(f"s_sb{k}", [P, GU, CH]) for k in range(2)]
            t.probs = [sb(f"probs{k}", [P, GU, CH]) for k in range(3)]
            t.pt = [sb(f"pt{k}", [P, GU, KT, P]) for k in range(3)]
            t.mstate, t.mnew, t.mdiff, t.mbias, t.alpha, t.rowsum, t.den, t.inv = (
                sb(n, [P, H * QT]) for n in ("mstate", "mnew", "mdiff", "mbias", "alpha", "rowsum", "den", "inv"))
            t.o = sb("o", [P, H * QT, DH])
            t.onorm = sb("onorm", [P, QT, H * DH])
            t.ot = [q[:, 0:8, :] for q in (t.qh, t.ql)]
            t.s_ps = [ctx.enter_context(nc.psum_tensor(f"s_ps{k}", [P, GU, CH], F32)) for k in range(2)]
            t.turn = [ctx.enter_context(nc.psum_tensor(f"turn{k}", [P, 512], F32)) for k in range(2)]
            t.proj = ctx.enter_context(nc.psum_tensor("proj", [P, 512], F32))
            t.pv_ps = ctx.enter_context(nc.psum_tensor("pv_ps", [P, GU, DH], F32))
            cross_stage(nc, t, sem_maker(ctx, "cross"), args)
        latent_stages(nc, t, sem_maker, args, out)


def constants():
    c = {"ident": np.eye(P, dtype=np.float32), "iota": np.tile(np.arange(NCH, dtype=np.float32), (B, 1))}
    c["first_key"] = (np.arange(B)[:, None] * CTX + np.arange(NCH)[None] * CH).astype(np.float32)
    i, j = np.arange(L)[:, None], np.arange(L)[None]
    seen = np.where(j <= i, 0.0, -BIG).astype(np.float32)
    c["causal"] = np.ascontiguousarray(seen.reshape(QT, P, L).transpose(1, 0, 2))
    near = np.where((j <= i) & (i <= j + P), 0.0, -FAR).astype(np.float32)
    c["window"] = np.ascontiguousarray(np.concatenate([near[:P, :P], near[P:]], axis=1))
    half = np.arange(0, LDH, 2, dtype=np.float32)
    pos = np.arange(L, dtype=np.float32)
    freq = pos[:, None] * (np.float32(1.0) / np.float32(10000.0) ** (half / np.float32(LDH)))[None]
    base = (half + np.float32(0.4 * LDH)) / np.float32(1.4 * LDH)
    growth = base[None] ** ((pos - L // 2) / np.float32(P // 2))[:, None]
    growth = np.concatenate([growth, growth], axis=1)
    cos, sin = (np.tile(f(freq), (1, 2)) for f in (np.cos, np.sin))
    sign = np.where(np.arange(LDH) < LDH // 2, -1.0, 1.0).astype(np.float32)
    for name, table in (("rot_cos", cos), ("rot_sin", sin * sign)):
        both = np.stack([table * growth, table / growth], axis=1).astype(np.float32)
        c[name] = np.ascontiguousarray(both.reshape(QT, P, 2, LDH).transpose(1, 0, 2, 3))
    return c


_INS = ['x', 'ctx_1024', 'mask_BxS2_bk0', 'L0_xattn_g1', 'L0_xattn_b1', 'L0_xattn_g2', 'L0_xattn_b2', 'L0_xattn_Wq',
        'L0_xattn_Wkv', 'L0_xattn_Wout', 'L0_attn_Qw', 'L0_attn_Kw', 'L0_attn_Vw', 'L0_ffn_wqkv', 'L0_ffn_q_scale',
        'L0_ffn_k_scale', 'L0_ffn_wo', 'L0_ffn_ln_g', 'L0_ffn_ln_b', 'L0_ffn_w1', 'L0_ffn_b1', 'L0_ffn_w2', 'L0_ffn_b2']


def kernel(**inputs):
    import concourse.bacc as _bacc
    from concourse.bass_utils import run_bass_kernel_spmd as _run

    nc = _bacc.Bacc("TRN2", target_bir_lowering=False, num_devices=1)
    arrays, args = {}, {}
    for name, value in list(constants().items()) + [(n, inputs[n]) for n in _INS]:
        a = np.ascontiguousarray(value)
        arrays[f"in_{name}"] = a
        args[name] = nc.dram_tensor(f"in_{name}", a.shape, mybir.dt.from_np(a.dtype), kind="ExternalInput").ap()
    out = nc.dram_tensor("out", (B, L, D), F32, kind="ExternalOutput").ap()
    program(nc, args, out)
    result = _run(nc, [arrays], core_ids=[0])
    return result.results[0]["out"]
```

```python
from contextlib import ExitStack

import numpy as np

import concourse.bass as bass
from concourse import mybir

F32 = mybir.dt.float32
F32R = mybir.dt.float32r
I32 = mybir.dt.int32
U8 = mybir.dt.uint8
ALU = mybir.AluOpType
ACT = mybir.ActivationFunctionType
X_AXIS = mybir.AxisListType.X

P = 128
BIG = 3.0e38
FAR = 1.0e25
EPS = 1e-5

B, L, D = 4, 256, 256
CTX = 4096
H, DH = 16, 64
CH = 256
NCH = CTX // CH
KC = D // P
QT = L // P
KT = CH // P
NG = H // 2
GU = 2 * QT
TILES = B * QT
ITEMS = 1 + NCH
PLAN = 2 * ITEMS + 2

LH, LDH, LI = 8, 64, 512
HID = 682
HB = 6
DEPTH = 2


def split_product(pe, out, stationary, moving, first, last):
    (s_hi, s_lo), (m_hi, m_lo) = stationary, moving
    pe.matmul(out, s_hi, m_hi, start=first, stop=False)
    pe.matmul(out, s_hi, m_lo, start=False, stop=False)
    return pe.matmul(out, s_lo, m_hi, start=False, stop=last)


def prepare_stage(nc, t, sems, args):
    s = {n: sems(n) for n in (
        "ident_loaded", "wkv_loaded", "wq_loaded", "wout_loaded", "params_loaded", "mask_loaded", "iota_loaded",
        "hi_done", "lo_done", "any_done", "plan_rows", "plan_moved", "plan_done", "x_loaded", "x_var", "x_std")}
    weights = [("wkv_loaded", t.wkv_raw, t.wkv), ("wq_loaded", t.wq_raw, t.wq), ("wout_loaded", t.wout_raw, t.wout)]

    def low_parts(eng, n):
        _, raw, (hi, lo) = weights[n]
        eng.wait_ge(s["hi_done"], n + 1)
        eng.tensor_tensor(lo[:], raw[:], hi[:].bitcast(F32), ALU.subtract).then_inc(s["lo_done"], 1)

    with nc.Block() as block:
        @block.sync
        def _(sp):
            sp.dma_start(t.ident[:], args["ident"]).then_inc(s["ident_loaded"], 16)
            sp.dma_start(t.mask_rows[:], args["mask_BxS2_bk0"]).then_inc(s["mask_loaded"], 16)
            sp.dma_start(t.iota[:], args["iota"]).then_inc(s["iota_loaded"], 16)
            sp.dma_start(t.first_key[:], args["first_key"]).then_inc(s["iota_loaded"], 16)
            sp.dma_start(t.next_slot[:], args["next_slot"]).then_inc(s["iota_loaded"], 16)
            sp.dma_start(t.x[:], args["x"].rearrange("b (t p) d -> p (b t) d", p=P)).then_inc(s["x_loaded"], 16)
            sp.dma_start(t.wkv_raw[:], args["L0_xattn_Wkv"].rearrange("(k p) n -> p k n", p=P)).then_inc(s["wkv_loaded"], 16)
            sp.dma_start(t.wq_raw[:], args["L0_xattn_Wq"].rearrange("(k p) n -> p k n", p=P)).then_inc(s["wq_loaded"], 16)
            sp.dma_start(t.wout_raw[:], args["L0_xattn_Wout"].rearrange("(k p) n -> p k n", p=P)).then_inc(s["wout_loaded"], 16)
            for col, name in enumerate(("g1", "b1", "g2", "b2")):
                with nc.allow_non_contiguous_dma("a vector of the width onto the partitions"):
                    sp.dma_start(t.norm[:, col // 2, (col % 2) * KC:(col % 2 + 1) * KC], args[f"L0_xattn_{name}"].rearrange("(k p) -> p k", p=P)
                                 ).then_inc(s["params_loaded"], 16)
            sp.wait_ge(s["plan_rows"], 1)
            sp.dma_start(t.plan_flat[0:1, :].rearrange("p (b c) -> p b c", b=B), t.plan_rows[:]).then_inc(s["plan_moved"], 16)
            sp.wait_ge(s["params_loaded"], 64)
            sp.wait_ge(s["plan_moved"], 16)

        @block.scalar
        def _(act):
            act.wait_ge(s["x_var"], 1)
            act.activation(t.x_std[:], t.x_mv[:, :, 1], ACT.Sqrt, bias=t.eps[:]).then_inc(s["x_std"], 1)
            for loaded, raw, (hi, lo) in weights:
                act.wait_ge(s[loaded], 16)
                act.activation(hi[:], raw[:], ACT.Copy).then_inc(s["hi_done"], 1)

        @block.gpsimd
        def _(pool):
            low_parts(pool, 1)
            pool.wait_ge(s["lo_done"], 3)

        @block.vector
        def _(dve):
            dve.memset(t.mask8[:], 1)
            dve.memset(t.eps[:], EPS)
            dve.wait_ge(s["mask_loaded"], 16)
            dve.wait_ge(s["iota_loaded"], 48)
            step = [0]

            def then(ins):
                step[0] += 1
                ins.then_inc(s["any_done"], 1)
                dve.wait_ge(s["any_done"], step[0])

            flags, upto, place = t.scratch[0:B, 0:NCH], t.scratch[0:B, 16:32], t.scratch[0:B, 32:48]
            then(dve.tensor_reduce(flags, t.mask_rows[:].rearrange("b (c k) -> b c k", k=CH), X_AXIS, ALU.max))
            then(dve.memset(t.ones[:], 1.0))
            then(dve.tensor_tensor_scan(upto, t.ones[0:B, :], flags, 0.0, ALU.mult, ALU.add))
            then(dve.tensor_scalar(place, flags, -1001.0, 1000.0, ALU.mult, ALU.add))
            then(dve.tensor_tensor(place, place, upto, ALU.add))
            hits = t.hits[0:B]
            then(dve.tensor_tensor(hits, place.unsqueeze(1).broadcast_to([B, NCH, NCH]),
                                   t.iota[:, 0:NCH].unsqueeze(2).broadcast_to([B, NCH, NCH]), ALU.is_equal))
            then(dve.tensor_tensor(hits, hits, t.first_key[:].unsqueeze(1).broadcast_to([B, NCH, NCH]), ALU.mult))
            then(dve.tensor_reduce(t.plan_rows[:, 0:NCH], hits, X_AXIS, ALU.add))
            dve.memset(t.plan_rows[:, NCH:ITEMS], 0.0)
            slots = t.plan_rows[:, ITEMS:2 * ITEMS]
            then(dve.tensor_scalar(slots, t.iota[:], upto[:, NCH - 1:NCH], None, ALU.is_equal))
            then(dve.tensor_scalar(slots, slots, t.next_slot[:], None, ALU.mult))
            then(dve.tensor_scalar(t.plan_rows[:, 2 * ITEMS:PLAN - 1], upto[:, NCH - 1:NCH], 1.0, None, ALU.add))
            dve.memset(t.plan_rows[:, PLAN - 1:PLAN], 0.0).then_inc(s["plan_rows"], 1)
            dve.wait_ge(s["x_loaded"], 16)
            for k in range(TILES):
                last = dve.bn_stats(t.x_stats[:, k, :], t.x[:, k, :])
            then(last)
            for k in range(TILES):
                last = dve.bn_aggr(t.x_mv[:, k, :], t.x_stats[:, k, :])
            last.then_inc(s["x_var"], 1)
            dve.wait_ge(s["x_std"], 1)
            then(dve.reciprocal(t.x_rstd[:], t.x_std[:]))
            for k in range(TILES):
                dve.tensor_scalar(t.raw[:, 1 + k // QT, k % QT, :], t.x[:, k, :], t.x_mv[:, k, 0:1], t.x_rstd[:, k:k + 1],
                                  ALU.subtract, ALU.mult)
            dve.wait_ge(s["plan_moved"], 16)
            flat = t.plan_flat[:].rearrange("p (b c) -> p b c", b=B)
            for b in range(1, B):
                then(dve.tensor_tensor(flat[:, b, PLAN - 1:PLAN], flat[:, b - 1, PLAN - 1:PLAN],
                                       flat[:, b - 1, PLAN - 2:PLAN - 1], ALU.add))
            dve.tensor_copy(t.plan[:], t.plan_flat[:]).then_inc(s["plan_done"], 1)
            low_parts(dve, 0)
            low_parts(dve, 2)
            dve.wait_ge(s["params_loaded"], 64)
            for slot in range(1 + B):
                last = dve.tensor_copy(t.gains[:, slot, :], t.norm[:, 0 if slot == 0 else 1, :])
            then(last)


PE_BETWEEN = {(1, 1): ["K2", "K3"], (2, 1): ["V0", "V1", "V2"], (3, 1): ["V3"], (6, 0): ["turn"], (8, 0): ["K0"],
              (9, 2): ["K1"]}
ACT_BETWEEN = {(0, 1): ["K2", "K3"], (1, 1): ["V0"], (2, 0): ["V2"], (2, 1): ["std"], (6, 0): ["x"], (7, 2): ["K0"],
               (9, 2): ["K1"]}
DVE_BETWEEN = {(1, 0): ["stats"], (1, 1): ["var", "K2", "K3"], (2, 1): ["V1"], (3, 1): ["V3"], (4, 0): ["rstd", "z"],
               (6, 0): ["wide"], (7, 0): ["x"], (10, 0): ["K0"], (10, 2): ["pen"], (11, 2): ["K1"]}


def cross_stage(nc, t, sems, args):
    names = (
        "raw_loaded", "pen_loaded", "pen_used", "q_done", "q_hi", "q_ready", "state_zero",
        "stats_done", "var", "std", "rstd_done", "z_ready", "z_turned", "wide", "x_hi", "x_ready",
        "k_done", "k_hi", "k_ready", "v_done", "v_act", "v_dve",
        "s_done", "s_read", "bias_ready", "alpha_ready", "p_ready", "t_done", "pt_act", "pt_dve",
        "pv_done", "rescaled", "o_added", "dve_step", "pool_step",
        "o_norm", "o_turned", "ot_hi", "ot_lo", "out_done", "x_added")
    s = {n: sems(n) for n in names}
    tokens = args["ctx_1024"].rearrange("b n d -> (b n) d")
    mask_row = args["mask_BxS2_bk0"].rearrange("b (o n) -> o (b n)", o=1)
    wk = [w[:, :, 0:H * DH] for w in t.wkv]
    wv = [w[:, :, H * DH:2 * H * DH] for w in t.wkv]
    q_banks = [t.turn[0], t.turn[1], t.proj]
    k_banks = [t.proj[:], t.s_ps[0][:, 0:2, :].rearrange("p u n -> p (u n)"), t.turn[0][:], t.turn[1][:]]
    v_banks = [t.proj, t.turn[0], t.turn[1], t.proj]

    def counts(eng, b):
        n = eng.value_load(t.plan[0:1, bass.ds(b * PLAN + 2 * ITEMS, 1)], min_val=1, max_val=ITEMS)
        before = eng.value_load(t.plan[0:1, bass.ds(b * PLAN + 2 * ITEMS + 1, 1)], min_val=0, max_val=(B - 1) * ITEMS)
        return n, before

    def value_part(u):
        return t.v[:, u % 2, (u // 2) * 512:(u // 2 + 1) * 512]

    with nc.Block() as block:
        @block.sync
        def _(sp):
            with sp.Fori(0, B) as b:
                count, before = counts(sp, b)
                with sp.Fori(0, count) as i:
                    n = before + i
                    first_key = sp.value_load(t.plan[0:1, bass.ds(b * PLAN + i, 1)], min_val=0, max_val=B * CTX - CH)
                    sp.wait_ge(s["z_ready"], n + 1)
                    sp.dma_start(t.raw[:, 0, :, :], tokens[bass.ds(first_key, CH), :].rearrange("(t p) d -> p t d", p=P)).then_inc(s["raw_loaded"], 16)
                    sp.wait_ge(s["pen_used"], n + 1)
                    sp.dma_start(t.mask8[:, 0, :], mask_row[:, bass.ds(first_key, CH)].partition_broadcast(P)).then_inc(s["pen_loaded"], 16)

        @block.tensor
        def _(pe):
            def queries(b):
                pe.wait_ge(s["x_added"], 2 * b + 2)
                for u in range(4):
                    if u == 3:
                        pe.wait_ge(s["q_ready"], 4 * b + 1)
                    for m in range(2):
                        mt = 2 * u + m
                        for kc in range(KC):
                            last = split_product(pe, q_banks[u % 3][:, m * L:(m + 1) * L],
                                                 [w[:, kc, mt * P:(mt + 1) * P] for w in t.wq],
                                                 [x[:, kc, :] for x in t.xt], kc == 0, kc == KC - 1)
                    last.then_inc(s["q_done"], 1)

            def turn_tokens(m):
                pe.wait_ge(s["z_ready"], m + 1)
                for kc in range(KC):
                    for kt in range(KT):
                        last = pe.transpose(t.proj[:, (kc * KT + kt) * P:(kc * KT + kt + 1) * P],
                                            t.z[:, kt, kc * P:(kc + 1) * P], t.ident[:])
                last.then_inc(s["z_turned"], 1)

            def project_keys(m, u):
                if u == 0:
                    pe.wait_ge(s["x_ready"], m + 1)
                if u == 1:
                    pe.wait_ge(s["s_read"], 8 * m + 1)
                for half in range(2):
                    mt = 2 * u + half
                    for kc in range(KC):
                        last = split_product(pe, k_banks[u][:, half * CH:(half + 1) * CH],
                                             [w[:, kc, mt * P:(mt + 1) * P] for w in wk],
                                             [x[:, kc, :] for x in t.xt], kc == 0, kc == KC - 1)
                last.then_inc(s["k_done"], 1)

            def project_values(n, u):
                if u == 0:
                    pe.wait_ge(s["k_ready"], 4 * n + 1)
                if u == 1 or u == 2:
                    pe.wait_ge(s["k_ready"], 4 * n + u + 2)
                if u == 3:
                    pe.wait_ge(s["v_act"], 2 * n + 1)
                for kc in range(KC):
                    last = split_product(pe, v_banks[u][:], [x[:, kc, u % 2 * P:(u % 2 + 1) * P] for x in t.xt],
                                         [w[:, kc, (u // 2) * 512:(u // 2 + 1) * 512] for w in wv], kc == 0, kc == KC - 1)
                last.then_inc(s["v_done"], 1)

            def scores(b, n, g):
                if g == 0:
                    pe.wait_ge(s["k_ready"], 4 * n + 2)
                    pe.wait_ge(s["q_ready"], 4 * b + 1)
                if g == 4 or g == 6:
                    pe.wait_ge(s["k_ready"], 4 * n + g // 2 + 1)
                pe.wait_ge(s["s_read"], 8 * n + g + 1)
                for u in range(GU):
                    h, qt = 2 * g + u // QT, u % QT
                    pe.matmul(t.s_ps[g % 2][:, u, :], t.qh[:, h, qt * P:(qt + 1) * P], t.kp[:, h, :], start=True, stop=False)
                    last = pe.matmul(t.s_ps[g % 2][:, u, :], t.ql[:, h, qt * P:(qt + 1) * P], t.kp[:, h, :], start=False, stop=True)
                last.then_inc(s["s_done"], 1)

            def turn_probs(n, g):
                pe.wait_ge(s["p_ready"], 8 * n + g + 1)
                if g == 0:
                    pe.wait_ge(s["v_act"], 2 * n + 2)
                    pe.wait_ge(s["v_dve"], 2 * n + 1)
                else:
                    pe.wait_ge(s["pt_act"], 8 * n + g)
                    pe.wait_ge(s["pt_dve"], 8 * n + g)
                for u in range(GU):
                    for kt in range(KT):
                        last = pe.transpose(t.turn[u // 2][:, ((u % 2) * KT + kt) * P:((u % 2) * KT + kt + 1) * P],
                                            t.probs[g % 3][:, u, kt * P:(kt + 1) * P], t.ident[:])
                last.then_inc(s["t_done"], 1)

            def weighted_values(n, g):
                pe.wait_ge(s["pt_act"], 8 * n + g + 1)
                pe.wait_ge(s["pt_dve"], 8 * n + g + 1)
                pe.wait_ge(s["o_added"], 8 * n + g + NG)
                for u in range(GU):
                    h = 2 * g + u // QT
                    for kt in range(KT):
                        last = pe.matmul(t.pv_ps[:, u, :], t.pt[g % 3][:, u, kt, :], t.v[:, kt, h * DH:(h + 1) * DH],
                                         start=(kt == 0), stop=(kt == KT - 1))
                last.then_inc(s["pv_done"], 1)

            def output_projection(b):
                pe.wait_ge(s["o_norm"], b + 1)
                for u in range(4):
                    if u >= 2:
                        pe.wait_ge(s["ot_lo"], 4 * b + u - 1)
                    for k in range(2):
                        for qt in range(QT):
                            last = pe.transpose(t.turn[u % 2][:, k * L + qt * P:k * L + (qt + 1) * P],
                                                t.onorm[:, qt, (2 * u + k) * P:(2 * u + k + 1) * P], t.ident[:])
                    last.then_inc(s["o_turned"], 1)
                pe.wait_ge(s["ot_lo"], 4 * b + 4)
                for qt in range(QT):
                    for k in range(8):
                        last = split_product(pe, t.s_ps[qt][:, 0, :], [o[:, k, qt * P:(qt + 1) * P] for o in t.ot],
                                             [w[:, k, :] for w in t.wout], k == 0, k == 7)
                    last.then_inc(s["out_done"], 1)

            def prepare(b, n, what):
                if what == "turn":
                    pe.wait_ge(s["v_dve"], 2 * n + 2)
                    turn_tokens(n + 1)
                elif what[0] == "V":
                    project_values(n, int(what[1]))
                elif what in ("K0", "K1"):
                    project_keys(n + 1, int(what[1]))
                else:
                    pe.wait_ge(s["q_ready"], 4 * b + 4)
                    project_keys(n, int(what[1]))

            turn_tokens(0)
            for u in range(2):
                project_keys(0, u)
            with pe.Fori(0, B) as b:
                count, before = counts(pe, b)
                pe.wait_ge(s["k_ready"], 4 * before + 1)
                queries(b)
                with pe.Fori(0, count) as i:
                    n = pe.snap(before + i)
                    for j in range(NG + 4):
                        for what in PE_BETWEEN.get((j, 0), ()):
                            prepare(b, n, what)
                        if j < NG:
                            scores(b, n, j)
                        for what in PE_BETWEEN.get((j, 1), ()):
                            prepare(b, n, what)
                        if j >= 4:
                            weighted_values(n, j - 4)
                        if 2 <= j < NG + 2:
                            turn_probs(n, j - 2)
                        for what in PE_BETWEEN.get((j, 2), ()):
                            prepare(b, n, what)
                output_projection(b)

        @block.scalar
        def _(act):
            def deviations(m):
                act.wait_ge(s["var"], m + 1)
                act.activation(t.std[:], t.mv[:, :, 1], ACT.Sqrt, bias=t.eps[:]).then_inc(s["std"], 1)

            def tokens_hi(m):
                act.wait_ge(s["wide"], m + 1)
                act.activation(t.xt[0][:].rearrange("p k n -> p (k n)"), t.wide[:].rearrange("p k n -> p (k n)"), ACT.Copy
                               ).then_inc(s["x_hi"], 1)

            def keys_hi(m, u):
                act.wait_ge(s["k_done"], 4 * m + u + 1)
                pair = k_banks[u].rearrange("p (m n) -> p m n", m=2)
                heads = t.kp[0:DH, 4 * u:4 * u + 4, :].rearrange("p (m o) n -> p m o n", o=2)
                act.activation(heads[:, :, 0, :], pair[0:DH], ACT.Copy)
                act.activation(heads[:, :, 1, :], pair[DH:P], ACT.Copy).then_inc(s["k_hi"], 1)

            def softmax_part(n, g):
                act.wait_ge(s["bias_ready"], 8 * n + g + 1)
                act.wait_ge(s["rescaled"], 8 * n + g + 1)
                act.activation(t.alpha[:, GU * g:GU * (g + 1)], t.mdiff[:, GU * g:GU * (g + 1)], ACT.Exp,
                               scale=0.125).then_inc(s["alpha_ready"], 1)
                for u in range(GU):
                    at = GU * g + u
                    last = act.activation(t.probs[g % 3][:, u, :], t.s_sb[g % 2][:, u, :], ACT.Exp,
                                          bias=t.mbias[:, at:at + 1], scale=0.125, accum_out=t.rowsum[:, at:at + 1])
                last.then_inc(s["p_ready"], 1)

            def store_turned(n, g):
                act.wait_ge(s["t_done"], 8 * n + g + 1)
                if g >= 3:
                    act.wait_ge(s["pv_done"], 8 * n + g - 2)
                act.activation(t.pt[g % 3][:, 0:2, :, :].rearrange("p u k q -> p (u k q)"), t.turn[0][:], ACT.Copy
                               ).then_inc(s["pt_act"], 1)

            def prepare(n, what):
                if what == "std":
                    deviations(n + 1)
                elif what == "x":
                    tokens_hi(n + 1)
                elif what[0] == "V":
                    u = int(what[1])
                    act.wait_ge(s["v_done"], 4 * n + u + 1)
                    act.activation(value_part(u), v_banks[u][:], ACT.Copy).then_inc(s["v_act"], 1)
                else:
                    u = int(what[1])
                    keys_hi(n + 1 if u < 2 else n, u)

            deviations(0)
            tokens_hi(0)
            for u in range(2):
                keys_hi(0, u)
            with act.Fori(0, B) as b:
                count, before = counts(act, b)
                for u in range(4):
                    act.wait_ge(s["q_done"], 4 * b + u + 1)
                    pair = q_banks[u % 3][:].rearrange("p (m n) -> p m n", m=2)
                    for o in range(2):
                        for half in (slice(0, DH), slice(DH, P)):
                            last = act.activation(t.qh[half, 4 * u + o:4 * u + 4:2, :], pair[o * DH:(o + 1) * DH], ACT.Copy)
                    last.then_inc(s["q_hi"], 1)
                with act.Fori(0, count) as i:
                    n = act.snap(before + i)
                    for g in range(NG + 3):
                        for what in ACT_BETWEEN.get((g, 0), ()):
                            prepare(n, what)
                        if g < NG:
                            softmax_part(n, g)
                        for what in ACT_BETWEEN.get((g, 1), ()):
                            prepare(n, what)
                        if 2 <= g < NG + 2:
                            store_turned(n, g - 2)
                        for what in ACT_BETWEEN.get((g, 2), ()):
                            prepare(n, what)
                for u in range(4):
                    act.wait_ge(s["o_turned"], 4 * b + u + 1)
                    act.activation(t.ot[0][:, 2 * u:2 * u + 2, :].rearrange("p k n -> p (k n)"), t.turn[u % 2][:], ACT.Copy
                                   ).then_inc(s["ot_hi"], 1)

        @block.gpsimd
        def _(pool):
            with pool.Fori(0, B) as b:
                count, before = counts(pool, b)
                with pool.Fori(0, count) as i:
                    n = pool.snap(before + i)
                    for g in range(NG):
                        cols = slice(GU * g, GU * (g + 1))
                        if g == 0:
                            pool.wait_ge(s["state_zero"], b + 1)
                        pool.wait_ge(s["alpha_ready"], 8 * n + g + 1)
                        pool.wait_ge(s["o_added"], 8 * n + g + 1)
                        pool.tensor_tensor(t.o[:, cols, :], t.o[:, cols, :],
                                           t.alpha[:, cols].unsqueeze(2).broadcast_to([P, GU, DH]), ALU.mult)
                        pool.tensor_tensor(t.den[:, cols], t.den[:, cols], t.alpha[:, cols], ALU.mult).then_inc(s["pool_step"], 1)
                        pool.wait_ge(s["pool_step"], 8 * n + g + 1)
                        pool.wait_ge(s["p_ready"], 8 * n + g + 1)
                        pool.tensor_tensor(t.den[:, cols], t.den[:, cols], t.rowsum[:, cols], ALU.add).then_inc(s["rescaled"], 1)

        @block.vector
        def _(dve):
            dve.memset(t.tick[:], 0.0).then_inc(s["s_read"], 2)
            dve.memset(t.pen[:], 0.0).then_inc(s["o_added"], NG)
            dve.memset(t.mbias[:], 0.0).then_inc(s["rescaled"], NG)
            dve.memset(t.mdiff[:], 0.0).then_inc(s["pen_used"], 1)
            dve.memset(t.mnew[:], 0.0).then_inc(s["x_added"], 2)

            def slot_of(buffer, slot):
                return buffer[:, bass.ds(slot, 1)].rearrange("p o k n -> p (o k) n")

            def statistics(m, slot):
                for k in range(KT):
                    last = dve.bn_stats(t.stats[:, k, :], slot_of(t.raw, slot)[:, k, :])
                last.then_inc(s["stats_done"], 1)

            def variances(m):
                dve.wait_ge(s["stats_done"], m + 1)
                dve.memset(t.tick[:, 1:2], 0.0)
                for k in range(KT):
                    last = dve.bn_aggr(t.mv[:, k, :], t.stats[:, k, :])
                last.then_inc(s["var"], 1)

            def inverse_deviations(m):
                dve.wait_ge(s["std"], m + 1)
                dve.reciprocal(t.rstd[:], t.std[:]).then_inc(s["rstd_done"], 1)

            def normalised(m, slot):
                dve.wait_ge(s["rstd_done"], m + 1)
                for k in range(KT):
                    last = dve.tensor_scalar(t.z[:, k, :], slot_of(t.raw, slot)[:, k, :], t.mv[:, k, 0:1], t.rstd[:, k:k + 1],
                                             ALU.subtract, ALU.mult)
                last.then_inc(s["z_ready"], 1)

            def gained(m, slot):
                dve.wait_ge(s["z_turned"], m + 1)
                gain = t.gains[:, bass.ds(slot, 1), :].rearrange("p o n -> p (o n)")
                for kc in range(KC):
                    last = dve.tensor_scalar(t.wide[:, kc, :], t.proj[:, kc * CH:(kc + 1) * CH], gain[:, kc:kc + 1],
                                             gain[:, KC + kc:KC + kc + 1], ALU.mult, ALU.add)
                last.then_inc(s["wide"], 1)

            def tokens_lo(m):
                dve.wait_ge(s["x_hi"], m + 1)
                dve.tensor_tensor(t.xt[1][:], t.wide[:], t.xt[0][:].bitcast(F32), ALU.subtract).then_inc(s["x_ready"], 1)

            def keys_lo(m, u):
                dve.wait_ge(s["k_hi"], 4 * m + u + 1)
                pair = k_banks[u].rearrange("p (m n) -> p m n", m=2)
                hi = t.kp[0:DH, 4 * u:4 * u + 4, :].rearrange("p (m o) n -> p m o n", o=2).bitcast(F32)
                lo = t.kp[DH:P, 4 * u:4 * u + 4, :].rearrange("p (m o) n -> p m o n", o=2)
                dve.tensor_tensor(lo[:, :, 0, :], pair[0:DH], hi[:, :, 0, :], ALU.subtract)
                dve.tensor_tensor(lo[:, :, 1, :], pair[DH:P], hi[:, :, 1, :], ALU.subtract).then_inc(s["k_ready"], 1)

            def prepare(n, slot, what):
                if what == "stats":
                    dve.wait_ge(s["raw_loaded"], 16 * n + 16)
                    dve.memset(t.tick[:, 2:3], 0.0)
                    statistics(n + 1, slot)
                elif what == "var":
                    variances(n + 1)
                elif what == "rstd":
                    inverse_deviations(n + 1)
                elif what == "z":
                    normalised(n + 1, slot)
                elif what == "wide":
                    gained(n + 1, slot)
                elif what == "x":
                    tokens_lo(n + 1)
                elif what == "pen":
                    dve.wait_ge(s["pen_loaded"], 16 * n + 16)
                    dve.tensor_scalar(t.pen[:], t.mask8[:, bass.ds(slot, 1), :].rearrange("p o n -> p (o n)"), -1.0, BIG,
                                      ALU.add, ALU.mult).then_inc(s["pen_used"], 1)
                elif what[0] == "V":
                    u = int(what[1])
                    dve.wait_ge(s["v_done"], 4 * n + u + 1)
                    dve.tensor_copy(value_part(u), v_banks[u][:]).then_inc(s["v_dve"], 1)
                else:
                    u = int(what[1])
                    keys_lo(n + 1 if u < 2 else n, u)

            statistics(0, 1)
            variances(0)
            inverse_deviations(0)
            normalised(0, 1)
            gained(0, 1)
            tokens_lo(0)
            for u in range(2):
                keys_lo(0, u)
            with dve.Fori(0, B) as b:
                count, before = counts(dve, b)
                dve.memset(t.mstate[:], -BIG)
                dve.memset(t.den[:], 0.0)
                dve.memset(t.o[:], 0.0).then_inc(s["state_zero"], 1)
                for u in range(4):
                    dve.wait_ge(s["q_hi"], 4 * b + u + 1)
                    pair = q_banks[u % 3][:].rearrange("p (m n) -> p m n", m=2)
                    for o in range(2):
                        for half in (slice(0, DH), slice(DH, P)):
                            last = dve.tensor_tensor(t.ql[half, 4 * u + o:4 * u + 4:2, :], pair[o * DH:(o + 1) * DH],
                                                     t.qh[half, 4 * u + o:4 * u + 4:2, :].bitcast(F32), ALU.subtract)
                    last.then_inc(s["q_ready"], 1)

                with dve.Fori(0, count) as i:
                    n = dve.snap(before + i)
                    slot = dve.value_load(t.plan[0:1, bass.ds(b * PLAN + ITEMS + i, 1)], min_val=0, max_val=B)
                    for g in range(NG + 5):
                        if g >= 5:
                            cols = slice(GU * (g - 5), GU * (g - 4))
                            dve.wait_ge(s["pv_done"], 8 * n + g - 4)
                            dve.wait_ge(s["rescaled"], 8 * n + g - 4 + NG)
                            dve.tensor_tensor(t.o[:, cols, :], t.o[:, cols, :], t.pv_ps[:], ALU.add).then_inc(s["o_added"], 1)
                        for what in DVE_BETWEEN.get((g, 0), ()):
                            prepare(n, slot, what)
                        if g < NG:
                            cols = slice(GU * g, GU * (g + 1))
                            dve.wait_ge(s["s_done"], 8 * n + g + 1)
                            if g >= 2:
                                dve.wait_ge(s["p_ready"], 8 * n + g - 1)
                            dve.memset(t.tick[:, 0:1], 0.0)
                            for u in range(GU):
                                at = GU * g + u
                                last = dve.tensor_tensor_reduce(
                                    out=t.s_sb[g % 2][:, u, :], in0=t.s_ps[g % 2][:, u, :], in1=t.pen[:], scale=1.0,
                                    scalar=t.mstate[:, at:at + 1], op0=ALU.add, op1=ALU.max, accum_out=t.mnew[:, at:at + 1])
                            last.then_inc(s["s_read"], 1)
                            dve.wait_ge(s["s_read"], 8 * n + g + 3)
                            dve.tensor_tensor(t.mdiff[:, cols], t.mstate[:, cols], t.mnew[:, cols], ALU.subtract)
                            dve.tensor_scalar(t.mbias[:, cols], t.mnew[:, cols], -0.125, None, ALU.mult).then_inc(s["bias_ready"], 1)
                            dve.wait_ge(s["bias_ready"], 8 * n + g + 1)
                            dve.tensor_copy(t.mstate[:, cols], t.mnew[:, cols])
                        for what in DVE_BETWEEN.get((g, 1), ()):
                            prepare(n, slot, what)
                        if 2 <= g < NG + 2:
                            dve.wait_ge(s["t_done"], 8 * n + g - 1)
                            if g - 2 >= 3:
                                dve.wait_ge(s["pv_done"], 8 * n + g - 4)
                            dve.tensor_copy(t.pt[(g - 2) % 3][:, 2:4, :, :].rearrange("p u k q -> p (u k q)"), t.turn[1][:]
                                            ).then_inc(s["pt_dve"], 1)
                        for what in DVE_BETWEEN.get((g, 2), ()):
                            prepare(n, slot, what)
                dve.wait_ge(s["o_added"], 8 * (before + count) + NG)
                dve.wait_ge(s["rescaled"], 8 * (before + count) + NG)
                dve.reciprocal(t.inv[:], t.den[:]).then_inc(s["dve_step"], 1)
                dve.wait_ge(s["dve_step"], b + 1)
                dve.tensor_tensor(t.onorm[:].rearrange("p q (h d) -> p h q d", h=H),
                                  t.o[:].rearrange("p (h q) d -> p h q d", q=QT),
                                  t.inv[:].rearrange("p (h q) -> p h q", q=QT).unsqueeze(3).broadcast_to([P, H, QT, DH]),
                                  ALU.mult).then_inc(s["o_norm"], 1)
                for u in range(4):
                    dve.wait_ge(s["ot_hi"], 4 * b + u + 1)
                    out, hi = (o[:, 2 * u:2 * u + 2, :].rearrange("p k n -> p (k n)") for o in (t.ot[1], t.ot[0]))
                    dve.tensor_tensor(out, t.turn[u % 2][:], hi.bitcast(F32), ALU.subtract).then_inc(s["ot_lo"], 1)
                for qt in range(QT):
                    dve.wait_ge(s["out_done"], 2 * b + qt + 1)
                    x = t.x[:, bass.ds(b * QT + qt, 1), :].rearrange("p o n -> p (o n)")
                    dve.tensor_tensor(x, x, t.s_ps[qt][:, 0, :], ALU.add).then_inc(s["x_added"], 1)


def split_blocks(w, k, cols):
    return [part[:, k, cols] for part in w]


def attend_stage(nc, t, sems, args):
    s = {n: sems(n) for n in (
        "w_loaded", "w_hi", "w_ready", "mask_loaded", "step", "var", "std", "z_ready", "turned", "xt_hi", "xt_ready",
        "qk_done", "qk_hi", "qk_ready", "v_done", "v_act", "v_dve", "s_done", "s_read", "bias_ready", "p_ready",
        "t_done", "pt_ready", "pv_done", "x_done")}
    with nc.Block() as block:
        @block.sync
        def _(sp):
            for k, name in enumerate("QKV"):
                sp.dma_start(t.w_raw[k][:], args[f"L0_attn_{name}w"].rearrange("(k p) n -> p k n", p=P)).then_inc(s["w_loaded"], 16)
            sp.dma_start(t.causal[:], args["causal"]).then_inc(s["mask_loaded"], 16)

        @block.tensor
        def _(pe):
            for half in range(2):
                pe.wait_ge(s["z_ready"], 4 * half + 4)
                for kc in range(KC):
                    for k in range(4):
                        last = pe.transpose(t.bank[2 * half + kc][:, k * P:(k + 1) * P],
                                            t.z[:, 4 * half + k, kc * P:(kc + 1) * P], t.ident[:])
                    last.then_inc(s["turned"], 1)
            pe.wait_ge(s["w_ready"], 3)
            for half in range(2):
                pe.wait_ge(s["xt_ready"], 2 * half + 2)
                for m in range(4):
                    which, mt = m // 2, m % 2
                    for kc in range(KC):
                        last = split_product(pe, t.bank[(4 + 4 * half + m) % 8][:],
                                             split_blocks(t.w[which], kc, slice(mt * P, (mt + 1) * P)),
                                             split_blocks(t.xt, kc, slice(half * 512, half * 512 + 512)), kc == 0, kc == KC - 1)
                    last.then_inc(s["qk_done"], 1)
            for pair in range(4):
                pe.wait_ge(s["qk_ready"], pair + 1)
                for k in range(2):
                    for kc in range(KC):
                        last = split_product(pe, t.bank[4 + pair][:, k * D:(k + 1) * D],
                                             split_blocks(t.xt, kc, slice((2 * pair + k) * P, (2 * pair + k + 1) * P)),
                                             split_blocks(t.w[2], kc, slice(0, D)), kc == 0, kc == KC - 1)
                last.then_inc(s["v_done"], 1)
            for b in range(B):
                pe.wait_ge(s["qk_ready"], 8)
                for qt in range(QT):
                    for kc in range(KC):
                        last = split_product(pe, t.bank[b][:, qt * L:(qt + 1) * L],
                                             split_blocks(t.qt, kc, slice(b * L + qt * P, b * L + (qt + 1) * P)),
                                             split_blocks(t.kt, kc, slice(b * L, (b + 1) * L)), kc == 0, kc == KC - 1)
                last.then_inc(s["s_done"], 1)
            for b in range(B):
                pe.wait_ge(s["p_ready"], b + 1)
                pe.wait_ge(s["v_act"], 2)
                pe.wait_ge(s["v_dve"], 2)
                for k, (qt, kt) in enumerate(((0, 0), (1, 0), (1, 1))):
                    last = pe.transpose(t.bank[4 + b][:, k * P:(k + 1) * P], t.p[:, 2 * b + qt, kt * P:(kt + 1) * P], t.ident[:])
                last.then_inc(s["t_done"], 1)
            for b in range(B):
                pe.wait_ge(s["pt_ready"], b + 1)
                pe.matmul(t.bank[b][:, 0:D], t.pt[:, b, 0, :], t.v[:, 2 * b, :], start=True, stop=True)
                pe.matmul(t.bank[b][:, D:2 * D], t.pt[:, b, 1, :], t.v[:, 2 * b, :], start=True, stop=False)
                pe.matmul(t.bank[b][:, D:2 * D], t.pt[:, b, 2, :], t.v[:, 2 * b + 1, :], start=False, stop=True
                          ).then_inc(s["pv_done"], 1)

        @block.scalar
        def _(act):
            act.wait_ge(s["var"], 1)
            act.activation(t.std[:], t.mv[:, :, 1], ACT.Sqrt, bias=t.eps[:]).then_inc(s["std"], 1)
            for k in range(3):
                act.wait_ge(s["w_loaded"], 48)
                act.activation(t.w[k][0][:], t.w_raw[k][:], ACT.Copy).then_inc(s["w_hi"], 1)
            for a in range(4):
                half, kc = a // 2, a % 2
                act.wait_ge(s["turned"], a + 1)
                act.activation(t.xt[0][:, kc, half * 512:half * 512 + 512], t.bank[a][:], ACT.Copy).then_inc(s["xt_hi"], 1)
            for c in range(8):
                half, which, mt = c // 4, c % 4 // 2, c % 2
                act.wait_ge(s["qk_done"], c + 1)
                act.activation((t.qt, t.kt)[which][0][:, mt, half * 512:half * 512 + 512], t.bank[(4 + c) % 8][:], ACT.Copy
                               ).then_inc(s["qk_hi"], 1)
            for pair in (0, 2):
                act.wait_ge(s["v_done"], pair + 1)
                act.activation(t.v[:, 2 * pair:2 * pair + 2, :].rearrange("p k n -> p (k n)"), t.bank[4 + pair][:], ACT.Copy
                               ).then_inc(s["v_act"], 1)
            for b in range(B):
                act.wait_ge(s["bias_ready"], b + 1)
                for qt in range(QT):
                    at = 2 * b + qt
                    last = act.activation(t.p[:, at, :], t.s_sb[:, at, :], ACT.Exp, bias=t.bias[:, at:at + 1],
                                          scale=1.0 / 16.0, accum_out=t.rowsum[:, at:at + 1])
                last.then_inc(s["p_ready"], 1)

        @block.vector
        def _(dve):
            step = [0]

            def then(ins):
                step[0] += 1
                ins.then_inc(s["step"], 1)
                dve.wait_ge(s["step"], step[0])

            for k in range(TILES):
                last = dve.bn_stats(t.stats[:, k, :], t.x[:, k, :])
            then(last)
            for k in range(TILES):
                last = dve.bn_aggr(t.mv[:, k, :], t.stats[:, k, :])
            last.then_inc(s["var"], 1)
            dve.wait_ge(s["std"], 1)
            then(dve.reciprocal(t.rstd[:], t.std[:]))
            for k in range(TILES):
                dve.tensor_scalar(t.z[:, k, :], t.x[:, k, :], t.mv[:, k, 0:1], t.rstd[:, k:k + 1], ALU.subtract, ALU.mult
                                  ).then_inc(s["z_ready"], 1)
            for k in range(3):
                dve.wait_ge(s["w_hi"], k + 1)
                dve.tensor_tensor(t.w[k][1][:], t.w_raw[k][:], t.w[k][0][:].bitcast(F32), ALU.subtract).then_inc(s["w_ready"], 1)
            for a in range(4):
                half, kc = a // 2, a % 2
                dve.wait_ge(s["xt_hi"], a + 1)
                hi, lo = (x[:, kc, half * 512:half * 512 + 512] for x in t.xt)
                dve.tensor_tensor(lo, t.bank[a][:], hi.bitcast(F32), ALU.subtract).then_inc(s["xt_ready"], 1)
            for c in range(8):
                half, which, mt = c // 4, c % 4 // 2, c % 2
                dve.wait_ge(s["qk_hi"], c + 1)
                hi, lo = (x[:, mt, half * 512:half * 512 + 512] for x in (t.qt, t.kt)[which])
                dve.tensor_tensor(lo, t.bank[(4 + c) % 8][:], hi.bitcast(F32), ALU.subtract).then_inc(s["qk_ready"], 1)
            for pair in (1, 3):
                dve.wait_ge(s["v_done"], pair + 1)
                dve.tensor_copy(t.v[:, 2 * pair:2 * pair + 2, :].rearrange("p k n -> p (k n)"), t.bank[4 + pair][:]
                                ).then_inc(s["v_dve"], 1)
            dve.wait_ge(s["mask_loaded"], 16)
            for b in range(B):
                dve.wait_ge(s["s_done"], b + 1)
                for qt in range(QT):
                    at = 2 * b + qt
                    last = dve.tensor_tensor_reduce(
                        out=t.s_sb[:, at, :], in0=t.bank[b][:, qt * L:(qt + 1) * L], in1=t.causal[:, qt, :], scale=1.0,
                        scalar=-BIG, op0=ALU.add, op1=ALU.max, accum_out=t.mx[:, at:at + 1])
                then(last)
                dve.tensor_scalar(t.bias[:, 2 * b:2 * b + 2], t.mx[:, 2 * b:2 * b + 2], -1.0 / 16.0, None, ALU.mult
                                  ).then_inc(s["bias_ready"], 1)
            for b in range(B):
                dve.wait_ge(s["t_done"], b + 1)
                dve.tensor_copy(t.pt[:, b, :, :].rearrange("p k q -> p (k q)"), t.bank[4 + b][:, 0:3 * P]).then_inc(s["pt_ready"], 1)
            then(dve.reciprocal(t.inv[:], t.rowsum[:]))
            for b in range(B):
                dve.wait_ge(s["pv_done"], b + 1)
                for qt in range(QT):
                    at = 2 * b + qt
                    last = dve.scalar_tensor_tensor(out=t.x[:, at, :], in0=t.bank[b][:, qt * D:(qt + 1) * D],
                                                    scalar=t.inv[:, at:at + 1], in1=t.x[:, at, :], op0=ALU.mult, op1=ALU.add)
            last.then_inc(s["x_done"], 1)
            dve.wait_ge(s["x_done"], 1)


def attention_order(between):
    order = [("B", i, k) for i in range(2) for k in range(5)]
    order += [("N", 0), ("N", 1), ("C", 0), ("C", 1)]
    for b in range(B):
        for j in range(LH + 3):
            order.append(("D", b, j))
            if j in between and b + 1 < B:
                tile, steps = between[j]
                order += [("B", 2 * b + 2 + tile, k) for k in steps]
        following = (2 * b + 2, 2 * b + 3) if b + 1 < B else ()
        order += [("N", i) for i in following] + [("E", b)] + [("C", i) for i in following]
    return order


PE_ORDER = attention_order({0: (0, [0]), 2: (0, [1]), 3: (0, [2]), 4: (1, [0]), 5: (1, [1]), 6: (1, [2])})
ACT_ORDER = attention_order({1: (0, [0]), 2: (0, [1]), 3: (0, [2]), 5: (1, [0]), 6: (1, [1]), 7: (1, [2])})
DVE_ORDER = attention_order({3: (0, [3]), 5: (0, [4]), 7: (1, [3]), 8: (1, [4])})


def transformer_stage(nc, t, sems, args, out):
    names = (
        "const_loaded", "vec_loaded", "stage_loaded", "split_done",
        "ends_zero", "first_hi", "tables_ready", "first_var", "first_std", "y_ready", "turned", "xt_hi", "xt_ready", "edge_ready",
        "qkv_done", "qkv_copied", "squared", "reduced", "rooted", "cos_part", "sin_part", "summed", "rotated", "c_done", "c_hi", "c_ready",
        "s_done", "s_read", "bias_ready", "p_ready", "t_done", "pt_act", "pt_dve", "pv_done", "o_half",
        "o_turned", "o_hi", "o_ready", "e_done", "e_added", "half_stats", "stats_shifted", "var", "std", "mv_ready",
        "mv_shifted", "edge_row", "edge_done", "z_ready", "wide_ready", "up_done", "gelu_done", "gated", "u_hi", "u_ready",
        "down_done", "b2_added", "step", "first_step", "split_step", "result", "stored")
    s = {n: sems(n) for n in names}
    HEADS = LH * B
    STEPS = 3 * TILES + HEADS + 2 * B

    def halves(bank):
        return bank[:].rearrange("p (b n) -> p b n", b=2)

    def keys_of(h):
        return ((0, slice(0, P), slice(0, P)), (1, slice(P, 3 * P), slice(0, L)))

    with nc.Block() as block:
        @block.sync
        def _(sp):
            sp.dma_start(t.rot_cos[:], args["rot_cos"]).then_inc(s["const_loaded"], 16)
            sp.dma_start(t.rot_sin[:], args["rot_sin"]).then_inc(s["const_loaded"], 16)
            sp.dma_start(t.window[:], args["window"]).then_inc(s["const_loaded"], 16)
            sp.dma_start(t.staging[:].rearrange("p (k n) -> p k n", k=KC),
                         args["L0_ffn_wqkv"][0].rearrange("(k p) n -> p k n", p=P)).then_inc(s["stage_loaded"], 16)
            sp.wait_ge(s["ends_zero"], 1)
            with sp.Fori(0, DEPTH) as l:
                def layer(name):
                    return args[f"L0_ffn_{name}"][bass.ds(l, 1)]

                def load(dst, src, sem):
                    sp.dma_start(dst, src).then_inc(s[sem], 16)

                sp.wait_ge(s["y_ready"], 8 * l + 8)
                with nc.allow_non_contiguous_dma("vectors onto the partitions"):
                    load(t.scales[:, 0, :], layer("q_scale").partition_broadcast(P).rearrange("p o n -> p (o n)"), "vec_loaded")
                    load(t.scales[:, 1, :], layer("k_scale").partition_broadcast(P).rearrange("p o n -> p (o n)"), "vec_loaded")
                    load(t.ln[:, 0, :], layer("ln_g").rearrange("o (k p) -> p (o k)", p=P), "vec_loaded")
                    load(t.ln[:, 1, :], layer("ln_b").rearrange("o (k p) -> p (o k)", p=P), "vec_loaded")
                    load(t.b2[:], layer("b2").partition_broadcast(P).rearrange("p o n -> p (o n)"), "vec_loaded")
                    for side in range(2):
                        b1 = layer("b1")[:, side * HID:(side + 1) * HID]
                        load(t.b1[:, side, 0:5], b1[:, 0:5 * P].rearrange("o (m p) -> p (o m)", p=P), "vec_loaded")
                        load(t.b1[0:HID - 5 * P, side, 5:6], b1[:, 5 * P:HID].rearrange("o (m p) -> p (o m)", m=1), "vec_loaded")
                sp.wait_ge(s["split_done"], 4 * l + 1)
                load(t.staging[:, 0:4 * D].rearrange("p (k n) -> p k n", k=4),
                     layer("wo").rearrange("o (k p) n -> p (o k) n", p=P), "stage_loaded")
                sp.wait_ge(s["split_done"], 4 * l + 2)
                load(t.staging[:, 0:4 * HID].rearrange("p (k n) -> p k n", k=KC),
                     layer("w1").rearrange("o (k p) n -> p (o k) n", p=P), "stage_loaded")
                sp.wait_ge(s["half_stats"], l + 1)
                tails = t.tail_stats[:].rearrange("p (b q) n -> p b q n", q=2)
                stats = t.stats[:].rearrange("p (b q) n -> p b q n", q=2)
                load(t.stats[1:P, :, 6:12], t.tail_stats[0:P - 1, :, :], "stats_shifted")
                load(stats[0:1, :, 1, 6:12], tails[P - 1:P, :, 0, :], "stats_shifted")
                sp.wait_ge(s["mv_ready"], l + 1)
                up = t.mv_up[:].rearrange("p (b q) n -> p b q n", q=2)
                mv = t.mv[:].rearrange("p (b q) n -> p b q n", q=2)
                load(t.mv_up[0:P - 1, :, :], t.mv[1:P, :, :], "mv_shifted")
                load(up[P - 1:P, :, 0, :], mv[0:1, :, 1, :], "mv_shifted")
                sp.wait_ge(s["split_done"], 4 * l + 3)
                load(t.staging[:, 0:5 * D].rearrange("p (k n) -> p k n", k=5),
                     layer("w2")[:, 0:5 * P, :].rearrange("o (k p) n -> p (o k) n", p=P), "stage_loaded")
                load(t.staging[0:HID - 5 * P, 5 * D:6 * D], layer("w2")[:, 5 * P:HID, :].rearrange("o k n -> (o k) n"),
                     "stage_loaded")
                sp.wait_ge(s["split_done"], 4 * l + 4)
                load(t.staging[:].rearrange("p (k n) -> p k n", k=KC),
                     args["L0_ffn_wqkv"][DEPTH - 1].rearrange("(k p) n -> p k n", p=P), "stage_loaded")
            sp.wait_ge(s["result"], 1)
            sp.dma_start(out.rearrange("b (t p) d -> p (b t) d", p=P), t.x[:]).then_inc(s["stored"], 16)
            sp.wait_ge(s["stored"], 16)
            sp.wait_ge(s["split_done"], 4 * DEPTH + 1)

        @block.gpsimd
        def _(pool):
            pool.memset(t.tick[:], 0.0)
            pool.memset(t.b1[:], 0.0).then_inc(s["ends_zero"], 1)
            for part in t.w1 + t.w2:
                last = pool.memset(part[:].bitcast(F32), 0.0)
            last.then_inc(s["split_step"], 1)
            pool.wait_ge(s["split_step"], 1)

            def split(parts, raw, loads, base):
                hi, lo = parts
                pool.wait_ge(s["stage_loaded"], loads)
                pool.tensor_tensor(t.tick[:, 1:2], t.tick[:, 0:1], t.tick[:, 0:1], ALU.add)
                for k in range(len(raw)):
                    last = pool.tensor_copy(hi[k], raw[k])
                last.then_inc(s["split_step"], 1)
                pool.wait_ge(s["split_step"], base)
                for k in range(len(raw)):
                    last = pool.tensor_tensor(lo[k], raw[k], hi[k].bitcast(F32), ALU.subtract)
                last.then_inc(s["split_done"], 1)

            whole = t.staging[:].rearrange("p (k n) -> p k n", k=KC)
            with pool.Fori(0, DEPTH) as l:
                def cosines(i):
                    pool.wait_ge(s["qkv_copied"], 24 * l + 3 * i + 2)
                    if i:
                        pool.wait_ge(s["summed"], 8 * l + i)
                    for w in range(2):
                        last = pool.tensor_tensor(
                            t.cos_part[:, w, :, :], t.qk_sb[i % 2][:, w, :].rearrange("p (h d) -> p h d", h=LH),
                            t.cos[:, i % 2, w, :].unsqueeze(1).broadcast_to([P, LH, LDH]), ALU.mult)
                    last.then_inc(s["cos_part"], 1)

                pool.wait_ge(s["vec_loaded"], 144 * l + 144)
                pool.wait_ge(s["const_loaded"], 48)
                for q in range(QT):
                    pool.tensor_tensor(t.cos[:, q], t.rot_cos[:, q], t.scales[:], ALU.mult)
                    for a, b in ((0, 32), (32, 0)):
                        last = pool.tensor_tensor(t.sin[:, q, :, a:a + 32], t.rot_sin[:, q, :, a:a + 32],
                                                  t.scales[:, :, b:b + 32], ALU.mult)
                last.then_inc(s["tables_ready"], 1)
                pool.wait_ge(s["tables_ready"], l + 1)
                for step in DVE_ORDER:
                    if step[0] == "B" and step[2] == 3:
                        cosines(step[1])
                    if step == ("C", 0):
                        split([[w[:]] for w in t.wo], [t.staging[:, 0:4 * D].rearrange("p (k n) -> p k n", k=4)],
                              80 * l + 32, 4 * l + 2)
                sides = [w[:].rearrange("p k (s n) -> p k s n", s=2)[:, :, :, 0:HID] for w in t.w1]
                raw = t.staging[:, 0:4 * HID].rearrange("p (k s n) -> p k s n", k=KC, s=2)
                split([[w[:, k] for k in range(KC)] for w in sides], [raw[:, k] for k in range(KC)], 80 * l + 48, 4 * l + 3)
                pool.wait_ge(s["z_ready"], 2 * l + 2)
                pool.tensor_tensor(t.y[:], t.y[:], t.b2[:].unsqueeze(1).broadcast_to([P, TILES, D]), ALU.add).then_inc(s["b2_added"], 1)
                split([[w[:, 0:5, :], w[0:HID - 5 * P, 5, :]] for w in t.w2],
                      [t.staging[:, 0:5 * D].rearrange("p (k n) -> p k n", k=5), t.staging[0:HID - 5 * P, 5 * D:6 * D]],
                      80 * l + 80, 4 * l + 4)
                split([[w[:]] for w in t.wqkv], [whole], 80 * l + 96, 4 * l + 5)

        @block.tensor
        def _(pe):
            with pe.Fori(0, DEPTH) as l:
                def turn_latents(src, ready, value):
                    for a in range(4):
                        half, kc = a // 2, a % 2
                        if kc == 0:
                            pe.wait_ge(s[ready], value(half))
                        for k in range(4):
                            last = pe.transpose(t.bank[a][:, k * P:(k + 1) * P], src[:, 4 * half + k, kc * P:(kc + 1) * P], t.ident[:])
                        last.then_inc(s["turned"], 1)

                def project(i, w):
                    if w > 2:
                        return
                    if i == 0 and w == 0:
                        pe.wait_ge(s["xt_ready"], 8 * l + 4)
                        pe.wait_ge(s["split_done"], 4 * l + 1)
                    b, q = i // 2, i % 2
                    if i:
                        pe.wait_ge(s["qkv_copied"], 24 * l + 3 * (i - 1) + w + 1)
                    for kc in range(KC):
                        last = split_product(pe, t.bank[w][:], [x[:, kc, b, q * P:(q + 1) * P] for x in t.xt],
                                             split_blocks(t.wqkv, kc, slice(w * LI, (w + 1) * LI)), kc == 0, kc == KC - 1)
                    last.then_inc(s["qkv_done"], 1)

                def turn_heads(i):
                    pe.wait_ge(s["rotated"], 8 * l + i + 1)
                    for c in range(3):
                        if i:
                            pe.wait_ge(s["c_ready"], 24 * l + 3 * i + c - 2)
                        for k in range(4):
                            src = t.rot_k[i % 2][:, k * P:(k + 1) * P] if c == 2 else \
                                t.rot_q[i % 2][:, 4 * c + k, :, :].rearrange("p o d -> p (o d)")
                            last = pe.transpose(t.bank[3 + c][:, k * P:(k + 1) * P], src, t.ident[:])
                        last.then_inc(s["c_done"], 1)

                def attend(b, j):
                    n = 32 * l + 8 * b
                    if j < LH:
                        if j == 0:
                            pe.wait_ge(s["c_ready"], 24 * l + 6 * b + 6)
                        if j >= 2:
                            pe.wait_ge(s["s_read"], n + j - 1)
                        for q, cols, keys in keys_of(j):
                            pe.matmul(t.bank[4 + j % 2][:, cols], t.qh[:, j, q * P:(q + 1) * P], t.kp[:, j, keys], start=True, stop=False)
                            last = pe.matmul(t.bank[4 + j % 2][:, cols], t.ql[:, j, q * P:(q + 1) * P], t.kp[:, j, keys], start=False, stop=True)
                        last.then_inc(s["s_done"], 1)
                    if j >= 3:
                        h = j - 3
                        pe.wait_ge(s["pt_act" if h % 2 else "pt_dve"], 16 * l + 4 * b + h // 2 + 1)
                        if h == 4:
                            pe.wait_ge(s["o_half"], 8 * l + 2 * b + 1)
                        o = t.bank[7][:].rearrange("p (q h d) -> p q h d", q=QT, h=4)
                        v = [t.v[:, (2 * b + k) % 4, h * LDH:(h + 1) * LDH] for k in range(2)]
                        pe.matmul(o[:, 0, h % 4, :], t.pt[h % 2][:, 0, :], v[0], start=True, stop=True)
                        pe.matmul(o[:, 1, h % 4, :], t.pt[h % 2][:, 1, :], v[0], start=True, stop=False)
                        pe.matmul(o[:, 1, h % 4, :], t.pt[h % 2][:, 2, :], v[1], start=False, stop=True).then_inc(s["pv_done"], 1)
                    if 2 <= j < LH + 2:
                        h = j - 2
                        pe.wait_ge(s["p_ready"], n + h + 1)
                        if h == 0 and b:
                            pe.wait_ge(s["e_added"], 8 * l + 2 * b)
                        if h >= 2:
                            pe.wait_ge(s["pt_act" if h % 2 else "pt_dve"], 16 * l + 4 * b + h // 2)
                        for k in range(3):
                            last = pe.transpose(t.bank[(6, 3)[h % 2]][:, k * P:(k + 1) * P], t.p[h % 4][:, k * P:(k + 1) * P], t.ident[:])
                        last.then_inc(s["t_done"], 1)

                def project_output(b):
                    if b == 0:
                        pe.wait_ge(s["split_done"], 4 * l + 2)
                    pe.wait_ge(s["o_half"], 8 * l + 2 * b + 2)
                    for q in range(QT):
                        for k in range(4):
                            last = pe.transpose(t.bank[(6, 3)[q]][:, k * P:(k + 1) * P], t.o[:, q, k * P:(k + 1) * P], t.ident[:])
                        last.then_inc(s["o_turned"], 1)
                    for q in range(QT):
                        pe.wait_ge(s["o_ready"], 8 * l + 2 * b + q + 1)
                        for k in range(4):
                            last = split_product(pe, t.bank[7 - q][:, 0:D], [o[:, q, k, :] for o in t.ot],
                                                 [w[:, k, :] for w in t.wo], k == 0, k == 3)
                        last.then_inc(s["e_done"], 1)

                def up(k):
                    half, m = k // 6, k % 6
                    if m == 0:
                        pe.wait_ge(s["xt_ready"], 8 * l + 4 + 2 * half + 2)
                    if k == 0:
                        pe.wait_ge(s["xt_ready"], 8 * l + 8)
                        pe.wait_ge(s["split_done"], 4 * l + 3)
                    if k >= 3:
                        pe.wait_ge(s["gated"], 12 * l + k - 2)
                    for side, bank in ((1, t.pairs[k % 3][0]), (0, t.pairs[k % 3][1])):
                        for kc in range(KC):
                            last = split_product(pe, halves(bank), [w[:, kc, side * 768 + m * P:side * 768 + (m + 1) * P] for w in t.w1],
                                                 [x[:, kc, 2 * half:2 * half + 2, 0:L] for x in t.xt], kc == 0, kc == KC - 1)
                        last.then_inc(s["up_done"], 1)

                def down(half):
                    pe.wait_ge(s["u_ready"], 12 * l + 6 * half + 6)
                    if half == 0:
                        pe.wait_ge(s["split_done"], 4 * l + 4)
                    for k in range(4):
                        tile = 4 * half + k
                        if tile >= 2:
                            pe.wait_ge(s["y_ready"], 8 * l + 8 + tile - 1)
                        for m in range(HB):
                            last = split_product(pe, t.bank[(4, 7)[tile % 2]][:, 0:D], [u[:, m, k * P:(k + 1) * P] for u in t.u],
                                                 [w[:, m, :] for w in t.w2], m == 0, m == HB - 1)
                        last.then_inc(s["down_done"], 1)

                turn_latents(t.y, "y_ready", lambda half: 8 * l + 8)
                for step in PE_ORDER:
                    if step[0] != "N":
                        {"B": project, "C": turn_heads, "D": attend, "E": project_output}[step[0]](*step[1:])
                pe.wait_ge(s["edge_row"], l + 1)
                pe.matmul(t.bank[4][:, 0:B], t.ones[:], t.edge[:], start=True, stop=True).then_inc(s["edge_done"], 1)
                turn_latents(t.z, "z_ready", lambda half: 2 * l + half + 1)
                for k in range(8):
                    up(k)
                down(0)
                for k in range(8, 12):
                    up(k)
                down(1)

        @block.scalar
        def _(act):
            act.wait_ge(s["first_var"], 1)
            act.activation(t.std[:], t.mv[:, :, 1], ACT.Sqrt, bias=t.eps[:]).then_inc(s["first_std"], 1)
            act.wait_ge(s["stage_loaded"], 16)
            act.activation(t.wqkv[0][:].rearrange("p k n -> p (k n)"), t.staging[:], ACT.Copy).then_inc(s["first_hi"], 1)
            with act.Fori(0, DEPTH) as l:
                def store_tile(i, w):
                    if w > 2:
                        return
                    act.wait_ge(s["qkv_done"], 24 * l + 3 * i + w + 1)
                    if w == 0 and i >= 2:
                        act.wait_ge(s["summed"], 8 * l + i - 1)
                    dst = t.qk_sb[i % 2][:, w, :] if w < 2 else t.v[:, i % 4, :]
                    act.activation(dst, t.bank[w][:], ACT.Copy).then_inc(s["qkv_copied"], 1)
                    if w < 2:
                        return
                    act.wait_ge(s["qkv_copied"], 24 * l + 3 * i + 3)
                    if i:
                        act.wait_ge(s["reduced"], 8 * l + i)
                    act.activation(t.squares[:], t.qk_sb[i % 2][:], ACT.Square).then_inc(s["squared"], 1)

                def find_norms(i):
                    act.wait_ge(s["reduced"], 8 * l + i + 1)
                    act.activation(t.norms[:, i % 2], t.sums[:, i % 2], ACT.Sqrt).then_inc(s["rooted"], 1)

                def store_heads(i):
                    q = slice((i % 2) * P, (i % 2 + 1) * P)
                    for c in range(3):
                        act.wait_ge(s["c_done"], 24 * l + 3 * i + c + 1)
                        bank = t.bank[3 + c][:].rearrange("p (k n) -> p k n", k=4)
                        if c < 2:
                            act.activation(t.qh[:, 4 * c:4 * c + 4, q], bank, ACT.Copy).then_inc(s["c_hi"], 1)
                        else:
                            act.activation(t.kp[0:LDH, 0:LH:2, q], bank[0:LDH], ACT.Copy)
                            act.activation(t.kp[0:LDH, 1:LH:2, q], bank[LDH:P], ACT.Copy).then_inc(s["c_hi"], 1)

                def attend(b, j):
                    n = 32 * l + 8 * b
                    if j < LH + 2:
                        if j < LH:
                            act.wait_ge(s["bias_ready"], n + j + 1)
                            for q, cols, _ in keys_of(j):
                                last = act.activation(t.p[j % 4][:, cols], t.p[j % 4][:, cols], ACT.Exp,
                                                      bias=t.bias[:, j, q:q + 1], scale=t.q_norm[:, 2 * b + q, j:j + 1],
                                                      accum_out=t.rowsum[:, j, q:q + 1])
                            last.then_inc(s["p_ready"], 1)
                        if j >= 2 and j % 2:
                            h = j - 2
                            act.wait_ge(s["t_done"], n + h + 1)
                            if h >= 2:
                                act.wait_ge(s["pv_done"], n + h - 1)
                            act.activation(t.pt[h % 2][:].rearrange("p k q -> p (k q)"), t.bank[3][:, 0:3 * P], ACT.Copy
                                           ).then_inc(s["pt_act"], 1)

                def store_output(b):
                    for q in range(QT):
                        act.wait_ge(s["o_turned"], 8 * l + 2 * b + q + 1)
                        act.activation(t.ot[0][:, q, :, :].rearrange("p k n -> p (k n)"), t.bank[(6, 3)[q]][:], ACT.Copy).then_inc(s["o_hi"], 1)

                for a in range(4):
                    half, kc = a // 2, a % 2
                    act.wait_ge(s["turned"], 8 * l + a + 1)
                    act.activation(t.xt[0][:, kc, 2 * half:2 * half + 2, kc:kc + L], halves(t.bank[a]), ACT.Copy).then_inc(s["xt_hi"], 1)
                for step in ACT_ORDER:
                    {"B": store_tile, "N": find_norms, "C": store_heads, "D": attend, "E": store_output}[step[0]](*step[1:])
                act.wait_ge(s["var"], l + 1)
                act.activation(t.std[:], t.mv[:, :, 1], ACT.Sqrt, bias=t.eps[:]).then_inc(s["std"], 1)
                for a in range(4):
                    half, kc = a // 2, a % 2
                    act.wait_ge(s["wide_ready"], 4 * l + a + 1)
                    act.activation(t.xt[0][:, kc, 2 * half:2 * half + 2, 0:L + kc], t.wide[:, kc, 2 * half:2 * half + 2, 0:L + kc],
                                   ACT.Copy).then_inc(s["xt_hi"], 1)

                def gelu(k):
                    act.wait_ge(s["up_done"], 24 * l + 2 * k + 1)
                    if k >= 2:
                        act.wait_ge(s["gated"], 12 * l + k - 1)
                    act.activation(t.gelu[k % 2][:], t.pairs[k % 3][0][:], ACT.Gelu, bias=t.b1[:, 1, k % 6:k % 6 + 1]
                                   ).then_inc(s["gelu_done"], 1)

                def hidden_hi(k):
                    act.wait_ge(s["gated"], 12 * l + k + 1)
                    if k == 6:
                        act.wait_ge(s["down_done"], 8 * l + 4)
                    act.activation(t.u[0][:, k % 6, :], t.hidden[k % 2][:], ACT.Copy).then_inc(s["u_hi"], 1)

                for k in range(12):
                    gelu(k)
                    if k:
                        hidden_hi(k - 1)
                hidden_hi(11)

        @block.vector
        def _(dve):
            first = [0]

            def at_first(ins):
                first[0] += 1
                ins.then_inc(s["first_step"], 1)
                dve.wait_ge(s["first_step"], first[0])

            dve.memset(t.ones[:], 1.0)
            dve.memset(t.mv_up[:], 0.0)
            at_first(dve.memset(t.stats[:], 0.0))
            for k in (6, 9):
                last = dve.memset(t.stats[0:1, 0:TILES:2, k:k + 1], 64.0)
            at_first(last)
            for k in range(TILES):
                last = dve.bn_stats(t.tail_stats[:, k, :], t.x[:, k, :])
            at_first(last)
            for k in range(TILES):
                last = dve.bn_aggr(t.mv[:, k, :], t.tail_stats[:, k, :])
            last.then_inc(s["first_var"], 1)
            dve.wait_ge(s["first_std"], 1)
            at_first(dve.reciprocal(t.rstd[:], t.std[:]))
            for k in range(TILES):
                dve.tensor_scalar(t.y[:, k, :], t.x[:, k, :], t.mv[:, k, 0:1], t.rstd[:, k:k + 1], ALU.subtract, ALU.mult
                                  ).then_inc(s["y_ready"], 1)

            dve.wait_ge(s["first_hi"], 1)
            hi, lo = (w[:].rearrange("p k n -> p (k n)") for w in t.wqkv)
            dve.tensor_tensor(lo, t.staging[:], hi.bitcast(F32), ALU.subtract).then_inc(s["split_done"], 1)

            with dve.Fori(0, DEPTH) as l:
                step_count = [0]

                def then(ins):
                    step_count[0] += 1
                    ins.then_inc(s["step"], 1)
                    dve.wait_ge(s["step"], STEPS * l + step_count[0])

                def low_part(lo, full, hi):
                    return dve.tensor_tensor(lo, full, hi.bitcast(F32), ALU.subtract)

                def rotate_tile(i, part):
                    if part == 3:
                        sine_part(i)
                    elif part == 4:
                        add_parts(i)

                def sine_part(i):
                    qk = t.qk_sb[i % 2][:].rearrange("p w (h d) -> p w h d", h=LH)
                    dve.wait_ge(s["qkv_copied"], 24 * l + 3 * i + 2)
                    if i == 0:
                        dve.wait_ge(s["tables_ready"], l + 1)
                    else:
                        dve.wait_ge(s["summed"], 8 * l + i)
                    for a, b in ((0, 32), (32, 0)):
                        for w in range(2):
                            last = dve.tensor_tensor(t.sin_part[:, w, :, a:a + 32], qk[:, w, :, b:b + 32],
                                                     t.sin[:, i % 2, w, a:a + 32].unsqueeze(1).broadcast_to([P, LH, 32]), ALU.mult)
                    last.then_inc(s["sin_part"], 1)

                def add_parts(i):
                    dve.wait_ge(s["sin_part"], 8 * l + i + 1)
                    dve.wait_ge(s["squared"], 8 * l + i + 1)
                    dve.tensor_reduce(t.sums[:, i % 2], t.squares[:].rearrange("p w (h d) -> p (w h) d", h=LH), X_AXIS, ALU.add
                                      ).then_inc(s["reduced"], 1)
                    dve.wait_ge(s["reduced"], 8 * l + i + 1)
                    dve.wait_ge(s["cos_part"], 8 * l + i + 1)
                    if i >= 2:
                        dve.wait_ge(s["c_done"], 24 * l + 3 * (i - 1))
                    dve.tensor_tensor(t.rot_q[i % 2][:], t.cos_part[:, 0].unsqueeze(2).broadcast_to([P, LH, 2, LDH]),
                                      t.sin_part[:, 0].unsqueeze(2).broadcast_to([P, LH, 2, LDH]), ALU.add)
                    k_view = t.rot_k[i % 2][:].rearrange("p (h d) -> p h d", h=LH)
                    dve.tensor_tensor(k_view, t.cos_part[:, 1], t.sin_part[:, 1], ALU.add).then_inc(s["summed"], 1)

                def divide_norms(i):
                    k_view = t.rot_k[i % 2][:].rearrange("p (h d) -> p h d", h=LH)
                    dve.wait_ge(s["summed"], 8 * l + i + 1)
                    dve.wait_ge(s["rooted"], 8 * l + i + 1)
                    then(dve.tensor_scalar(t.norms_kept[:], t.norms[:, i % 2], 1e-12, None, ALU.max))
                    then(dve.reciprocal(t.inverses[:], t.norms_kept[:]))
                    dve.tensor_scalar(t.q_norm[:, i, :], t.inverses[:, 0:LH], 8.0, None, ALU.mult)
                    dve.tensor_tensor(k_view, k_view, t.inverses[:, LH:2 * LH].unsqueeze(2).broadcast_to([P, LH, LDH]), ALU.mult
                                      ).then_inc(s["rotated"], 1)
                    then(dve.memset(t.tick_dve[:], 0.0))

                def store_heads(i):
                    q = slice((i % 2) * P, (i % 2 + 1) * P)
                    for c in range(3):
                        dve.wait_ge(s["c_hi"], 24 * l + 3 * i + c + 1)
                        bank = t.bank[3 + c][:].rearrange("p (k n) -> p k n", k=4)
                        if c < 2:
                            last = low_part(t.ql[:, 4 * c:4 * c + 4, q], bank, t.qh[:, 4 * c:4 * c + 4, q])
                        else:
                            low_part(t.kp[LDH:P, 0:LH:2, q], bank[0:LDH], t.kp[0:LDH, 0:LH:2, q])
                            last = low_part(t.kp[LDH:P, 1:LH:2, q], bank[LDH:P], t.kp[0:LDH, 1:LH:2, q])
                        last.then_inc(s["c_ready"], 1)

                def normalise(b, half):
                    dve.wait_ge(s["pv_done"], 32 * l + 8 * b + 4 * half + 4)
                    then(dve.reciprocal(t.inv[:], t.rowsum[:, 4 * half:4 * half + 4, :]))
                    o = t.bank[7][:].rearrange("p (q h d) -> p q h d", q=QT, h=4)
                    for q in range(QT):
                        last = dve.tensor_tensor(t.o[:, q, half * L:(half + 1) * L].rearrange("p (h d) -> p h d", h=4), o[:, q],
                                                 t.inv[:, :, q].unsqueeze(2).broadcast_to([P, 4, LDH]), ALU.mult)
                    last.then_inc(s["o_half"], 1)

                def attend(b, j):
                    n = 32 * l + 8 * b
                    if j < LH + 2:
                        if j == 7:
                            normalise(b, 0)
                        if j < LH:
                            dve.wait_ge(s["s_done"], n + j + 1)
                            if j >= 4:
                                dve.wait_ge(s["t_done"], n + j - 3)
                            dve.memset(t.tick_dve[:], 0.0)
                            for q, cols, _ in keys_of(j):
                                last = dve.tensor_tensor_reduce(
                                    out=t.p[j % 4][:, cols], in0=t.bank[4 + j % 2][:, cols], in1=t.window[:, cols], scale=1.0,
                                    scalar=-BIG, op0=ALU.add, op1=ALU.max, accum_out=t.mx[:, j, q:q + 1])
                            last.then_inc(s["s_read"], 1)
                            dve.wait_ge(s["s_read"], n + j + 1)
                            dve.scalar_tensor_tensor(out=t.bias[:, j, :], in0=t.mx[:, j, :], scalar=-1.0,
                                                     in1=t.q_norm[:, 2 * b:2 * b + 2, j], op0=ALU.mult, op1=ALU.mult
                                                     ).then_inc(s["bias_ready"], 1)
                            then(dve.memset(t.tick_dve[:], 0.0))
                        if j >= 2 and j % 2 == 0:
                            h = j - 2
                            dve.wait_ge(s["t_done"], n + h + 1)
                            if h >= 2:
                                dve.wait_ge(s["pv_done"], n + h - 1)
                            dve.tensor_copy(t.pt[h % 2][:].rearrange("p k q -> p (k q)"), t.bank[6][:, 0:3 * P]).then_inc(s["pt_dve"], 1)
                    else:
                        normalise(b, 1)

                def store_output(b):
                    for q in range(QT):
                        dve.wait_ge(s["o_hi"], 8 * l + 2 * b + q + 1)
                        lo, hi = (o[:, q, :, :].rearrange("p k n -> p (k n)") for o in (t.ot[1], t.ot[0]))
                        low_part(lo, t.bank[(6, 3)[q]][:], hi).then_inc(s["o_ready"], 1)
                    for q in range(QT):
                        dve.wait_ge(s["e_done"], 8 * l + 2 * b + q + 1)
                        dve.tensor_tensor(t.y[:, 2 * b + q, :], t.y[:, 2 * b + q, :], t.bank[7 - q][:, 0:D], ALU.add
                                          ).then_inc(s["e_added"], 1)
                    dve.wait_ge(s["e_added"], 8 * l + 2 * b + 2)
                    for k in (2 * b, 2 * b + 1):
                        dve.bn_stats(t.stats[:, k, 0:6], t.y[:, k, 0:P])
                        last = dve.bn_stats(t.tail_stats[:, k, :], t.y[:, k, P:D])
                    if b == B - 1:
                        last.then_inc(s["half_stats"], 1)

                dve.wait_ge(s["y_ready"], 8 * l + 8)
                for part in t.xt:
                    last = dve.memset(part[:, 1, :, 0:1].bitcast(F32), 0.0)
                for a in range(4):
                    half, kc = a // 2, a % 2
                    dve.wait_ge(s["xt_hi"], 8 * l + a + 1)
                    lo, hi = (x[:, kc, 2 * half:2 * half + 2, kc:kc + L] for x in (t.xt[1], t.xt[0]))
                    low_part(lo, halves(t.bank[a]), hi).then_inc(s["xt_ready"], 1)
                for step in DVE_ORDER:
                    {"B": rotate_tile, "N": divide_norms, "C": store_heads, "D": attend, "E": store_output}[step[0]](*step[1:])

                dve.wait_ge(s["stats_shifted"], 32 * l + 32)
                dve.memset(t.tick_dve[:], 0.0)
                for k in range(TILES):
                    last = dve.bn_aggr(t.mv[:, k, :], t.stats[:, k, :])
                last.then_inc(s["var"], 1)
                dve.wait_ge(s["std"], l + 1)
                dve.reciprocal(t.mv[:, :, 1], t.std[:]).then_inc(s["mv_ready"], 1)
                dve.wait_ge(s["mv_ready"], l + 1)
                dve.scalar_tensor_tensor(out=t.edge[:], in0=t.mv[0:1, 0:TILES:2, 0], scalar=-1.0, in1=t.mv[0:1, 0:TILES:2, 1],
                                         op0=ALU.mult, op1=ALU.mult).then_inc(s["edge_row"], 1)
                for k in range(TILES):
                    dve.tensor_scalar(t.z[:, k, 0:P], t.y[:, k, 0:P], t.mv[:, k, 0:1], t.mv[:, k, 1:2], ALU.subtract, ALU.mult)
                dve.wait_ge(s["mv_shifted"], 32 * l + 32)
                for k in range(TILES):
                    last = dve.tensor_scalar(t.z[:, k, P:D], t.y[:, k, P:D], t.mv_up[:, k, 0:1], t.mv_up[:, k, 1:2], ALU.subtract, ALU.mult)
                    if k % 4 == 3:
                        last.then_inc(s["z_ready"], 1)
                dve.wait_ge(s["edge_done"], l + 1)
                dve.tensor_scalar(t.wide[:, 1, :, 0], t.bank[4][:, 0:B], t.ln[:, 0, 1:2], t.ln[:, 1, 1:2], ALU.mult, ALU.add)
                for a in range(4):
                    half, kc = a // 2, a % 2
                    dve.wait_ge(s["turned"], 8 * l + 4 + a + 1)
                    dve.tensor_scalar(t.wide[:, kc, 2 * half:2 * half + 2, kc:kc + L], halves(t.bank[a]), t.ln[:, 0, kc:kc + 1],
                                      t.ln[:, 1, kc:kc + 1], ALU.mult, ALU.add).then_inc(s["wide_ready"], 1)
                for a in range(4):
                    half, kc = a // 2, a % 2
                    dve.wait_ge(s["xt_hi"], 8 * l + 4 + a + 1)
                    lo, hi, full = (x[:, kc, 2 * half:2 * half + 2, 0:L + kc] for x in (t.xt[1], t.xt[0], t.wide))
                    low_part(lo, full, hi).then_inc(s["xt_ready"], 1)

                def gate(k):
                    dve.wait_ge(s["up_done"], 24 * l + 2 * k + 2)
                    dve.wait_ge(s["gelu_done"], 12 * l + k + 1)
                    if k >= 2:
                        dve.wait_ge(s["u_ready"], 12 * l + k - 1)
                    dve.scalar_tensor_tensor(out=t.hidden[k % 2][:], in0=t.pairs[k % 3][1][:], scalar=t.b1[:, 0, k % 6:k % 6 + 1],
                                             in1=t.gelu[k % 2][:], op0=ALU.add, op1=ALU.mult).then_inc(s["gated"], 1)

                def hidden_lo(k):
                    dve.wait_ge(s["u_hi"], 12 * l + k + 1)
                    low_part(t.u[1][:, k % 6, :], t.hidden[k % 2][:], t.u[0][:, k % 6, :]).then_inc(s["u_ready"], 1)

                def add_down(half):
                    if half == 0:
                        dve.wait_ge(s["b2_added"], l + 1)
                    for k in range(4):
                        tile = 4 * half + k
                        dve.wait_ge(s["down_done"], 8 * l + tile + 1)
                        dve.tensor_tensor(t.y[:, tile, :], t.y[:, tile, :], t.bank[(4, 7)[tile % 2]][:, 0:D], ALU.add
                                          ).then_inc(s["y_ready"], 1)

                for k in range(12):
                    gate(k)
                    if k == 7:
                        add_down(0)
                    if k:
                        hidden_lo(k - 1)
                hidden_lo(11)
                add_down(1)
                assert step_count[0] == STEPS, step_count
            dve.wait_ge(s["y_ready"], 8 * DEPTH + 8)
            dve.tensor_tensor(t.x[:], t.x[:], t.y[:], ALU.add).then_inc(s["result"], 1)


def latent_stages(nc, t, sem_maker, args, out):
    with ExitStack() as ctx:
        def sb(name, shape, dt=F32):
            return ctx.enter_context(nc.sbuf_tensor(f"a_{name}", shape, dt))

        def parts(name, shape):
            return [sb(f"{name}_{part}", shape, F32R) for part in ("hi", "lo")]

        t.w_raw = [sb(f"w_raw{k}", [P, KC, D]) for k in range(3)]
        t.w = [parts(f"w{k}", [P, KC, D]) for k in range(3)]
        t.causal = sb("causal", [P, QT, L])
        t.z, t.v, t.s_sb, t.p = (sb(n, [P, TILES, D]) for n in ("z", "v", "s_sb", "p"))
        t.xt, t.qt, t.kt = (parts(n, [P, KC, B * L]) for n in ("xt", "qt", "kt"))
        t.pt = sb("pt", [P, B, 3, P])
        t.stats, t.mv = sb("stats", [P, TILES, 6]), sb("mv", [P, TILES, 2])
        t.std, t.rstd, t.mx, t.bias, t.rowsum, t.inv = (sb(n, [P, TILES]) for n in ("std", "rstd", "mx", "bias", "rowsum", "inv"))
        t.bank = [ctx.enter_context(nc.psum_tensor(f"a_bank{k}", [P, 512], F32)) for k in range(8)]
        attend_stage(nc, t, sem_maker(ctx, "att"), args)
    with ExitStack() as ctx:
        def sb(name, shape, dt=F32):
            return ctx.enter_context(nc.sbuf_tensor(f"f_{name}", shape, dt))

        def parts(name, shape):
            return [sb(f"{name}_{part}", shape, F32R) for part in ("hi", "lo")]

        t.y = sb("y", [P, TILES, D])
        t.wqkv, t.wo = parts("wqkv", [P, KC, 3 * LI]), parts("wo", [P, 4, D])
        t.w1, t.w2 = parts("w1", [P, KC, 2 * HB * P]), parts("w2", [P, HB, D])
        t.staging = sb("staging", [P, KC * 3 * LI])
        t.xt = parts("xt", [P, KC, B, L + 2])
        t.rot_cos, t.rot_sin, t.cos, t.sin = (sb(n, [P, QT, 2, LDH]) for n in ("rot_cos", "rot_sin", "cos", "sin"))
        t.window = sb("window", [P, 3 * P])
        t.scales, t.ln, t.b2, t.b1 = sb("scales", [P, 2, LDH]), sb("ln", [P, 2, KC]), sb("b2", [P, D]), sb("b1", [P, 2, HB])
        work = sb("work", [P, 5120])
        t.qk_sb = [work[:, k * 1024:(k + 1) * 1024].rearrange("p (w n) -> p w n", w=2) for k in range(2)]
        t.cos_part, t.sin_part = (work[:, k * 1024:(k + 1) * 1024].rearrange("p (w h d) -> p w h d", w=2, h=LH) for k in (2, 3))
        t.squares = work[:, 4096:5120].rearrange("p (w n) -> p w n", w=2)
        t.z = work[:, 0:2048].rearrange("p (k n) -> p k n", k=TILES)
        t.wide = work[:, 2048:2048 + 2 * B * (L + 2)].rearrange("p (k b n) -> p k b n", k=KC, b=B)
        heads = sb("heads", [P, 3 * LH * L], F32R)
        t.qh, t.ql, t.kp = (heads[:, k * LH * L:(k + 1) * LH * L].rearrange("p (h n) -> p h n", h=LH) for k in range(3))
        t.u = [heads[:, k * HB * 512:(k + 1) * HB * 512].rearrange("p (m n) -> p m n", m=HB) for k in range(2)]
        soft = sb("soft", [P, 6 * 3 * P])
        t.p = [soft[:, k * 384:(k + 1) * 384] for k in range(4)]
        t.pt = [soft[:, k * 384:(k + 1) * 384].rearrange("p (k q) -> p k q", k=3) for k in (4, 5)]
        t.gelu = [soft[:, k * 512:(k + 1) * 512] for k in range(2)]
        t.hidden = [soft[:, k * 512:(k + 1) * 512] for k in range(2, 4)]
        t.rot_q = [sb(f"rot_q{k}", [P, LH, 2, LDH]) for k in range(2)]
        t.rot_k = [sb(f"rot_k{k}", [P, LI]) for k in range(2)]
        t.v = sb("v", [P, 4, LI])
        t.o = sb("o", [P, QT, LI])
        t.ot = parts("ot", [P, QT, 4, P])
        t.stats, t.tail_stats, t.mv, t.mv_up = sb("stats", [P, TILES, 12]), sb("tail_stats", [P, TILES, 6]), sb("mv", [P, TILES, 2]), sb("mv_up", [P, TILES, 2])
        t.std, t.rstd = sb("std", [P, TILES]), sb("rstd", [P, TILES])
        t.sums, t.norms = (sb(n, [P, 2, 2 * LH]) for n in ("sums", "norms"))
        t.norms_kept, t.inverses = (sb(n, [P, 2 * LH]) for n in ("norms_kept", "inverses"))
        t.q_norm = sb("q_norm", [P, TILES, LH])
        t.mx, t.bias, t.rowsum = (sb(n, [P, LH, QT]) for n in ("mx", "bias", "rowsum"))
        t.inv = sb("inv", [P, 4, QT])
        t.ones, t.edge = sb("ones", [1, P]), sb("edge", [1, B])
        t.tick, t.tick_dve = sb("tick", [P, 2]), sb("tick_dve", [P, 1])
        t.bank = [ctx.enter_context(nc.psum_tensor(f"f_bank{k}", [P, 512], F32)) for k in range(8)]
        t.pairs = [(t.bank[0], t.bank[1]), (t.bank[2], t.bank[3]), (t.bank[5], t.bank[6])]
        transformer_stage(nc, t, sem_maker(ctx, "ffn"), args, out)


def program(nc, args, out):
    with ExitStack() as whole:
        class Tensors:
            pass

        t = Tensors()

        def sem_maker(ctx, prefix):
            return lambda name: ctx.enter_context(nc.semaphore(f"{prefix}_{name}"))

        t.x = whole.enter_context(nc.sbuf_tensor("x", [P, TILES, D], F32))
        t.ident = whole.enter_context(nc.sbuf_tensor("ident", [P, P], F32))
        t.eps = whole.enter_context(nc.sbuf_tensor("eps", [P, 1], F32))
        with ExitStack() as ctx:
            def sb(name, shape, dt=F32):
                return ctx.enter_context(nc.sbuf_tensor(name, shape, dt))

            def parts(name, shape):
                return [sb(f"{name}_{part}", shape, F32R) for part in ("hi", "lo")]

            t.wkv, t.wq, t.wout = parts("wkv", [P, KC, 2 * H * DH]), parts("wq", [P, KC, H * DH]), parts("wout", [P, 8, D])
            t.gains = sb("gains", [P, 1 + B, 2 * KC])
            t.raw, t.mask8 = sb("raw", [P, 1 + B, KT, D]), sb("mask8", [P, 1 + B, CH], U8)
            t.plan = sb("plan", [1, B * PLAN], I32)
            with ExitStack() as inner:
                def raw(name, shape, dt=F32):
                    return inner.enter_context(nc.sbuf_tensor(name, shape, dt))

                t.wkv_raw, t.wq_raw, t.wout_raw = raw("wkv_raw", [P, KC, 2 * H * DH]), raw("wq_raw", [P, KC, H * DH]), raw("wout_raw", [P, 8, D])
                t.mask_rows = raw("mask_rows", [B, CTX], U8)
                t.norm = raw("norm", [P, 2, 2 * KC])
                t.x_stats, t.x_mv = raw("x_stats", [P, TILES, 6]), raw("x_mv", [P, TILES, 2])
                t.x_std, t.x_rstd = raw("x_std", [P, TILES]), raw("x_rstd", [P, TILES])
                t.iota = raw("iota", [B, ITEMS])
                t.next_slot = raw("next_slot", [B, 1])
                t.first_key = raw("first_key", [B, NCH])
                t.ones = raw("ones", [B, NCH])
                t.scratch = raw("scratch", [B, 3 * NCH])
                t.hits = raw("hits", [B, NCH, NCH])
                t.plan_rows = raw("plan_rows", [B, PLAN])
                t.plan_flat = raw("plan_flat", [1, B * PLAN])
                prepare_stage(nc, t, sem_maker(inner, "prep"), args)
            t.z = sb("z", [P, 2, D])
            t.wide = sb("wide", [P, KC, CH])
            t.xt = parts("xt", [P, KC, CH])
            t.pen = sb("pen", [P, CH])
            t.tick, t.tick_pool = sb("tick", [P, 3]), sb("tick_pool", [P, 2])
            t.stats, t.mv, t.std, t.rstd = sb("stats", [P, 2, 6]), sb("mv", [P, 2, 2]), sb("std", [P, 2]), sb("rstd", [P, 2])
            t.qh, t.ql, t.kp = (sb(n, [P, H, L], F32R) for n in ("qh", "ql", "kp"))
            t.v = sb("v", [P, KT, H * DH])
            t.s_sb = [sb(f"s_sb{k}", [P, GU, CH]) for k in range(2)]
            t.probs = [sb(f"probs{k}", [P, GU, CH]) for k in range(3)]
            t.pt = [sb(f"pt{k}", [P, GU, KT, P]) for k in range(3)]
            t.mstate, t.mnew, t.mdiff, t.mbias, t.alpha, t.rowsum, t.den, t.inv = (
                sb(n, [P, H * QT]) for n in ("mstate", "mnew", "mdiff", "mbias", "alpha", "rowsum", "den", "inv"))
            t.o = sb("o", [P, H * QT, DH])
            t.onorm = sb("onorm", [P, QT, H * DH])
            t.ot = [q[:, 0:8, :] for q in (t.qh, t.ql)]
            t.s_ps = [ctx.enter_context(nc.psum_tensor(f"s_ps{k}", [P, GU, CH], F32)) for k in range(2)]
            t.turn = [ctx.enter_context(nc.psum_tensor(f"turn{k}", [P, 512], F32)) for k in range(2)]
            t.proj = ctx.enter_context(nc.psum_tensor("proj", [P, 512], F32))
            t.pv_ps = ctx.enter_context(nc.psum_tensor("pv_ps", [P, GU, DH], F32))
            cross_stage(nc, t, sem_maker(ctx, "cross"), args)
        latent_stages(nc, t, sem_maker, args, out)


def constants():
    c = {"ident": np.eye(P, dtype=np.float32), "iota": np.tile(np.arange(ITEMS, dtype=np.float32), (B, 1))}
    c["next_slot"] = np.minimum(np.arange(B) + 2, B).astype(np.float32)[:, None]
    c["first_key"] = (np.arange(B)[:, None] * CTX + np.arange(NCH)[None] * CH).astype(np.float32)
    i, j = np.arange(L)[:, None], np.arange(L)[None]
    seen = np.where(j <= i, 0.0, -BIG).astype(np.float32)
    c["causal"] = np.ascontiguousarray(seen.reshape(QT, P, L).transpose(1, 0, 2))
    near = np.where((j <= i) & (i <= j + P), 0.0, -FAR).astype(np.float32)
    c["window"] = np.ascontiguousarray(np.concatenate([near[:P, :P], near[P:]], axis=1))
    half = np.arange(0, LDH, 2, dtype=np.float32)
    pos = np.arange(L, dtype=np.float32)
    freq = pos[:, None] * (np.float32(1.0) / np.float32(10000.0) ** (half / np.float32(LDH)))[None]
    base = (half + np.float32(0.4 * LDH)) / np.float32(1.4 * LDH)
    growth = base[None] ** ((pos - L // 2) / np.float32(P // 2))[:, None]
    growth = np.concatenate([growth, growth], axis=1)
    cos, sin = (np.tile(f(freq), (1, 2)) for f in (np.cos, np.sin))
    sign = np.where(np.arange(LDH) < LDH // 2, -1.0, 1.0).astype(np.float32)
    for name, table in (("rot_cos", cos), ("rot_sin", sin * sign)):
        both = np.stack([table * growth, table / growth], axis=1).astype(np.float32)
        c[name] = np.ascontiguousarray(both.reshape(QT, P, 2, LDH).transpose(1, 0, 2, 3))
    return c


_INS = ['x', 'ctx_1024', 'mask_BxS2_bk0', 'L0_xattn_g1', 'L0_xattn_b1', 'L0_xattn_g2', 'L0_xattn_b2', 'L0_xattn_Wq',
        'L0_xattn_Wkv', 'L0_xattn_Wout', 'L0_attn_Qw', 'L0_attn_Kw', 'L0_attn_Vw', 'L0_ffn_wqkv', 'L0_ffn_q_scale',
        'L0_ffn_k_scale', 'L0_ffn_wo', 'L0_ffn_ln_g', 'L0_ffn_ln_b', 'L0_ffn_w1', 'L0_ffn_b1', 'L0_ffn_w2', 'L0_ffn_b2']


def kernel(**inputs):
    import concourse.bacc as _bacc
    from concourse.bass_utils import run_bass_kernel_spmd as _run

    nc = _bacc.Bacc("TRN2", target_bir_lowering=False, num_devices=1)
    arrays, args = {}, {}
    for name, value in list(constants().items()) + [(n, inputs[n]) for n in _INS]:
        a = np.ascontiguousarray(value)
        arrays[f"in_{name}"] = a
        args[name] = nc.dram_tensor(f"in_{name}", a.shape, mybir.dt.from_np(a.dtype), kind="ExternalInput").ap()
    out = nc.dram_tensor("out", (B, L, D), F32, kind="ExternalOutput").ap()
    program(nc, args, out)
    result = _run(nc, [arrays], core_ids=[0])
    return result.results[0]["out"]
```
